# Optimizing a Trainium2 kernel written in Bass

```python
import numpy as np
import jax
import jax.numpy as jnp

def _softmax(x, axis=-1):
    return jax.nn.softmax(x, axis=axis)

def _gelu(x):
    return jax.nn.gelu(x, approximate=True)

def _silu(x):
    return jax.nn.silu(x)

def _sigmoid(x):
    return jax.nn.sigmoid(x)

def _layernorm(x, axis=-1, eps=1e-05):
    m = jnp.mean(x, axis=axis, keepdims=True)
    v = jnp.var(x, axis=axis, keepdims=True)
    return (x - m) / jnp.sqrt(v + eps)

def _scatter_add(tgt, idx, src, axis=0):
    return tgt.at[idx].add(src)

def _segment_sum(src, seg, n):
    return jax.ops.segment_sum(src, seg, n)
kernel_name = 'mk_seq_preln_d1_jaxref_r8_751520'

def setup_inputs(seed: int=0):
    np.random.seed(seed)
    _w = jnp.asarray

    def _L0_attn_setup():
        import jax, jax.numpy as jnp
        import numpy as np
        import math
        D = 128
        H = 16
        KVH = 4
        HD = D // H
        W = 32
        N = 64
        DTR = 64
        SE = 512
        CD = D // 8
        B = 1
        L = 256

        def _forward(x, ln_g, ln_b, w_xproj, w_dt, b_dt, A_log, D_ssm, w_ssm_out, wq, wk, wv, wo, rel_bias, w_wm, b_wm, episodic, w_dc1, b_dc1, w_dc2, b_dc2, w_imp, b_imp, w_conv, b_conv):
            Bq, Lq, Dq = x.shape
            rw = jnp.asarray([0.2, 0.45, 0.15, 0.2], x.dtype)
            mu = x.mean(-1, keepdims=True)
            var = ((x - mu) ** 2).mean(-1, keepdims=True)
            xn = (x - mu) * jax.lax.rsqrt(var + 1e-05) * ln_g + ln_b
            xp = xn @ w_xproj
            dt_in, Bs, Cs = (xp[..., :DTR], xp[..., DTR:DTR + N], xp[..., DTR + N:])
            delta = jax.nn.softplus(dt_in @ w_dt + b_dt)
            A = -jnp.exp(A_log)

            def step(h, t):
                dt, bt, ct, xt = t
                h = jnp.exp(dt[:, :, None] * A) * h + (dt * xt)[:, :, None] * bt[:, None, :]
                return (h, jnp.einsum('bdn,bn->bd', h, ct))
            h0 = jnp.zeros((Bq, Dq, N), x.dtype)
            _, ysT = jax.lax.scan(step, h0, (delta.transpose(1, 0, 2), Bs.transpose(1, 0, 2), Cs.transpose(1, 0, 2), xn.transpose(1, 0, 2)))
            ssm_out = (ysT.transpose(1, 0, 2) + x * D_ssm) @ w_ssm_out
            q = (x @ wq).reshape(Bq, Lq, H, HD).transpose(0, 2, 1, 3)
            k = (x @ wk).reshape(Bq, Lq, KVH, HD).transpose(0, 2, 1, 3)
            v = (x @ wv).reshape(Bq, Lq, KVH, HD).transpose(0, 2, 1, 3)
            rep = H // KVH
            k = jnp.repeat(k, rep, axis=1)
            v = jnp.repeat(v, rep, axis=1)
            nb = Lq // W
            qb = q.reshape(Bq, H, nb, W, HD)
            kp = jnp.pad(k, ((0, 0), (0, 0), (W, W), (0, 0))).reshape(Bq, H, nb + 2, W, HD)
            vp = jnp.pad(v, ((0, 0), (0, 0), (W, W), (0, 0))).reshape(Bq, H, nb + 2, W, HD)
            k3 = jnp.concatenate([kp[:, :, i:i + nb] for i in range(3)], axis=3)
            v3 = jnp.concatenate([vp[:, :, i:i + nb] for i in range(3)], axis=3)
            scores = jnp.einsum('bhnqd,bhnkd->bhnqk', qb, k3) / math.sqrt(HD)
            qi = jnp.arange(W)
            kj = jnp.arange(3 * W)
            rel = kj[None, :] - W - qi[:, None]
            win_mask = jnp.abs(rel) <= W
            kglob = (jnp.arange(nb)[:, None] - 1) * W + kj[None, :]
            pad_mask = (kglob >= 0) & (kglob < Lq)
            bias = rel_bias[jnp.clip(rel + W, 0, 2 * W)].transpose(2, 0, 1)
            scores = scores + bias[None, :, None, :, :]
            mask = win_mask[None, :, :] & pad_mask[:, None, :]
            scores = jnp.where(mask[None, None], scores, jnp.asarray(-1000000000.0, scores.dtype))
            attn = jax.nn.softmax(scores, axis=-1)
            ao = jnp.einsum('bhnqk,bhnkd->bhnqd', attn, v3)
            ao = ao.reshape(Bq, H, Lq, HD).transpose(0, 2, 1, 3).reshape(Bq, Lq, Dq)
            attn_out = ao @ wo
            kernel = w_conv.T[:, None, :]
            xc = jax.lax.conv_general_dilated(x, kernel, (1,), [(3, 0)], dimension_numbers=('NWC', 'WIO', 'NWC'), feature_group_count=Dq)
            conv_out = jax.nn.silu(xc + b_conv)
            wm = x @ w_wm + b_wm
            dec = jax.nn.gelu(episodic @ w_dc1 + b_dc1, approximate=False) @ w_dc2 + b_dc2
            es = jnp.einsum('bld,sd->bls', x, dec[0]) / math.sqrt(Dq)
            eo = jax.nn.softmax(es, axis=-1) @ dec[0]
            mem_out = wm + 0.3 * eo
            return x + rw[0] * attn_out + rw[1] * ssm_out + rw[2] * conv_out + rw[3] * mem_out
        key = jax.random.key(seed)
        ks = jax.random.split(key, 20)

        def rn(k, shape, s=0.02):
            return jax.random.normal(k, shape, jnp.float32) * s
        return dict(x=jax.random.normal(ks[0], (B, L, D), jnp.float32), ln_g=jnp.ones((D,), jnp.float32), ln_b=jnp.zeros((D,), jnp.float32), w_xproj=rn(ks[1], (D, DTR + 2 * N)), w_dt=rn(ks[2], (DTR, D)), b_dt=jnp.zeros((D,), jnp.float32), A_log=jnp.log(jnp.tile(jnp.arange(1, N + 1, dtype=jnp.float32), (D, 1))), D_ssm=jnp.ones((D,), jnp.float32), w_ssm_out=rn(ks[3], (D, D)), wq=rn(ks[4], (D, D)), wk=rn(ks[5], (D, KVH * HD)), wv=rn(ks[6], (D, KVH * HD)), wo=rn(ks[7], (D, D)), rel_bias=rn(ks[8], (2 * W + 1, H), 0.01), w_wm=rn(ks[9], (D, D)), b_wm=jnp.zeros((D,), jnp.float32), episodic=rn(ks[10], (1, SE, CD)), w_dc1=rn(ks[11], (CD, D // 2)), b_dc1=jnp.zeros((D // 2,), jnp.float32), w_dc2=rn(ks[12], (D // 2, D)), b_dc2=jnp.zeros((D,), jnp.float32), w_imp=rn(ks[13], (D, 1)), b_imp=jnp.zeros((1,), jnp.float32), w_conv=rn(ks[14], (D, 4), 0.1), b_conv=jnp.zeros((D,), jnp.float32))
    _L0_attn_in = _L0_attn_setup()

    def _L0_ffn_setup():
        import jax, jax.numpy as jnp
        import numpy as np
        INT4_QMAX = 7.0

        def simulate_quantize_int4(w):
            scale = jnp.max(jnp.abs(w)) / INT4_QMAX
            q = jnp.clip(jnp.round(w / scale), -8.0, 7.0)
            return q * scale
        key = jax.random.key(seed)
        k_x, k_w, k_bias, k_a, k_b = jax.random.split(key, 5)
        d_in, features, rank = (128, 128, 16)
        x = jax.random.normal(k_x, (4, 1024, d_in), dtype=jnp.float32)
        kernel = jax.random.normal(k_w, (d_in, features), dtype=jnp.float32)
        bias = jax.random.normal(k_bias, (features,), dtype=jnp.float32)
        a = jax.random.normal(k_a, (d_in, rank), dtype=jnp.float32) * (1.0 / np.sqrt(d_in))
        b = jax.random.normal(k_b, (rank, features), dtype=jnp.float32) * 0.01
        return {'x': x, 'kernel': kernel, 'bias': bias, 'a': a, 'b': b}
    _L0_ffn_in = _L0_ffn_setup()
    _d = {'L0_attn_x': _L0_attn_in['x'], 'L0_attn_ln_g': _L0_attn_in['ln_g'], 'L0_attn_ln_b': _L0_attn_in['ln_b'], 'L0_attn_w_xproj': _L0_attn_in['w_xproj'], 'L0_attn_w_dt': _L0_attn_in['w_dt'], 'L0_attn_b_dt': _L0_attn_in['b_dt'], 'L0_attn_A_log': _L0_attn_in['A_log'], 'L0_attn_D_ssm': _L0_attn_in['D_ssm'], 'L0_attn_w_ssm_out': _L0_attn_in['w_ssm_out'], 'L0_attn_wq': _L0_attn_in['wq'], 'L0_attn_wk': _L0_attn_in['wk'], 'L0_attn_wv': _L0_attn_in['wv'], 'L0_attn_wo': _L0_attn_in['wo'], 'L0_attn_rel_bias': _L0_attn_in['rel_bias'], 'L0_attn_w_wm': _L0_attn_in['w_wm'], 'L0_attn_b_wm': _L0_attn_in['b_wm'], 'L0_attn_episodic': _L0_attn_in['episodic'], 'L0_attn_w_dc1': _L0_attn_in['w_dc1'], 'L0_attn_b_dc1': _L0_attn_in['b_dc1'], 'L0_attn_w_dc2': _L0_attn_in['w_dc2'], 'L0_attn_b_dc2': _L0_attn_in['b_dc2'], 'L0_attn_w_imp': _L0_attn_in['w_imp'], 'L0_attn_b_imp': _L0_attn_in['b_imp'], 'L0_attn_w_conv': _L0_attn_in['w_conv'], 'L0_attn_b_conv': _L0_attn_in['b_conv'], 'L0_ffn_kernel': _L0_ffn_in['kernel'], 'L0_ffn_bias': _L0_ffn_in['bias'], 'L0_ffn_a': _L0_ffn_in['a'], 'L0_ffn_b': _L0_ffn_in['b']}
    _x0 = _d['L0_attn_x']
    _d['L0_attn_x'] = jax.random.normal(jax.random.fold_in(jax.random.key(seed), 1), (8, 512, 128), dtype=_x0.dtype)
    del _x0
    return _d

def reference(L0_attn_x, L0_attn_ln_g, L0_attn_ln_b, L0_attn_w_xproj, L0_attn_w_dt, L0_attn_b_dt, L0_attn_A_log, L0_attn_D_ssm, L0_attn_w_ssm_out, L0_attn_wq, L0_attn_wk, L0_attn_wv, L0_attn_wo, L0_attn_rel_bias, L0_attn_w_wm, L0_attn_b_wm, L0_attn_episodic, L0_attn_w_dc1, L0_attn_b_dc1, L0_attn_w_dc2, L0_attn_b_dc2, L0_attn_w_imp, L0_attn_b_imp, L0_attn_w_conv, L0_attn_b_conv, L0_ffn_kernel, L0_ffn_bias, L0_ffn_a, L0_ffn_b):

    def _L0_attn_ref(x, ln_g, ln_b, w_xproj, w_dt, b_dt, A_log, D_ssm, w_ssm_out, wq, wk, wv, wo, rel_bias, w_wm, b_wm, episodic, w_dc1, b_dc1, w_dc2, b_dc2, w_imp, b_imp, w_conv, b_conv):
        import jax, jax.numpy as jnp
        import numpy as np
        import math
        D = 128
        H = 16
        KVH = 4
        HD = D // H
        W = 32
        N = 64
        DTR = 64
        SE = 512
        CD = D // 8
        B = 1
        L = 256

        def _forward(x, ln_g, ln_b, w_xproj, w_dt, b_dt, A_log, D_ssm, w_ssm_out, wq, wk, wv, wo, rel_bias, w_wm, b_wm, episodic, w_dc1, b_dc1, w_dc2, b_dc2, w_imp, b_imp, w_conv, b_conv):
            Bq, Lq, Dq = x.shape
            rw = jnp.asarray([0.2, 0.45, 0.15, 0.2], x.dtype)
            mu = x.mean(-1, keepdims=True)
            var = ((x - mu) ** 2).mean(-1, keepdims=True)
            xn = (x - mu) * jax.lax.rsqrt(var + 1e-05) * ln_g + ln_b
            xp = xn @ w_xproj
            dt_in, Bs, Cs = (xp[..., :DTR], xp[..., DTR:DTR + N], xp[..., DTR + N:])
            delta = jax.nn.softplus(dt_in @ w_dt + b_dt)
            A = -jnp.exp(A_log)

            def step(h, t):
                dt, bt, ct, xt = t
                h = jnp.exp(dt[:, :, None] * A) * h + (dt * xt)[:, :, None] * bt[:, None, :]
                return (h, jnp.einsum('bdn,bn->bd', h, ct))
            h0 = jnp.zeros((Bq, Dq, N), x.dtype)
            _, ysT = jax.lax.scan(step, h0, (delta.transpose(1, 0, 2), Bs.transpose(1, 0, 2), Cs.transpose(1, 0, 2), xn.transpose(1, 0, 2)))
            ssm_out = (ysT.transpose(1, 0, 2) + x * D_ssm) @ w_ssm_out
            q = (x @ wq).reshape(Bq, Lq, H, HD).transpose(0, 2, 1, 3)
            k = (x @ wk).reshape(Bq, Lq, KVH, HD).transpose(0, 2, 1, 3)
            v = (x @ wv).reshape(Bq, Lq, KVH, HD).transpose(0, 2, 1, 3)
            rep = H // KVH
            k = jnp.repeat(k, rep, axis=1)
            v = jnp.repeat(v, rep, axis=1)
            nb = Lq // W
            qb = q.reshape(Bq, H, nb, W, HD)
            kp = jnp.pad(k, ((0, 0), (0, 0), (W, W), (0, 0))).reshape(Bq, H, nb + 2, W, HD)
            vp = jnp.pad(v, ((0, 0), (0, 0), (W, W), (0, 0))).reshape(Bq, H, nb + 2, W, HD)
            k3 = jnp.concatenate([kp[:, :, i:i + nb] for i in range(3)], axis=3)
            v3 = jnp.concatenate([vp[:, :, i:i + nb] for i in range(3)], axis=3)
            scores = jnp.einsum('bhnqd,bhnkd->bhnqk', qb, k3) / math.sqrt(HD)
            qi = jnp.arange(W)
            kj = jnp.arange(3 * W)
            rel = kj[None, :] - W - qi[:, None]
            win_mask = jnp.abs(rel) <= W
            kglob = (jnp.arange(nb)[:, None] - 1) * W + kj[None, :]
            pad_mask = (kglob >= 0) & (kglob < Lq)
            bias = rel_bias[jnp.clip(rel + W, 0, 2 * W)].transpose(2, 0, 1)
            scores = scores + bias[None, :, None, :, :]
            mask = win_mask[None, :, :] & pad_mask[:, None, :]
            scores = jnp.where(mask[None, None], scores, jnp.asarray(-1000000000.0, scores.dtype))
            attn = jax.nn.softmax(scores, axis=-1)
            ao = jnp.einsum('bhnqk,bhnkd->bhnqd', attn, v3)
            ao = ao.reshape(Bq, H, Lq, HD).transpose(0, 2, 1, 3).reshape(Bq, Lq, Dq)
            attn_out = ao @ wo
            kernel = w_conv.T[:, None, :]
            xc = jax.lax.conv_general_dilated(x, kernel, (1,), [(3, 0)], dimension_numbers=('NWC', 'WIO', 'NWC'), feature_group_count=Dq)
            conv_out = jax.nn.silu(xc + b_conv)
            wm = x @ w_wm + b_wm
            dec = jax.nn.gelu(episodic @ w_dc1 + b_dc1, approximate=False) @ w_dc2 + b_dc2
            es = jnp.einsum('bld,sd->bls', x, dec[0]) / math.sqrt(Dq)
            eo = jax.nn.softmax(es, axis=-1) @ dec[0]
            mem_out = wm + 0.3 * eo
            return x + rw[0] * attn_out + rw[1] * ssm_out + rw[2] * conv_out + rw[3] * mem_out
        return _forward(x, ln_g, ln_b, w_xproj, w_dt, b_dt, A_log, D_ssm, w_ssm_out, wq, wk, wv, wo, rel_bias, w_wm, b_wm, episodic, w_dc1, b_dc1, w_dc2, b_dc2, w_imp, b_imp, w_conv, b_conv)

    def _L0_ffn_ref(x, kernel, bias, a, b):
        import jax, jax.numpy as jnp
        import numpy as np
        INT4_QMAX = 7.0

        def simulate_quantize_int4(w):
            scale = jnp.max(jnp.abs(w)) / INT4_QMAX
            q = jnp.clip(jnp.round(w / scale), -8.0, 7.0)
            return q * scale
        w = simulate_quantize_int4(kernel)
        y = jnp.einsum('bsd,df->bsf', x, w) + bias
        lora = jnp.einsum('bsr,rf->bsf', jnp.einsum('bsd,dr->bsr', x, a), b)
        return y + lora
    x = L0_attn_x
    x = x + _L0_attn_ref(_layernorm(x, axis=-1), L0_attn_ln_g, L0_attn_ln_b, L0_attn_w_xproj, L0_attn_w_dt, L0_attn_b_dt, L0_attn_A_log, L0_attn_D_ssm, L0_attn_w_ssm_out, L0_attn_wq, L0_attn_wk, L0_attn_wv, L0_attn_wo, L0_attn_rel_bias, L0_attn_w_wm, L0_attn_b_wm, L0_attn_episodic, L0_attn_w_dc1, L0_attn_b_dc1, L0_attn_w_dc2, L0_attn_b_dc2, L0_attn_w_imp, L0_attn_b_imp, L0_attn_w_conv, L0_attn_b_conv)
    x = x + _L0_ffn_ref(_layernorm(x, axis=-1), L0_ffn_kernel, L0_ffn_bias, L0_ffn_a, L0_ffn_b)
    return x

_drawn_inputs = setup_inputs


def setup_inputs(seed=0):
    import zlib

    import numpy as np

    out = dict(_drawn_inputs(seed))
    spreads = {'L0_attn_ln_g': (1.0, 0.6),
     'L0_attn_ln_b': (0.0, 0.8),
     'L0_attn_b_dt': (0.0, 0.8),
     'L0_attn_D_ssm': (1.0, 0.6),
     'L0_attn_b_wm': (0.0, 0.723),
     'L0_attn_b_dc1': (0.0, 2.0),
     'L0_attn_b_dc2': (0.0, 2.0),
     'L0_attn_b_conv': (0.0, 2.0)}
    factors = {'L0_attn_w_xproj': 3.333,
     'L0_attn_w_dt': 8.0,
     'L0_attn_A_log': 8.0,
     'L0_attn_wq': 8.0,
     'L0_attn_wk': 8.0,
     'L0_attn_wv': 8.0,
     'L0_attn_wo': 8.0,
     'L0_attn_rel_bias': 64.0,
     'L0_attn_episodic': 64.0,
     'L0_attn_w_dc1': 64.0,
     'L0_attn_w_dc2': 22.906,
     'L0_attn_w_conv': 7.839,
     'L0_ffn_a': 8.0,
     'L0_ffn_b': 8.0,
     'L0_attn_w_wm': 3.52}
    for name, (base, spread) in spreads.items():
        noise = np.random.default_rng([zlib.crc32(name.encode()), seed]).standard_normal(out[name].shape)
        drawn = base * np.exp(spread * noise) if base else spread * noise
        out[name] = jnp.asarray(drawn.astype(out[name].dtype))
    for name, factor in factors.items():
        out[name] = (out[name] * factor).astype(out[name].dtype)
    return out
```

```python
from contextlib import ExitStack

import concourse.bass as bass
from concourse import mybir

F32 = mybir.dt.float32
BF16 = mybir.dt.bfloat16
ALU = mybir.AluOpType
ACT = mybir.ActivationFunctionType
AX = mybir.AxisListType

NB = 8
L = 512
D = 128
NT = L // 128
H, KVH, HD = 16, 4, 8
REP = H // KVH
W = 32
NBLK = L // W
HALO = W
LP = L + 2 * HALO
NS = 64
DTR = 64
SE = 512
CD = 16
TAPS = 4
RANK = 16
EPS = 1e-5
MASKED = -1.0e9
UNITS = D // 2
GROUPS = UNITS // 4
RW_ATTN, RW_SSM, RW_CONV, RW_MEM, MEM_MIX = 0.2, 0.45, 0.15, 0.2, 0.3
ROUND = 12582912.0
RELPAD = 160

N_PRE, N_MEM, N_TAIL = 12, 9, 4
PRE = {n: i for i, n in enumerate(
    ["xaT", "xnT", "dti", "dtpre", "B", "C", "q0", "q1", "q2", "q3", "k", "v"])}
MEM = {n: i for i, n in enumerate(
    ["es0", "conv", "es1", "pt0", "es2", "pt1", "es3", "pt2", "pt3"])}
TAIL = {n: i for i, n in enumerate(["proj", "back", "zT", "ffn"])}

PE_SLOT = {13: ("t", "back"), 15: ("p", "xaT"), 17: ("p", "xnT"), 19: ("p", "dti"),
           21: ("t", "zT"), 23: ("t", "ffn"), 25: ("p", "dtpre"), 27: ("p", "B"), 29: ("p", "C"),
           31: ("m", "es0"), 34: ("m", "conv"), 37: ("m", "es1"), 40: ("m", "pt0"),
           42: ("m", "es2"), 45: ("m", "pt1"), 47: ("m", "es3"), 50: ("m", "pt2"),
           52: ("p", "q0"), 54: ("m", "pt3"), 55: ("p", "q1"), 57: ("p", "q2"), 59: ("p", "q3"),
           61: ("p", "k"), 62: ("p", "v")}

LN = {n: i + 1 for i, n in enumerate(
    ["stats", "aggr", "ve", "r", "vr", "vrr", "ve2", "r2", "xa", "xn"])}
N_LN = len(LN)
SP = {n: i + 1 for i, n in enumerate(
    ["abs", "relu", "exp", "ln", "t1", "t2", "t3", "dt", "u", "hi0", "hi1", "r0", "r1", "mid0",
     "mid1", "lo0", "lo1"])}
N_SP = len(SP)
CV = {n: i + 1 for i, n in enumerate(["v", "abs", "exp", "ln", "relu", "sum", "sig", "cs"])}
N_CV = len(CV)
L2 = {n: i + 1 for i, n in enumerate(["x1", "stats", "aggr", "ve", "r", "z", "x1b"])}
N_L2 = len(L2)
N_PARTS_DMA = 24


def hybrid_block_kernel(nc, x, ln_g, ln_b, w_xproj, w_dt, b_dt, A_log, D_ssm, w_ssm_out, wq, wk, wv,
                        wo, rel_bias, w_wm, b_wm, episodic, w_dc1, b_dc1, w_dc2, b_dc2, w_conv,
                        b_conv, ffn_w, ffn_bias, ffn_a, ffn_b, rel_dram, out):
    ctx = ExitStack()
    with ctx:
        def sb(name, shape, dt=F32):
            return ctx.enter_context(nc.sbuf_tensor(name, shape, dt))

        def sem(name):
            return ctx.enter_context(nc.semaphore(name))

        bank = [ctx.enter_context(nc.psum_tensor(f"bank{i}", [128, 512], F32)) for i in range(8)]
        dtP, uP, yP, sP, ptP, jobP = bank[0:2], bank[2:4], bank[4], bank[5], bank[6], bank[7]

        ident = sb("ident", [128, 128])
        sel_bc = sb("sel_bc", [96, GROUPS, 2, NS], BF16)
        sel_red = sb("sel_red", [128, GROUPS, 32])
        mhalf = sb("mhalf", [128, NT])
        eps_t = sb("eps_t", [128, NT])
        w_dti = sb("w_dti", [D, DTR])
        w_B2 = sb("w_B2", [D, 2, NS])
        w_C2 = sb("w_C2", [D, 2, NS])
        w_dt_s = sb("w_dt_s", [DTR, D])
        wq_raw = sb("wq_raw", [D, KVH, REP, HD])
        wk_raw = sb("wk_raw", [D, KVH, HD])
        wq_p = sb("wq_p", [D, REP, KVH, 32])
        wk_p = sb("wk_p", [D, KVH, 32])
        wv_s = sb("wv_s", [D, KVH * HD])
        wo_p = sb("wo_p", [128, REP, D])
        w_ssm = sb("w_ssm", [D, D])
        w_x = sb("w_x", [D, D])
        cs_id = sb("cs_id", [D, D])
        convdiag = sb("convdiag", [D, TAPS, D])
        ddiag = sb("ddiag", [D, D])
        cols = sb("cols", [128, 8])
        g_col, b_col, bdt_col, bconv_col, bwm_col, bdc2_col, dssm_col = (cols[:, i:i + 1] for i in range(7))
        bwm_s = sb("bwm_s", [128, 1])
        bdc1_col = sb("bdc1_col", [DTR, 1])
        wconv_s = sb("wconv_s", [128, TAPS])
        alog2 = sb("alog2", [D, 2, NS])
        A_rep = sb("A_rep", [128, UNITS])
        epi = sb("epi", [128, 4, CD])
        w_dc1_s = sb("w_dc1_s", [CD, 64])
        w_dc2_s = sb("w_dc2_s", [64, D])
        decTs = sb("decTs", [D, SE])
        dec_m = sb("dec_m", [128, 4, D])
        rel_raw = sb("rel_raw", [2 * W + 1, H])
        relpad = sb("relpad", [H, RELPAD])
        bias3 = sb("bias3", [128, 3, KVH, 3 * W])
        wf = sb("wf", [D, D])
        wf_abs = sb("wf_abs", [D, D])
        wmax = sb("wmax", [D, 1])
        wmax1 = sb("wmax1", [1, 1])
        ones_row = sb("ones_row", [1, 128])
        wsc = sb("wsc", [128, 4])
        W2 = sb("W2", [D, D])
        fa = sb("fa", [D, RANK])
        faT = sb("faT", [RANK, D])
        fb = sb("fb", [RANK, D])
        biasrep = sb("biasrep", [128, D])

        x_sb = sb("x_sb", [128, NB, NT, D])
        st = sb("st", [128, NT, 6])
        mv = sb("mv", [128, NT, 2])
        ve = sb("ve", [128, NT])
        rr = sb("rr", [128, NT])
        vr = sb("vr", [128, NT])
        rr2 = sb("rr2", [128, NT])
        xa = sb("xa", [128, NT, D])
        xn = sb("xn", [128, NT, D])
        xaT = [sb(f"xaT{p}", [D, LP]) for p in range(2)]
        xnT = sb("xnT", [D, L])
        B2 = [sb(f"B2_{p}", [128, L]) for p in range(2)]
        C2 = [sb(f"C2_{p}", [128, L]) for p in range(2)]
        sp_e = sb("sp_e", [D, L])
        sp_r = sb("sp_r", [D, L])
        sp_l = sb("sp_l", [D, L])
        sp_t = sb("sp_t", [D, L])
        uv = sb("uv", [D, L])
        dti, dtv, res = sp_l[0:DTR, :], sp_t, (sp_e, sp_r)
        parts = [sb(f"parts{i}", [D, 3, L], BF16) for i in range(2)]
        spread = [[sb(f"spread{i}_{p}", [96, 4, L], BF16) for p in range(2)] for i in range(2)]
        q4 = sb("q4", [128, NBLK, REP, W])
        k4 = sb("k4", [128, KVH, LP])
        vw = sb("vw", [3 * W, NBLK, KVH, 32])
        dbx = sb("dbx", [128, 2, L])
        hst = sb("hst", [128, 4, L])
        prod = sb("prod", [128, 8, L])
        epiT, hidT, decT = prod[0:CD, 0, :], prod[0:64, 1, :], prod[:, 2, :]
        yT = sb("yT", [D, L])
        s_sb = sb("s_sb", [128, 2, KVH, 3 * W])
        nmax = sb("nmax", [128, 2, KVH])
        prob = sb("prob", [128, 4, KVH, 3 * W])
        psum_r = sb("psum_r", [128, 4, KVH])
        pinv = sb("pinv", [128, 4, KVH])
        probT = sb("probT", [3 * W, KVH, 128])
        ao4 = sb("ao4", [128, REP, L])
        mmx = sb("mmx", [128, NT])
        msum = sb("msum", [128, NT])
        minv = sb("minv", [128, NT])
        mprob = sb("mprob", [128, 2, SE])
        mprobT = sb("mprobT", [128, 4, L])
        cv_v = sb("cv_v", [D, L])
        cv_a = sb("cv_a", [D, L])
        cv_l = sb("cv_l", [D, L])
        cv_m = sb("cv_m", [D, L])
        cs = sb("cs", [D, L])
        fT = sb("fT", [D, L])
        x1 = sb("x1", [128, NT, D])
        x1b = sb("x1b", [128, NT, D])
        st2 = sb("st2", [128, NT, 6])
        mv2 = sb("mv2", [128, NT, 2])
        vz = sb("vz", [128, NT])
        rz = sb("rz", [128, NT])
        z = sb("z", [128, NT, D])
        zT, outb = fT, x1b

        x_in = [sem(f"x_in{i}") for i in range(2)]
        w_in = sem("w_in")
        rel_out = sem("rel_out")
        bias_in = sem("bias_in")
        bias_done = sem("bias_done")
        pool_zeros = sem("pool_zeros")
        w_scaled = sem("w_scaled")
        const_ready = sem("const_ready")
        init = sem("init")
        dt_ready, u_ready = sem("dt_ready"), sem("u_ready")
        exp_done, dbx_done, scan_done = sem("exp_done"), sem("dbx_done"), sem("scan_done")
        prod_done, red_done, y_started, y_evac = sem("prod_done"), sem("red_done"), sem("y_started"), sem("y_evac")
        s_ready, s_biased, s_max = sem("s_ready"), sem("s_biased"), sem("s_max")
        p_exp, p_inv, p_norm = sem("p_exp"), sem("p_inv"), sem("p_norm")
        pt_ready, pt_evac, pv_ready, ao_evac = sem("pt_ready"), sem("pt_evac"), sem("pv_ready"), sem("ao_evac")
        ready = {f: sem(f"{f}_job_ready") for f in "pmt"}
        done = {f: sem(f"{f}_job_done") for f in "pmt"}
        ln_step, sp_step, cv_step, l2_step = sem("ln_step"), sem("sp_step"), sem("cv_step"), sem("l2_step")
        parts_in = sem("parts_in")
        m_max, m_exp, m_inv, m_norm = sem("m_max"), sem("m_exp"), sem("m_inv"), sem("m_norm")
        out_ready, out_done = sem("out_ready"), sem("out_done")

        COUNT = {"p": N_PRE, "m": N_MEM, "t": N_TAIL}
        INDEX = {"p": PRE, "m": MEM, "t": TAIL}

        def wait(eng, s, value):
            if isinstance(value, int) and value <= 0:
                return
            eng.wait_ge(s, value)

        def job_count(fam, B, name):
            return B * COUNT[fam] + INDEX[fam][name] + 1

        def wait_job(eng, fam, B, name):
            wait(eng, ready[fam], job_count(fam, B, name))

        def run_batches(eng, front, body, tail):
            front(0, 0)
            body(0, 0)
            with eng.Fori(0, (NB - 2) // 2) as k:
                body(k * 2 + 1, 1)
                body(k * 2 + 2, 0)
            body(NB - 1, 1)
            tail(NB - 1, 1)

        def first(B):
            return isinstance(B, int) and B == 0

        def last(B):
            return isinstance(B, int) and B == NB - 1

        INIT = {n: i + 1 for i, n in enumerate(
            ["A_t", "A_e", "A_n", "epi_t", "epi_c", "hid", "gelu", "dec", "dec_c", "dec_s", "dec_t", "dec_m",
             "rel_t", "rel_c",
             "w_abs", "w_max", "w_maxt", "w_max1", "w_bc", "w_c", "w_r", "w_s", "w_q1", "w_q2", "w_q3",
             "fa_t", "fa_c", "ab", "W2"])}
        N_W_DMA = 34

        block = ctx.enter_context(nc.Block())

        @block.sync
        def _(sp):
            for b in range(NB):
                sp.dma_start(x_sb[:, b, :, :], x[b].rearrange("(t p) d -> p t d", p=128)) \
                    .then_inc(x_in[min(b, 1)], 16)
            sp.wait_ge(init, INIT["rel_c"])
            sp.dma_start(rel_dram, relpad[:, :].unsqueeze(1).to_broadcast([H, W, RELPAD])).then_inc(rel_out, 16)
            sp.wait_ge(rel_out, 16)
            flat = rel_dram.rearrange("h q k -> (h q k)")
            for v in range(3):
                for r in range(REP):
                    src = bass.AP(flat.tensor, flat.offset + r * W * RELPAD + W,
                                  [[RELPAD - 1, W], [REP * W * RELPAD, KVH], [1, 3 * W]])
                    sp.dma_start(bias3[r * W:(r + 1) * W, v, :, :], src).then_inc(bias_in, 16)

            def send_parts(B, p):
                wait(sp, u_ready, (B - 1) * UNITS)
                wait(sp, dt_ready, (B - 1) * UNITS)
                for i in range(2):
                    wait(sp, sp_step, B * N_SP + SP[f"lo{i}"])
                    for part in range(3):
                        for c in range(4):
                            sp.dma_start(spread[i][p][32 * part:32 * part + 32, c, :],
                                         parts[i][32 * c:32 * c + 32, part, :]).then_inc(parts_in, 16)

            def store(B, p):
                wait(sp, out_ready, B + 1)
                if isinstance(B, int):
                    dst = out[B]
                else:
                    dst = out[bass.ds(B, 1)].rearrange("a l d -> (a l) d")
                sp.dma_start(dst.rearrange("(t p) d -> p t d", p=128), outb[:, :, :]).then_inc(out_done, 16)

            def body(B, p):
                if not first(B):
                    store(B - 1, 1 - p)
                if not last(B):
                    send_parts(B + 1, 1 - p)

            run_batches(sp, send_parts, body, store)
            sp.wait_ge(out_done, 16 * NB)

        @block.scalar
        def _(act):
            n = 0

            def load(dst, src):
                nonlocal n
                act.dma_start(dst, src).then_inc(w_in, 16)
                n += 1

            def column(v):
                return v.rearrange("(p a) -> p a", a=1)

            load(g_col, column(ln_g))
            load(b_col, column(ln_b))
            load(w_dti[:, :], w_xproj[:, 0:DTR])
            for j in range(2):
                load(w_B2[:, j, :], w_xproj[:, DTR:DTR + NS])
                load(w_C2[:, j, :], w_xproj[:, DTR + NS:DTR + 2 * NS])
                load(alog2[:, j, :], A_log)
            load(w_dt_s[:, :], w_dt)
            load(bdt_col, column(b_dt))
            load(wq_raw[:, :, :, :].rearrange("d a b c -> d (a b c)"), wq)
            load(wk_raw[:, :, :].rearrange("d a b -> d (a b)"), wk)
            load(wv_s[:, :], wv)
            load(bconv_col, column(b_conv))
            load(bwm_col, column(b_wm))
            load(bdc2_col, column(b_dc2))
            load(dssm_col, column(D_ssm))
            load(wconv_s[:, :], w_conv)
            load(epi[:, :, :], episodic[0].rearrange("(c p) k -> p c k", p=128))
            load(w_dc1_s[:, :], w_dc1)
            load(bdc1_col[:, :], column(b_dc1))
            load(w_dc2_s[:, :], w_dc2)
            load(rel_raw[:, :], rel_bias)
            load(wf[:, :], ffn_w)
            load(fa[:, :], ffn_a)
            load(fb[:, :], ffn_b)
            load(biasrep[:, :], ffn_bias.rearrange("(a n) -> a n", a=1).to_broadcast([128, D]))
            load(w_ssm[:, :], w_ssm_out)
            load(w_x[:, :], w_wm)
            act.wait_ge(const_ready, 1)
            for g in range(KVH):
                act.dma_start(wo_p[32 * g:32 * g + HD, :, :],
                              wo[g * REP * HD:(g + 1) * REP * HD, :].rearrange("(r h) e -> h r e", r=REP)) \
                    .then_inc(w_in, 16)
                n += 1
            assert n == N_W_DMA, n
            act.wait_ge(w_in, 16 * n)

            act.wait_ge(init, INIT["A_t"])
            for j in range(2):
                ins = nc.scalar.activation(A_rep[64 * j:64 * j + 64, :],
                                           jobP[64 * j:64 * j + 64, 0:D].rearrange("p (g j) -> p g j", j=2)[:, :, j],
                                           ACT.Exp)
            ins.then_inc(init, 1)
            act.wait_ge(init, INIT["A_e"])
            nc.scalar.activation(A_rep[:, :], A_rep[:, :], ACT.Copy, scale=-1.0).then_inc(init, 1)
            act.wait_ge(init, INIT["epi_t"])
            nc.scalar.activation(epiT[:, :], jobP[0:CD, :], ACT.Copy).then_inc(init, 1)
            act.wait_ge(init, INIT["hid"])
            nc.scalar.activation(hidT[:, :], jobP[0:64, :], ACT.Gelu, bias=bdc1_col[:, :]).then_inc(init, 1)
            act.wait_ge(init, INIT["dec"])
            nc.scalar.activation(decT[:, :], jobP[:, :], ACT.Identity, bias=bdc2_col).then_inc(init, 1)
            act.wait_ge(init, INIT["dec_c"])
            nc.scalar.activation(decTs[:, :], decT[:, :], ACT.Copy, scale=float(D) ** -0.5).then_inc(init, 1)
            act.wait_ge(init, INIT["dec_t"])
            nc.scalar.activation(dec_m[:, :, :].rearrange("p c d -> p (c d)"), jobP[:, :], ACT.Copy,
                                 scale=RW_MEM * MEM_MIX).then_inc(init, 1)
            act.wait_ge(init, INIT["rel_t"])
            nc.scalar.activation(relpad[:, W:W + 2 * W + 1], jobP[0:H, 0:2 * W + 1], ACT.Copy).then_inc(init, 1)
            nc.scalar.activation(wf_abs[:, :], wf[:, :], ACT.Abs).then_inc(init, 1)
            act.wait_ge(init, INIT["w_bc"])
            nc.scalar.activation(wsc[:, 0:1], jobP[:, 0:1], ACT.Copy).then_inc(init, 1)
            act.wait_ge(init, INIT["fa_t"])
            nc.scalar.activation(faT[:, :], jobP[0:RANK, 0:D], ACT.Copy).then_inc(init, 1)

            def scale_xn(B):
                wait(act, ln_step, B * N_LN + LN["xa"])
                for t in range(NT):
                    ins = nc.scalar.activation(xn[:, t, :], xa[:, t, :], ACT.Copy, scale=rr2[:, t:t + 1])
                ins.then_inc(ln_step, 1)

            def pre_job(name, B, p):
                wait_job(act, "p", B, name)
                if name == "xaT":
                    ins = nc.scalar.activation(xaT[p][:, HALO:HALO + L], jobP[:, :], ACT.Copy)
                elif name == "xnT":
                    ins = nc.scalar.activation(xnT[:, :], jobP[:, :], ACT.Identity, bias=b_col, scale=g_col)
                elif name == "dti":
                    ins = nc.scalar.activation(dti[:, :], jobP[0:DTR, :], ACT.Copy)
                elif name in "BC":
                    ins = nc.scalar.activation((B2 if name == "B" else C2)[p][:, :], jobP[:, :], ACT.Copy)
                elif name == "dtpre":
                    nc.scalar.activation(sp_e[:, :], jobP[:, :], ACT.Abs, bias=bdt_col).then_inc(sp_step, 1)
                    nc.scalar.activation(sp_r[:, :], jobP[:, :], ACT.Relu, bias=bdt_col).then_inc(sp_step, 1)
                    act.wait_ge(sp_step, B * N_SP + SP["relu"])
                    act.sem_inc(done["p"], 1)
                    return
                elif name == "k":
                    for g in range(KVH):
                        ins = nc.scalar.activation(k4[32 * g:32 * g + 32, g, HALO:HALO + L],
                                                   jobP[32 * g:32 * g + 32, :], ACT.Copy)
                elif name == "v":
                    ins = nc.scalar.activation(vw[:, :, :, 0:HD],
                                               jobP[0:3 * W, :].rearrange("p (n g h) -> p n g h", g=KVH, h=HD),
                                               ACT.Copy)
                else:
                    r = int(name[1])
                    ins = nc.scalar.activation(q4[:, :, r, :], jobP[:, :].rearrange("p (n q) -> p n q", q=W),
                                               ACT.Copy)
                ins.then_inc(done["p"], 1)

            def softplus_logs(B):
                nc.scalar.activation(sp_e[:, :], sp_e[:, :], ACT.Exp, scale=-1.0).then_inc(sp_step, 1)
                act.wait_ge(sp_step, B * N_SP + SP["exp"])
                nc.scalar.activation(sp_l[:, :], sp_e[:, :], ACT.Ln, bias=1.0).then_inc(sp_step, 1)

            def high_parts(B):
                wait(act, parts_in, B * 16 * N_PARTS_DMA)
                wait(act, sp_step, B * N_SP + SP["u"])
                for i, v in enumerate((dtv, uv)):
                    nc.scalar.activation(parts[i][:, 0, :], v[:, :], ACT.Copy).then_inc(sp_step, 1)

            def mid_parts(B):
                wait(act, sp_step, B * N_SP + SP["r1"])
                for i in range(2):
                    nc.scalar.activation(parts[i][:, 1, :], res[i][:, :], ACT.Copy).then_inc(sp_step, 1)

            def front(B, p):
                scale_xn(B)
                for name in ("xaT", "xnT", "dti", "dtpre"):
                    pre_job(name, B, p)
                softplus_logs(B)
                for name in ("B", "C"):
                    pre_job(name, B, p)
                high_parts(B)
                mid_parts(B)
                for name in ("q0", "q1", "q2", "q3", "k", "v"):
                    pre_job(name, B, p)

            def unit_exp(B, s):
                i, q = divmod(s, 4)
                wait(act, dt_ready, B * UNITS + s + 1)
                g = GROUPS * q + i
                nc.scalar.activation(dtP[s % 2][:, :], dtP[s % 2][:, :], ACT.Exp, scale=A_rep[:, g:g + 1]) \
                    .then_inc(exp_done, 1)

            def y_copy(B):
                wait(act, red_done, (B + 1) * GROUPS)
                wait(act, ready["t"], B * N_TAIL)
                nc.scalar.activation(yT[:, :], yP[:, :], ACT.Copy).then_inc(y_evac, 1)

            def probabilities(B, k):
                wait(act, s_max, B * NBLK + k + 1)
                wait(act, pt_ready, B * NBLK + k - 3)
                for g in range(KVH):
                    ins = nc.scalar.activation(prob[:, k % 4, g, :], s_sb[:, k % 2, g, :], ACT.Exp,
                                               bias=nmax[:, k % 2, g:g + 1], accum_out=psum_r[:, k % 4, g:g + 1])
                ins.then_inc(p_exp, 1)

            def probT_copy(B, k):
                wait(act, pt_ready, B * NBLK + k + 1)
                wait(act, pv_ready, B * NBLK + k)
                nc.scalar.activation(probT[:, :, :].rearrange("p g t -> p (g t)"), ptP[0:3 * W, :], ACT.Copy) \
                    .then_inc(pt_evac, 1)

            def ao_copy(B, k):
                wait(act, pv_ready, B * NBLK + k + 1)
                if k == 0:
                    wait(act, ready["t"], B * N_TAIL - N_TAIL + 1)
                nc.scalar.activation(ao4[:, :, k * W:(k + 1) * W],
                                     ptP[:, 0:128].rearrange("p (r q) -> p r q", r=REP), ACT.Copy).then_inc(ao_evac, 1)

            def mem_exp(B, t):
                wait(act, m_max, B * NT + t + 1)
                if t >= 2:
                    wait_job(act, "m", B, f"pt{t - 2}")
                ins = nc.scalar.activation(mprob[:, t % 2, :], jobP[:, :], ACT.Exp, bias=mmx[:, t:t + 1],
                                           accum_out=msum[:, t:t + 1])
                ins.then_inc(m_exp, 1)
                act.wait_ge(m_exp, B * NT + t + 1)
                act.sem_inc(done["m"], 1)

            def memT_copy(B, t):
                wait_job(act, "m", B, f"pt{t}")
                if t == 0:
                    wait(act, ready["t"], B * N_TAIL - N_TAIL + 1)
                nc.scalar.activation(mprobT[:, :, t * 128:(t + 1) * 128],
                                     jobP[:, :].rearrange("p (c t) -> p c t", c=4), ACT.Copy).then_inc(done["m"], 1)

            def conv_logs(B):
                wait_job(act, "m", B, "conv")
                nc.scalar.activation(cv_v[:, :], jobP[:, :], ACT.Identity, bias=bconv_col).then_inc(cv_step, 1)
                act.wait_ge(cv_step, B * N_CV + CV["v"])
                act.sem_inc(done["m"], 1)
                nc.scalar.activation(cv_a[:, :], cv_v[:, :], ACT.Abs).then_inc(cv_step, 1)
                act.wait_ge(cv_step, B * N_CV + CV["abs"])
                nc.scalar.activation(cv_a[:, :], cv_a[:, :], ACT.Exp, scale=-1.0).then_inc(cv_step, 1)
                act.wait_ge(cv_step, B * N_CV + CV["exp"])
                nc.scalar.activation(cv_l[:, :], cv_a[:, :], ACT.Ln, bias=1.0).then_inc(cv_step, 1)
                nc.scalar.activation(cv_m[:, :], cv_v[:, :], ACT.Relu, scale=-1.0).then_inc(cv_step, 1)

            def conv_sigmoid(B):
                wait(act, cv_step, B * N_CV + CV["sum"])
                nc.scalar.activation(cv_a[:, :], cv_l[:, :], ACT.Exp, scale=-1.0).then_inc(cv_step, 1)

            def proj_copy(B):
                wait_job(act, "t", B, "proj")
                nc.scalar.activation(fT[:, :], jobP[:, :], ACT.Identity, bias=bwm_s[:, :]).then_inc(done["t"], 1)

            def zT_copy(B):
                wait_job(act, "t", B, "zT")
                nc.scalar.activation(zT[:, :], jobP[:, :], ACT.Copy).then_inc(done["t"], 1)

            PRE_AT = {16: "xaT", 18: "xnT", 20: "dti", 26: "dtpre", 28: "B", 30: "C", 53: "q0", 56: "q1",
                      58: "q2", 60: "q3", 62: "k", 63: "v"}
            EXP_AT = {33: 0, 39: 1, 44: 2, 49: 3}
            MT_AT = {41: 0, 46: 1, 51: 2, 55: 3}

            def body(B, p):
                for s in range(UNITS):
                    unit_exp(B, s)
                    if not first(B):
                        if s == 4:
                            y_copy(B - 1)
                        if s == 12:
                            proj_copy(B - 1)
                        if s == 22:
                            zT_copy(B - 1)
                    if s >= 5 and (s - 5) % 3 == 0 and (s - 5) // 3 < NBLK:
                        probabilities(B, (s - 5) // 3)
                    if s >= 11 and (s - 11) % 3 == 0 and (s - 11) // 3 < NBLK:
                        probT_copy(B, (s - 11) // 3)
                    if s >= 12 and (s - 12) % 3 == 0 and (s - 12) // 3 < NBLK:
                        ao_copy(B, (s - 12) // 3)
                    if s in EXP_AT:
                        mem_exp(B, EXP_AT[s])
                    if s in MT_AT:
                        memT_copy(B, MT_AT[s])
                    if s == 35:
                        conv_logs(B)
                    if s == 43:
                        conv_sigmoid(B)
                    if not last(B):
                        if s == 12:
                            scale_xn(B + 1)
                        if s in PRE_AT:
                            pre_job(PRE_AT[s], B + 1, 1 - p)
                        if s == 27:
                            softplus_logs(B + 1)
                        if s == 36:
                            high_parts(B + 1)
                        if s == 41:
                            mid_parts(B + 1)

            def tail(B, p):
                y_copy(B)
                proj_copy(B)
                zT_copy(B)

            run_batches(act, front, body, tail)

        @block.tensor
        def _(pe):
            mm = nc.tensor.matmul

            def transposes(srcs, rows, step):
                for c, src in enumerate(srcs):
                    ins = nc.tensor.transpose(jobP[0:rows, c * step:(c + 1) * step], src, ident[:, :])
                return ins

            pe.wait_ge(const_ready, 2)
            pe.wait_ge(w_in, 16 * N_W_DMA)
            nc.tensor.transpose(jobP[:, 0:D], alog2[:, :, :].rearrange("p j n -> p (j n)"), ident[:, :]).then_inc(init, 1)
            pe.wait_ge(init, INIT["A_n"])
            transposes([epi[:, c, :] for c in range(4)], CD, 128).then_inc(init, 1)
            pe.wait_ge(init, INIT["epi_c"])
            mm(jobP[0:64, :], w_dc1_s[:, :], epiT[:, :], start=True, stop=True).then_inc(init, 1)
            pe.wait_ge(init, INIT["gelu"])
            mm(jobP[:, :], w_dc2_s[:, :], hidT[:, :], start=True, stop=True).then_inc(init, 1)
            pe.wait_ge(init, INIT["dec_s"])
            transposes([decT[:, c * 128:(c + 1) * 128] for c in range(4)], 128, 128).then_inc(init, 1)
            pe.wait_ge(init, INIT["dec_m"])
            nc.tensor.transpose(jobP[0:H, 0:2 * W + 1], rel_raw[:, :], ident[0:2 * W + 1, 0:2 * W + 1]).then_inc(init, 1)
            pe.wait_ge(init, INIT["w_max"])
            nc.tensor.transpose(jobP[0:1, 0:D], wmax[:, :], ident[:, :]).then_inc(init, 1)
            pe.wait_ge(init, INIT["w_max1"])
            mm(jobP[:, 0:1], ones_row[:, :], wmax1[:, :], start=True, stop=True).then_inc(init, 1)
            pe.wait_ge(init, INIT["w_q3"])
            nc.tensor.transpose(jobP[0:RANK, 0:D], fa[:, :], ident[:, :]).then_inc(init, 1)
            pe.wait_ge(init, INIT["fa_c"])
            mm(jobP[:, 0:D], faT[:, :], fb[:, :], start=True, stop=True).then_inc(init, 1)
            pe.wait_ge(init, INIT["W2"])
            pe.wait_ge(const_ready, 4)
            pe.wait_ge(w_scaled, 1)

            before = [None]

            def fill(fam, B, name):
                if before[0] is not None:
                    f, b, n = before[0]
                    wait(pe, done[f], job_count(f, b, n))

            def filled(ins, fam, B, name):
                ins.then_inc(ready[fam], 1)
                before[0] = (fam, B, name)

            def pre_job(name, B, p):
                fill("p", B, name)
                if name == "xaT":
                    wait(pe, ln_step, B * N_LN + LN["xa"])
                    ins = transposes([xa[:, t, :] for t in range(NT)], 128, 128)
                elif name == "xnT":
                    wait(pe, ln_step, B * N_LN + LN["xn"])
                    ins = transposes([xn[:, t, :] for t in range(NT)], 128, 128)
                elif name == "dti":
                    wait(pe, done["p"], job_count("p", B, "xnT"))
                    ins = mm(jobP[0:DTR, :], w_dti[:, :], xnT[:, :], start=True, stop=True)
                elif name == "dtpre":
                    wait(pe, done["p"], job_count("p", B, "dti"))
                    ins = mm(jobP[:, :], w_dt_s[:, :], dti[:, :], start=True, stop=True)
                elif name in "BC":
                    w = w_B2 if name == "B" else w_C2
                    ins = mm(jobP[:, :], w[:, :, :].rearrange("d j n -> d (j n)"), xnT[:, :], start=True, stop=True)
                elif name == "k":
                    ins = mm(jobP[:, :], wk_p[:, :, :].rearrange("d g h -> d (g h)"), xaT[p][:, HALO:HALO + L],
                             start=True, stop=True)
                elif name == "v":
                    for n in range(NBLK):
                        ins = mm(jobP[0:3 * W, n * 32:(n + 1) * 32], xaT[p][:, n * W:n * W + 3 * W], wv_s[:, :],
                                 start=True, stop=True)
                else:
                    r = int(name[1])
                    ins = mm(jobP[:, :], wq_p[:, r, :, :].rearrange("d g h -> d (g h)"), xaT[p][:, HALO:HALO + L],
                             start=True, stop=True)
                filled(ins, "p", B, name)

            def front(B, p):
                for name in PRE:
                    pre_job(name, B, p)

            def unit_spread(B, p, s):
                i, q = divmod(s, 4)
                if s == 0:
                    wait(pe, parts_in, (B + 1) * 16 * N_PARTS_DMA)
                sel = sel_bc[:, i, :, :].rearrange("k j n -> k (j n)")
                wait(pe, scan_done, B * UNITS + s - 1)
                mm(dtP[s % 2][:, :], sel, spread[0][p][:, q, :], start=True, stop=True).then_inc(dt_ready, 1)
                wait(pe, dbx_done, B * UNITS + s - 1)
                mm(uP[s % 2][:, :], sel, spread[1][p][:, q, :], start=True, stop=True).then_inc(u_ready, 1)

            def y_start(B, p):
                wait(pe, y_evac, B)
                mm(yP[:, :], ddiag[:, :], xaT[p][:, HALO:HALO + L], start=True, stop=False,
                   skip_group_check=True).then_inc(y_started, 1)

            def reduce_group(B, i):
                wait(pe, prod_done, B * UNITS + 4 * i + 4)
                for q in range(4):
                    ins = mm(yP[32 * q:32 * q + 32, :], sel_red[:, i, :], prod[:, (i % 2) * 4 + q, :], start=False,
                             stop=(i == GROUPS - 1), skip_group_check=True)
                ins.then_inc(red_done, 1)

            def scores(B, p, k):
                if k == 0:
                    wait(pe, done["p"], job_count("p", B, "k"))
                wait(pe, s_biased, B * NBLK + k)
                mm(sP[:, 0:KVH * 3 * W], q4[:, k, :, :].rearrange("p r q -> p (r q)"), k4[:, :, k * W:k * W + 3 * W],
                   start=True, stop=True).then_inc(s_ready, 1)

            def prob_transposes(B, k):
                wait(pe, p_norm, B * NBLK + k + 1)
                wait(pe, ao_evac, B * NBLK + k)
                for g in range(KVH):
                    ins = nc.tensor.transpose(ptP[0:3 * W, g * 128:(g + 1) * 128], prob[:, k % 4, g, :], ident[:, :])
                ins.then_inc(pt_ready, 1)

            def values(B, p, k):
                if k == 0:
                    wait(pe, done["p"], job_count("p", B, "v"))
                wait(pe, pt_evac, B * NBLK + k + 1)
                for g in range(KVH):
                    ins = mm(ptP[32 * g:32 * g + 32, 0:128], vw[:, k, g, :], probT[:, g, :], start=True, stop=True)
                ins.then_inc(pv_ready, 1)

            def mem_job(name, B, p):
                fill("m", B, name)
                if name == "conv":
                    for tap in range(TAPS):
                        o = HALO - (TAPS - 1) + tap
                        ins = mm(jobP[:, :], convdiag[:, tap, :], xaT[p][:, o:o + L], start=(tap == 0),
                                 stop=(tap == TAPS - 1))
                elif name[:2] == "es":
                    t = int(name[2])
                    ins = mm(jobP[:, :], xaT[p][:, HALO + t * 128:HALO + (t + 1) * 128], decTs[:, :], start=True,
                             stop=True)
                else:
                    t = int(name[2])
                    wait(pe, m_norm, B * NT + t + 1)
                    ins = transposes([mprob[:, t % 2, c * 128:(c + 1) * 128] for c in range(4)], 128, 128)
                filled(ins, "m", B, name)

            def project(B, p, n):
                if n == 0:
                    fill("t", B, "proj")
                    ins = mm(jobP[:, :], w_x[:, :], xaT[p][:, HALO:HALO + L], start=True, stop=False)
                elif n == 1:
                    wait(pe, cv_step, (B + 1) * N_CV)
                    ins = mm(jobP[:, :], cs_id[:, :], cs[:, :], start=False, stop=False)
                elif n < 6:
                    wait(pe, done["m"], job_count("m", B, "pt3"))
                    ins = mm(jobP[:, :], dec_m[:, n - 2, :], mprobT[:, n - 2, :], start=False, stop=False)
                elif n < 10:
                    wait(pe, ao_evac, (B + 1) * NBLK)
                    ins = mm(jobP[:, :], wo_p[:, n - 6, :], ao4[:, n - 6, :], start=False, stop=False)
                else:
                    wait(pe, y_evac, B + 1)
                    ins = mm(jobP[:, :], w_ssm[:, :], yT[:, :], start=False, stop=True)
                    filled(ins, "t", B, "proj")

            def tail_job(name, B, p):
                fill("t", B, name)
                if name == "back":
                    wait(pe, done["t"], job_count("t", B, "proj"))
                    ins = transposes([fT[:, t * 128:(t + 1) * 128] for t in range(NT)], 128, 128)
                elif name == "zT":
                    wait(pe, l2_step, B * N_L2 + L2["z"])
                    ins = transposes([z[:, t, :] for t in range(NT)], 128, 128)
                else:
                    wait(pe, done["t"], job_count("t", B, "zT"))
                    for t in range(NT):
                        ins = mm(jobP[:, t * D:(t + 1) * D], zT[:, t * 128:(t + 1) * 128], W2[:, :], start=True,
                                 stop=True)
                filled(ins, "t", B, name)

            def body(B, p):
                before[0] = ("p", B, "v")
                for s in range(UNITS):
                    unit_spread(B, p, s)
                    if s == 3 and not first(B):
                        reduce_group(B - 1, GROUPS - 1)
                    if s == 6:
                        y_start(B, p)
                    if s >= 7 and s % 4 == 3:
                        reduce_group(B, (s - 7) // 4)
                    if 1 <= s < 12 and not first(B):
                        project(B - 1, 1 - p, s - 1)
                    if s >= 2 and (s - 2) % 3 == 0 and (s - 2) // 3 < NBLK:
                        scores(B, p, (s - 2) // 3)
                    if s >= 10 and (s - 10) % 3 == 0 and (s - 10) // 3 < NBLK:
                        prob_transposes(B, (s - 10) // 3)
                    if s >= 11 and (s - 11) % 3 == 0 and (s - 11) // 3 < NBLK:
                        values(B, p, (s - 11) // 3)
                    if s in PE_SLOT:
                        fam, name = PE_SLOT[s]
                        if fam == "t" and not first(B):
                            tail_job(name, B - 1, 1 - p)
                        if fam == "p" and not last(B):
                            pre_job(name, B + 1, 1 - p)
                        if fam == "m":
                            mem_job(name, B, p)

            def tail(B, p):
                reduce_group(B, GROUPS - 1)
                for n in range(11):
                    project(B, p, n)
                for name in ("back", "zT", "ffn"):
                    tail_job(name, B, p)

            run_batches(pe, front, body, tail)

        @block.vector
        def _(dve):
            v = nc.vector
            dve.wait_ge(const_ready, 2)
            dve.wait_ge(w_in, 16 * N_W_DMA)
            v.tensor_scalar(wq_p[:, :, :, 0:HD], wq_raw[:, :, :, :].rearrange("d g r h -> d r g h"),
                            float(HD) ** -0.5, None, ALU.mult)
            v.tensor_copy(wk_p[:, :, 0:HD], wk_raw[:, :, :])
            v.tensor_scalar(wo_p[:, :, :], wo_p[:, :, :], RW_ATTN, None, ALU.mult)
            v.tensor_scalar(w_ssm[:, :], w_ssm[:, :], RW_SSM, None, ALU.mult)
            v.scalar_tensor_tensor(w_x[:, :], w_x[:, :], RW_MEM, ident[:, :], ALU.mult, ALU.add)
            v.tensor_scalar(cs_id[:, :], ident[:, :], RW_CONV, None, ALU.mult)
            v.tensor_scalar(bwm_s[:, :], bwm_col, RW_MEM, None, ALU.mult)
            v.tensor_scalar(ddiag[:, :], ident[:, :], dssm_col, None, ALU.mult)
            for k in range(TAPS):
                ins = v.tensor_scalar(convdiag[:, k, :], ident[:, :], wconv_s[:, k:k + 1], None, ALU.mult)
            ins.then_inc(w_scaled, 1)
            dve.wait_ge(init, INIT["w_abs"])
            v.tensor_reduce(wmax[:, :], wf_abs[:, :], AX.X, ALU.max).then_inc(init, 1)
            dve.wait_ge(init, INIT["w_maxt"])
            v.tensor_reduce(wmax1[:, :], jobP[0:1, 0:D], AX.X, ALU.max).then_inc(init, 1)
            dve.wait_ge(init, INIT["w_c"])
            v.reciprocal(wsc[:, 3:4], wsc[:, 0:1]).then_inc(init, 1)
            dve.wait_ge(init, INIT["w_r"])
            v.tensor_scalar(wsc[:, 1:2], wsc[:, 3:4], 7.0, None, ALU.mult)
            v.tensor_scalar(wsc[:, 2:3], wsc[:, 0:1], 1.0 / 7.0, None, ALU.mult).then_inc(init, 1)
            dve.wait_ge(init, INIT["w_s"])
            v.tensor_scalar(wf_abs[:, :], wf[:, :], wsc[:, 1:2], ROUND, ALU.mult, ALU.add).then_inc(init, 1)
            dve.wait_ge(init, INIT["w_q1"])
            v.tensor_scalar(wf_abs[:, :], wf_abs[:, :], ROUND, 7.0, ALU.subtract, ALU.min).then_inc(init, 1)
            dve.wait_ge(init, INIT["w_q2"])
            v.tensor_scalar(wf_abs[:, :], wf_abs[:, :], -8.0, wsc[:, 2:3], ALU.max, ALU.mult).then_inc(init, 1)
            dve.wait_ge(init, INIT["ab"])
            v.tensor_tensor(W2[:, :], wf_abs[:, :], jobP[:, 0:D], ALU.add).then_inc(init, 1)
            dve.wait_ge(bias_in, 16 * 3 * REP)
            v.memset(bias3[:, 0, :, 0:W], MASKED)
            v.memset(bias3[:, 2, :, 2 * W:3 * W], MASKED).then_inc(bias_done, 1)

            def ln_stats(B):
                dve.wait_ge(x_in[0], 16)
                if not first(B):
                    dve.wait_ge(x_in[1], 16 * (NB - 1))
                for t in range(NT):
                    ins = v.bn_stats(st[:, t, :], xin(B)[:, t, :])
                ins.then_inc(ln_step, 1)

            def ln_stats_there(B):
                dve.wait_ge(ln_step, B * N_LN + LN["stats"])

            def ln_aggr(B):
                for t in range(NT):
                    ins = v.bn_aggr(mv[:, t, :], st[:, t, :])
                ins.then_inc(ln_step, 1)
                dve.wait_ge(ln_step, B * N_LN + LN["aggr"])
                v.tensor_scalar(ve[:, :], mv[:, :, 1], EPS, None, ALU.add).then_inc(ln_step, 1)

            def xin(B):
                if isinstance(B, int):
                    return x_sb[:, B, :, :]
                return x_sb[:, bass.ds(B, 1), :, :].rearrange("p a t d -> p (a t) d")

            def ln_apply(B):
                dve.wait_ge(ln_step, B * N_LN + LN["r2"])
                for t in range(NT):
                    ins = v.tensor_scalar(xa[:, t, :], xin(B)[:, t, :], mv[:, t, 0:1], rr[:, t:t + 1], ALU.subtract,
                                          ALU.mult)
                ins.then_inc(ln_step, 1)

            def softplus_rounding(B):
                dve.wait_ge(sp_step, B * N_SP + SP["ln"])
                v.tensor_scalar(sp_t[:, :], sp_e[:, :], 1.0, 1.0, ALU.add, ALU.subtract).then_inc(sp_step, 1)

            def front(B, p):
                ln_stats(B)
                ln_stats_there(B)
                ln_aggr(B)
                ln_apply(B)
                softplus_rounding(B)

            def unit_input(B, p, s):
                if s == 0:
                    wait(dve, done["p"], job_count("p", B, "C"))
                wait(dve, u_ready, B * UNITS + s + 1)
                wait(dve, scan_done, B * UNITS + s - 1)
                v.tensor_tensor(dbx[:, s % 2, :], uP[s % 2][:, :], B2[p][:, :], ALU.mult).then_inc(dbx_done, 1)

            def unit_scan(B, s):
                wait(dve, exp_done, B * UNITS + s + 1)
                wait(dve, dbx_done, B * UNITS + s + 1)
                wait(dve, prod_done, B * UNITS + s - 3)
                v.tensor_tensor_scan(hst[:, s % 4, :], dtP[s % 2][:, :], dbx[:, s % 2, :], 0.0, ALU.mult,
                                     ALU.add).then_inc(scan_done, 1)

            def bias_and_max(B, k):
                row = 0 if k == 0 else 2 if k == NBLK - 1 else 1
                wait(dve, s_ready, B * NBLK + k + 1)
                wait(dve, p_exp, B * NBLK + k - 1)
                v.tensor_tensor(s_sb[:, k % 2, :, :], sP[:, 0:KVH * 3 * W].rearrange("p (g k) -> p g k", g=KVH),
                                bias3[:, row, :, :], ALU.add).then_inc(s_biased, 1)
                dve.wait_ge(s_biased, B * NBLK + k + 1)
                v.tensor_reduce(nmax[:, k % 2, :], s_sb[:, k % 2, :, :], AX.X, ALU.max, negate=True).then_inc(s_max, 1)

            def inverse_sums(B, k):
                wait(dve, p_exp, B * NBLK + k + 1)
                wait(dve, p_norm, B * NBLK + k - 3)
                v.reciprocal(pinv[:, k % 4, :], psum_r[:, k % 4, :]).then_inc(p_inv, 1)

            def mem_max(B, t):
                wait_job(dve, "m", B, f"es{t}")
                v.tensor_reduce(mmx[:, t:t + 1], jobP[:, :], AX.X, ALU.max, negate=True).then_inc(m_max, 1)

            def mem_norm(B, t):
                wait(dve, m_exp, B * NT + t + 1)
                v.reciprocal(minv[:, t:t + 1], msum[:, t:t + 1]).then_inc(m_inv, 1)
                dve.wait_ge(m_inv, B * NT + t + 1)
                v.tensor_scalar(mprob[:, t % 2, :], mprob[:, t % 2, :], minv[:, t:t + 1], None, ALU.mult) \
                    .then_inc(m_norm, 1)

            def residual(B):
                wait_job(dve, "t", B, "back")
                v.tensor_tensor(x1[:, :, :], jobP[:, :].rearrange("p (t d) -> p t d", t=NT), xin(B), ALU.add) \
                    .then_inc(l2_step, 1)
                dve.wait_ge(l2_step, B * N_L2 + L2["x1"])
                dve.sem_inc(done["t"], 1)
                for t in range(NT):
                    ins = v.bn_stats(st2[:, t, :], x1[:, t, :])
                ins.then_inc(l2_step, 1)

            def stats2_there(B):
                dve.wait_ge(l2_step, B * N_L2 + L2["stats"])

            def aggr2(B):
                for t in range(NT):
                    ins = v.bn_aggr(mv2[:, t, :], st2[:, t, :])
                ins.then_inc(l2_step, 1)
                dve.wait_ge(l2_step, B * N_L2 + L2["aggr"])
                v.tensor_scalar(vz[:, :], mv2[:, :, 1], EPS, None, ALU.add).then_inc(l2_step, 1)

            def normalise2(B):
                wait(dve, l2_step, B * N_L2 + L2["r"])
                for t in range(NT):
                    ins = v.tensor_scalar(z[:, t, :], x1[:, t, :], mv2[:, t, 0:1], rz[:, t:t + 1], ALU.subtract,
                                          ALU.mult)
                ins.then_inc(l2_step, 1)

            def output(B):
                wait_job(dve, "t", B, "ffn")
                wait(dve, l2_step, B * N_L2 + L2["x1b"])
                wait(dve, out_done, B * 16)
                v.tensor_tensor(outb[:, :, :], jobP[:, :].rearrange("p (t d) -> p t d", t=NT), x1b[:, :, :], ALU.add) \
                    .then_inc(out_ready, 1)
                dve.wait_ge(out_ready, B + 1)
                dve.sem_inc(done["t"], 1)

            MAX_AT = {32: 0, 38: 1, 43: 2, 48: 3}
            NORM_AT = {35: 0, 41: 1, 46: 2, 51: 3}

            def body(B, p):
                for s in range(UNITS):
                    if s == 2 and not last(B):
                        ln_stats_there(B + 1)
                    if s == 15 and not first(B):
                        stats2_there(B - 1)
                    unit_input(B, p, s)
                    if s >= 1:
                        unit_scan(B, s - 1)
                    if s >= 3 and (s - 3) % 3 == 0 and (s - 3) // 3 < NBLK:
                        bias_and_max(B, (s - 3) // 3)
                    if s >= 6 and (s - 6) % 3 == 0 and (s - 6) // 3 < NBLK:
                        inverse_sums(B, (s - 6) // 3)
                    if s in MAX_AT:
                        mem_max(B, MAX_AT[s])
                    if s in NORM_AT:
                        mem_norm(B, NORM_AT[s])
                    if not first(B):
                        if s == 14:
                            residual(B - 1)
                        if s == 15:
                            aggr2(B - 1)
                        if s == 17:
                            normalise2(B - 1)
                        if s == 24:
                            output(B - 1)
                    if not last(B):
                        if s == 1:
                            ln_stats(B + 1)
                        if s == 2:
                            ln_aggr(B + 1)
                        if s == 10:
                            ln_apply(B + 1)
                        if s == 28:
                            softplus_rounding(B + 1)
                unit_scan(B, UNITS - 1)

            def tail(B, p):
                residual(B)
                stats2_there(B)
                aggr2(B)
                normalise2(B)
                output(B)

            run_batches(dve, front, body, tail)

        @block.gpsimd
        def _(pool):
            g = nc.gpsimd
            g.memset(wo_p[:, :, :], 0.0).then_inc(const_ready, 1)
            g.memset(ident[:, :], 0.0)
            g.memset(sel_bc[:, :, :, :], 0.0)
            g.memset(sel_red[:, :, :], 0.0)
            g.memset(wq_p[:, :, :, :], 0.0)
            g.memset(wk_p[:, :, :], 0.0)
            g.memset(ones_row[:, :], 1.0)
            g.memset(relpad[:, :], MASKED)
            g.memset(eps_t[:, :], EPS)
            g.memset(mhalf[:, :], -0.5).then_inc(pool_zeros, 1)
            pool.wait_ge(pool_zeros, 1)
            g.affine_select(out=ident[:, :], in_=ident[:, :], compare_op=ALU.not_equal, fill=1.0, base=0,
                            pattern=[[-1, 128]], channel_multiplier=1).then_inc(const_ready, 1)
            pool.wait_ge(const_ready, 2)
            turn = 1
            for part in range(3):
                rows = sel_bc[32 * part:32 * part + 32, :, :, :]
                g.affine_select(out=rows, in_=rows, compare_op=ALU.not_equal, fill=1.0, base=0,
                                pattern=[[-2, GROUPS], [-1, 2], [0, NS]], channel_multiplier=1) \
                    .then_inc(pool_zeros, 1)
                turn += 1
                pool.wait_ge(pool_zeros, turn)
            for j in range(2):
                rows = sel_red[64 * j:64 * j + 64, :, :]
                g.affine_select(out=rows, in_=rows, compare_op=ALU.not_equal, fill=1.0, base=-j,
                                pattern=[[-2, GROUPS], [1, 32]], channel_multiplier=0).then_inc(pool_zeros, 1)
                turn += 1
                pool.wait_ge(pool_zeros, turn)
            g.memset(k4[:, :, :], 0.0)
            g.memset(vw[:, :, :, :], 0.0)
            for p in range(2):
                g.memset(xaT[p][:, 0:HALO], 0.0)
                ins = g.memset(xaT[p][:, HALO + L:LP], 0.0)
            ins.then_inc(const_ready, 2)

            def ln_roots(B):
                wait(pool, ln_step, B * N_LN + LN["ve"])
                g.tensor_tensor(rr[:, :], ve[:, :], mhalf[:, :], ALU.pow).then_inc(ln_step, 1)
                pool.wait_ge(ln_step, B * N_LN + LN["r"])
                g.tensor_tensor(vr[:, :], mv[:, :, 1], rr[:, :], ALU.mult).then_inc(ln_step, 1)
                pool.wait_ge(ln_step, B * N_LN + LN["vr"])
                g.tensor_tensor(vr[:, :], vr[:, :], rr[:, :], ALU.mult).then_inc(ln_step, 1)
                pool.wait_ge(ln_step, B * N_LN + LN["vrr"])
                g.tensor_tensor(vr[:, :], vr[:, :], eps_t[:, :], ALU.add).then_inc(ln_step, 1)
                pool.wait_ge(ln_step, B * N_LN + LN["ve2"])
                g.tensor_tensor(rr2[:, :], vr[:, :], mhalf[:, :], ALU.pow).then_inc(ln_step, 1)

            def softplus_step(B, name):
                steps = {"t2": (sp_t, sp_e, sp_t, ALU.subtract),
                         "t3": (sp_l, sp_l, sp_t, ALU.add),
                         "dt": (dtv, sp_l, sp_r, ALU.add),
                         "u": (uv, dtv, xnT, ALU.mult)}
                o, a, b, op = steps[name]
                wait(pool, sp_step, B * N_SP + SP[name] - 1)
                g.tensor_tensor(o[:, :], a[:, :], b[:, :], op).then_inc(sp_step, 1)

            def part_step(B, name):
                i = int(name[-1])
                v = (dtv, uv)[i]
                if name[0] == "r":
                    wait(pool, sp_step, B * N_SP + SP["hi1"] + i)
                    g.tensor_tensor(res[i][:, :], v[:, :], parts[i][:, 0, :], ALU.subtract).then_inc(sp_step, 1)
                else:
                    wait(pool, sp_step, B * N_SP + SP["mid1"] + i)
                    g.tensor_tensor(parts[i][:, 2, :], res[i][:, :], parts[i][:, 1, :], ALU.subtract) \
                        .then_inc(sp_step, 1)

            def front(B, p):
                ln_roots(B)
                for name in ("t2", "t3", "dt", "u"):
                    softplus_step(B, name)
                for name in ("r0", "r1", "lo0", "lo1"):
                    part_step(B, name)

            def unit_product(B, p, s):
                wait(pool, scan_done, B * UNITS + s + 1)
                if s % 4 == 0:
                    wait(pool, red_done, B * GROUPS + s // 4 - 1)
                g.tensor_tensor(prod[:, s % 8, :], hst[:, s % 4, :], C2[p][:, :], ALU.mult).then_inc(prod_done, 1)

            def prob_norm(B, k):
                wait(pool, p_inv, B * NBLK + k + 1)
                g.tensor_tensor(prob[:, k % 4, :, :], prob[:, k % 4, :, :],
                                pinv[:, k % 4, :].unsqueeze(2).to_broadcast([128, KVH, 3 * W]), ALU.mult) \
                    .then_inc(p_norm, 1)

            def conv_sum(B):
                wait(pool, cv_step, B * N_CV + CV["relu"])
                g.tensor_tensor(cv_l[:, :], cv_l[:, :], cv_m[:, :], ALU.add).then_inc(cv_step, 1)

            def conv_product(B):
                wait(pool, cv_step, B * N_CV + CV["sig"])
                wait(pool, ready["t"], B * N_TAIL - N_TAIL + 1)
                g.tensor_tensor(cs[:, :], cv_v[:, :], cv_a[:, :], ALU.mult).then_inc(cv_step, 1)

            def root2(B):
                wait(pool, l2_step, B * N_L2 + L2["ve"])
                g.tensor_tensor(rz[:, :], vz[:, :], mhalf[:, :], ALU.pow).then_inc(l2_step, 1)

            def add_bias(B):
                wait(pool, l2_step, B * N_L2 + L2["z"])
                wait(pool, out_done, B * 16)
                g.tensor_tensor(x1b[:, :, :], x1[:, :, :], biasrep[:, :].unsqueeze(1).to_broadcast([128, NT, D]),
                                ALU.add).then_inc(l2_step, 1)

            SP_AT = {25: "t2", 26: "t3", 27: "dt", 28: "u"}
            PART_AT = {33: "r0", 34: "r1", 38: "lo0", 39: "lo1"}

            def body(B, p):
                for s in range(UNITS):
                    unit_product(B, p, s)
                    if s >= 4 and (s - 4) % 3 == 0 and (s - 4) // 3 < NBLK:
                        prob_norm(B, (s - 4) // 3)
                    if s == 36:
                        conv_sum(B)
                    if s == 41:
                        conv_product(B)
                    if not first(B):
                        if s == 12:
                            root2(B - 1)
                        if s == 16:
                            add_bias(B - 1)
                    if not last(B):
                        if s == 1:
                            ln_roots(B + 1)
                        if s in SP_AT:
                            softplus_step(B + 1, SP_AT[s])
                        if s in PART_AT:
                            part_step(B + 1, PART_AT[s])

            def tail(B, p):
                root2(B)
                add_bias(B)

            run_batches(pool, front, body, tail)


_INS = ["L0_attn_x", "L0_attn_ln_g", "L0_attn_ln_b", "L0_attn_w_xproj", "L0_attn_w_dt", "L0_attn_b_dt",
        "L0_attn_A_log", "L0_attn_D_ssm", "L0_attn_w_ssm_out", "L0_attn_wq", "L0_attn_wk", "L0_attn_wv",
        "L0_attn_wo", "L0_attn_rel_bias", "L0_attn_w_wm", "L0_attn_b_wm", "L0_attn_episodic", "L0_attn_w_dc1",
        "L0_attn_b_dc1", "L0_attn_w_dc2", "L0_attn_b_dc2", "L0_attn_w_conv", "L0_attn_b_conv", "L0_ffn_kernel",
        "L0_ffn_bias", "L0_ffn_a", "L0_ffn_b"]


def kernel(**inputs):
    import numpy as _np
    import concourse.bacc as _bacc
    from concourse import mybir as _mybir
    from concourse.bass_utils import run_bass_kernel_spmd as _run

    nc = _bacc.Bacc("TRN2", target_bir_lowering=False, num_devices=1)
    arrays, args = {}, []
    for name in _INS:
        a = _np.ascontiguousarray(inputs[name])
        arrays[f"in_{name}_dram"] = a
        args.append(nc.dram_tensor(f"in_{name}_dram", a.shape, _mybir.dt.from_np(a.dtype), kind="ExternalInput").ap())
    rel_dram = nc.dram_tensor("rel_table", [H, W, RELPAD], F32, kind="Internal").ap()
    out = nc.dram_tensor("out_0_dram", (NB, L, D), F32, kind="ExternalOutput").ap()
    hybrid_block_kernel(nc, *args, rel_dram, out)
    r = _run(nc, [arrays], core_ids=[0])
    return r.results[0]["out_0_dram"]
```

```python
from contextlib import ExitStack

import concourse.bass as bass
from concourse import mybir

F32 = mybir.dt.float32
BF16 = mybir.dt.bfloat16
ALU = mybir.AluOpType
ACT = mybir.ActivationFunctionType
AX = mybir.AxisListType

NB = 8
L = 512
D = 128
NT = L // 128
H, KVH, HD = 16, 4, 8
REP = H // KVH
W = 32
NBLK = L // W
HALO = W
LP = L + 2 * HALO
NS = 64
DTR = 64
SE = 512
CD = 16
TAPS = 4
RANK = 16
EPS = 1e-5
MASKED = -1.0e9
UNITS = D // 2
GROUPS = UNITS // 4
RW_ATTN, RW_SSM, RW_CONV, RW_MEM, MEM_MIX = 0.2, 0.45, 0.15, 0.2, 0.3
ROUND = 12582912.0
RELPAD = 160

PRE = {n: i for i, n in enumerate(["xaT", "xnT", "dti", "dtpre", "B", "C", "q", "k", "v"])}
MEM = {n: i for i, n in enumerate(["es0", "conv", "es1", "pt0", "es2", "pt1", "es3", "pt2", "pt3"])}
TAIL = {n: i for i, n in enumerate(["proj", "back", "zT", "ffn"])}
N_PRE, N_MEM, N_TAIL = len(PRE), len(MEM), len(TAIL)

JOB_AT = {12: ("t", "back"), 14: ("p", "xaT"), 16: ("p", "xnT"), 18: ("t", "zT"), 20: ("t", "ffn"),
          22: ("p", "dti"), 24: ("p", "dtpre"), 26: ("p", "B"), 28: ("p", "C"), 30: ("m", "es0"),
          36: ("m", "conv"), 38: ("m", "es1"), 41: ("m", "pt0"), 43: ("m", "es2"), 46: ("m", "pt1"),
          48: ("m", "es3"), 51: ("m", "pt2"), 53: ("p", "q"), 55: ("m", "pt3"), 57: ("p", "k"),
          62: ("p", "v")}
SCORES_AT = {17 * k // 5: k for k in range(NBLK)}
BIAS_LAG, EXP_LAG, INV_LAG, NORM_LAG, PT_LAG, PV_LAG = 1, (2, 3), 4, 4, 9, 11
AHEAD = 2


def block_at(s, lag):
    return SCORES_AT.get(s - lag)


def memory_tile_at(s, lag):
    fam, name = JOB_AT.get(s - lag, ("", ""))
    return int(name[2]) if name[:2] == "es" else None


LN = {n: i + 1 for i, n in enumerate(
    ["stats", "aggr", "ve", "r", "vr", "vrr", "ve2", "r2", "xa", "xn"])}
N_LN = len(LN)
SP = {n: i + 1 for i, n in enumerate(
    ["abs", "relu", "exp", "ln", "t1", "t2", "t3", "dt", "u", "hi0", "hi1", "r0", "r1", "mid0",
     "mid1", "lo0", "lo1"])}
N_SP = len(SP)
CV = {n: i + 1 for i, n in enumerate(["v", "tanh", "cs"])}
N_CV = len(CV)
L2 = {n: i + 1 for i, n in enumerate(["x1", "stats", "aggr", "ve", "r", "z", "x1b"])}
N_L2 = len(L2)
N_PARTS_DMA = 24
N_PROJ = 3 + 4 + REP
N_Q_DMA = KVH * REP
N_V_DMA = 12


def hybrid_block_kernel(nc, x, ln_g, ln_b, w_xproj, w_dt, b_dt, A_log, D_ssm, w_ssm_out, wq, wk, wv,
                        wo, rel_bias, w_wm, b_wm, episodic, w_dc1, b_dc1, w_dc2, b_dc2, w_conv,
                        b_conv, ffn_w, ffn_bias, ffn_a, ffn_b, rel_dram, out):
    ctx = ExitStack()
    with ctx:
        def sb(name, shape, dt=F32):
            return ctx.enter_context(nc.sbuf_tensor(name, shape, dt))

        def sem(name):
            return ctx.enter_context(nc.semaphore(name))

        bank = [ctx.enter_context(nc.psum_tensor(f"bank{i}", [128, 512], F32)) for i in range(8)]
        dtP, uP, yP, sP, ptP, jobP = bank[0:2], bank[2:4], bank[4], bank[5], bank[6], bank[7]

        ident = sb("ident", [128, 128])
        sel_bc = sb("sel_bc", [96, GROUPS, 2, NS], BF16)
        sel_red = sb("sel_red", [128, GROUPS, 32])
        mhalf = sb("mhalf", [128, NT])
        eps_t = sb("eps_t", [128, NT])
        w_dti = sb("w_dti", [D, DTR])
        w_B2 = sb("w_B2", [D, 2, NS])
        w_C2 = sb("w_C2", [D, 2, NS])
        w_dt_s = sb("w_dt_s", [DTR, D])
        wq_s = sb("wq_s", [D, H * HD])
        wv_raw = sb("wv_raw", [D, KVH, HD])
        wk_raw = sb("wk_raw", [D, KVH, HD])
        wk_p = sb("wk_p", [D, KVH, 32])
        wv_p = sb("wv_p", [D, KVH, 32])
        wo_p = sb("wo_p", [128, REP, D])
        w_ssm = sb("w_ssm", [D, D])
        w_x = sb("w_x", [D, D])
        cs_id = sb("cs_id", [D, D])
        convdiag = sb("convdiag", [D, TAPS, D])
        ddiag = sb("ddiag", [D, D])
        cols = sb("cols", [128, 8])
        g_col, b_col, bdt_col, bconv_col, bwm_col, bdc2_col, dssm_col = (cols[:, i:i + 1] for i in range(7))
        bwm_s = sb("bwm_s", [128, 1])
        bdc1_col = sb("bdc1_col", [DTR, 1])
        wconv_s = sb("wconv_s", [128, TAPS])
        alog2 = sb("alog2", [D, 2, NS])
        A_rep = sb("A_rep", [128, UNITS])
        epi = sb("epi", [128, 4, CD])
        w_dc1_s = sb("w_dc1_s", [CD, 64])
        w_dc2_s = sb("w_dc2_s", [64, D])
        decTs = sb("decTs", [D, SE])
        dec_m = sb("dec_m", [128, 4, D])
        rel_raw = sb("rel_raw", [2 * W + 1, H])
        relpad = sb("relpad", [H, RELPAD])
        bias3 = sb("bias3", [128, 3, KVH, 3 * W])
        wf = sb("wf", [D, D])
        wf_abs = sb("wf_abs", [D, D])
        wmax = sb("wmax", [D, 1])
        wmax1 = sb("wmax1", [1, 1])
        ones_row = sb("ones_row", [1, 128])
        wsc = sb("wsc", [128, 4])
        W2 = sb("W2", [D, D])
        fa = sb("fa", [D, RANK])
        faT = sb("faT", [RANK, D])
        fb = sb("fb", [RANK, D])
        biasrep = sb("biasrep", [128, D])

        x_sb = sb("x_sb", [128, NB, NT, D])
        st = sb("st", [128, NT, 6])
        mv = sb("mv", [128, NT, 2])
        ve = sb("ve", [128, NT])
        rr = sb("rr", [128, NT])
        vr = sb("vr", [128, NT])
        rr2 = sb("rr2", [128, NT])
        xa = sb("xa", [128, NT, D])
        xn = sb("xn", [128, NT, D])
        xaT = [sb(f"xaT{p}", [D, LP]) for p in range(2)]
        xnT = sb("xnT", [D, L])
        B2 = [sb(f"B2_{p}", [128, L]) for p in range(2)]
        C2 = [sb(f"C2_{p}", [128, L]) for p in range(2)]
        sp_e, sp_r = (t[:, :, :].rearrange("p t d -> p (t d)") for t in (xn, xa))
        sp_l = sb("sp_l", [D, L])
        sp_t = sb("sp_t", [D, L])
        uv = sb("uv", [D, L])
        dti, dtv, res = sp_l[0:DTR, :], sp_t, (sp_e, sp_r)
        parts = [sb(f"parts{i}", [D, 3, L], BF16) for i in range(2)]
        spread = [[sb(f"spread{i}_{p}", [96, 4, L], BF16) for p in range(2)] for i in range(2)]
        qn = sb("qn", [H * HD, L])
        v_tok = sb("v_tok", [128, NT, KVH * 32])
        q4 = sb("q4", [128, NBLK, REP, W])
        k4 = sb("k4", [128, KVH, LP])
        vw = sb("vw", [3 * W, NBLK, KVH, 32])
        dA = sb("dA", [128, 4, L])
        dbx = sb("dbx", [128, 2, L])
        hst = sb("hst", [128, 4, L])
        prod = sb("prod", [128, 8, L])
        yT = sb("yT", [D, L])
        s_sb = sb("s_sb", [128, 2, KVH, 3 * W])
        nmax = sb("nmax", [128, 2, KVH])
        prob = sb("prob", [128, 4, KVH, 3 * W])
        psum_r = sb("psum_r", [128, 4, KVH])
        pinv = sb("pinv", [128, 4, KVH])
        probT = sb("probT", [3 * W, KVH, 128])
        ao4 = sb("ao4", [128, REP, L])
        mmx = sb("mmx", [128, NT])
        msum = sb("msum", [128, NT])
        minv = sb("minv", [128, NT])
        mprob = sb("mprob", [128, 2, SE])
        mprobT = sb("mprobT", [128, 4, L])
        epiT, hidT, decT = mprobT[0:CD, 0, :], mprobT[0:64, 1, :], mprobT[:, 2, :]
        cv_v = sb("cv_v", [D, L])
        cv_a = sb("cv_a", [D, L])
        cs = sb("cs", [D, L])
        fT = sb("fT", [D, L])
        x1 = sb("x1", [128, NT, D])
        x1b = sb("x1b", [128, NT, D])
        st2 = sb("st2", [128, NT, 6])
        mv2 = sb("mv2", [128, NT, 2])
        vz = sb("vz", [128, NT])
        rz = sb("rz", [128, NT])
        z = sb("z", [128, NT, D])
        zT, outb = fT, x1b

        x_in = [sem(f"x_in{i}") for i in range(2)]
        w_first, w_in = sem("w_first"), sem("w_in")
        a_in = sem("a_in")
        rel_out = sem("rel_out")
        bias_in = sem("bias_in")
        bias_done = sem("bias_done")
        pool_zeros = sem("pool_zeros")
        w_padded = sem("w_padded")
        w_scaled = sem("w_scaled")
        const_ready = sem("const_ready")
        init = sem("init")
        dt_ready, u_ready = sem("dt_ready"), sem("u_ready")
        exp_done, dbx_done, scan_done = sem("exp_done"), sem("dbx_done"), sem("scan_done")
        prod_done, red_done, y_started, y_evac = sem("prod_done"), sem("red_done"), sem("y_started"), sem("y_evac")
        s_ready, s_biased, s_max = sem("s_ready"), sem("s_biased"), sem("s_max")
        p_exp, p_inv, p_norm = sem("p_exp"), sem("p_inv"), sem("p_norm")
        pt_ready, pt_evac, pv_ready, ao_evac = sem("pt_ready"), sem("pt_evac"), sem("pv_ready"), sem("ao_evac")
        ready = {f: sem(f"{f}_job_ready") for f in "pmt"}
        done = {f: sem(f"{f}_job_done") for f in "pmt"}
        ln_step, sp_step, cv_step, l2_step = sem("ln_step"), sem("sp_step"), sem("cv_step"), sem("l2_step")
        parts_in, q_in, v_in = sem("parts_in"), sem("q_in"), sem("v_in")
        m_max, m_exp, m_inv, m_norm = sem("m_max"), sem("m_exp"), sem("m_inv"), sem("m_norm")
        out_ready, out_done = sem("out_ready"), sem("out_done")

        COUNT = {"p": N_PRE, "m": N_MEM, "t": N_TAIL}
        INDEX = {"p": PRE, "m": MEM, "t": TAIL}

        def wait(eng, s, value):
            if isinstance(value, int) and value <= 0:
                return
            eng.wait_ge(s, value)

        def job_count(fam, B, name):
            return B * COUNT[fam] + INDEX[fam][name] + 1

        def wait_job(eng, fam, B, name):
            wait(eng, ready[fam], job_count(fam, B, name))

        def run_batches(eng, front, body, tail):
            front(0, 0)
            body(0, 0)
            with eng.Fori(0, (NB - 2) // 2) as k:
                body(k * 2 + 1, 1)
                body(k * 2 + 2, 0)
            body(NB - 1, 1)
            tail(NB - 1, 1)

        def first(B):
            return isinstance(B, int) and B == 0

        def last(B):
            return isinstance(B, int) and B == NB - 1

        INIT = {n: i + 1 for i, n in enumerate(
            ["A_t", "A_e", "A_n", "rel_t", "rel_c",
             "epi_t", "epi_c", "hid", "gelu", "dec", "dec_c", "dec_s", "dec_t", "dec_m",
             "w_abs", "w_max", "w_maxt", "w_max1", "w_bc", "w_c", "w_r", "w_s", "w_q1", "w_q2", "w_q3",
             "fa_t", "fa_c", "ab", "W2"])}
        N_FIRST_DMA, N_W_DMA = 12, 19

        block = ctx.enter_context(nc.Block())

        @block.sync
        def _(sp):
            def column(v):
                return v.rearrange("(p a) -> p a", a=1)

            def x_load(b):
                sp.dma_start(x_sb[:, b, :, :], x[b].rearrange("(t p) d -> p t d", p=128)) \
                    .then_inc(x_in[min(b, 1)], 16)

            x_load(0)
            n = 0
            for dst, src in ((g_col, column(ln_g)), (b_col, column(ln_b)), (w_dti[:, :], w_xproj[:, 0:DTR]),
                             (w_dt_s[:, :], w_dt), (bdt_col, column(b_dt)),
                             (w_B2[:, 0, :], w_xproj[:, DTR:DTR + NS]), (w_B2[:, 1, :], w_xproj[:, DTR:DTR + NS]),
                             (w_C2[:, 0, :], w_xproj[:, DTR + NS:]), (w_C2[:, 1, :], w_xproj[:, DTR + NS:]),
                             (wq_s[:, :], wq), (wk_raw[:, :, :].rearrange("d a b -> d (a b)"), wk),
                             (wv_raw[:, :, :].rearrange("d a b -> d (a b)"), wv)):
                sp.dma_start(dst, src).then_inc(w_first, 16)
                n += 1
            assert n == N_FIRST_DMA
            for b in range(1, NB):
                x_load(b)
            sp.wait_ge(init, INIT["rel_c"])
            sp.dma_start(rel_dram, relpad[:, :].unsqueeze(1).to_broadcast([H, W, RELPAD])).then_inc(rel_out, 16)
            sp.wait_ge(rel_out, 16)
            flat = rel_dram.rearrange("h q k -> (h q k)")
            for v in range(3):
                for r in range(REP):
                    src = bass.AP(flat.tensor, flat.offset + r * W * RELPAD + W,
                                  [[RELPAD - 1, W], [REP * W * RELPAD, KVH], [1, 3 * W]])
                    sp.dma_start(bias3[r * W:(r + 1) * W, v, :, :], src).then_inc(bias_in, 16)

            def body(B, p):
                if not first(B):
                    store(B - 1, 1 - p)
                if not last(B):
                    front(B + 1, 1 - p)

            def front(B, p):
                wait(sp, u_ready, (B - 1) * UNITS)
                wait(sp, dt_ready, (B - 1) * UNITS)
                for i in range(2):
                    wait(sp, sp_step, B * N_SP + SP[f"lo{i}"])
                    for part in range(3):
                        for c in range(4):
                            sp.dma_start(spread[i][p][32 * part:32 * part + 32, c, :],
                                         parts[i][32 * c:32 * c + 32, part, :]).then_inc(parts_in, 16)
                wait(sp, done["p"], job_count("p", B, "q"))
                for g in range(KVH):
                    for r in range(REP):
                        h = g * REP + r
                        sp.dma_start(q4[32 * g:32 * g + HD, :, r, :],
                                     qn[h * HD:(h + 1) * HD, :].rearrange("p (n q) -> p n q", q=W)).then_inc(q_in, 16)
                wait(sp, done["p"], job_count("p", B, "v"))
                for j in range(3):
                    for m in range(4):
                        blocks = [n for n in range(NBLK) if 0 <= n - 1 + j < NBLK and (n - 1 + j) % 4 == m]
                        t0 = (blocks[0] - 1 + j) // 4
                        sp.dma_start(vw[32 * j:32 * j + 32, blocks[0]:blocks[-1] + 1:4, :, :]
                                     .rearrange("p n g h -> p n (g h)"),
                                     v_tok[32 * m:32 * m + 32, t0:t0 + len(blocks), :]).then_inc(v_in, 16)

            def store(B, p):
                wait(sp, out_ready, B + 1)
                dst = out[B] if isinstance(B, int) else out[bass.ds(B, 1)].rearrange("a l d -> (a l) d")
                sp.dma_start(dst.rearrange("(t p) d -> p t d", p=128), outb[:, :, :]).then_inc(out_done, 16)

            run_batches(sp, front, body, store)
            sp.wait_ge(out_done, 16 * NB)

        @block.scalar
        def _(act):
            n = 0

            def load(dst, src):
                nonlocal n
                act.dma_start(dst, src).then_inc(w_in, 16)
                n += 1

            def column(v):
                return v.rearrange("(p a) -> p a", a=1)

            for j in range(2):
                act.dma_start(alog2[:, j, :], A_log).then_inc(a_in, 16)
            act.dma_start(rel_raw[:, :], rel_bias).then_inc(a_in, 16)
            load(bconv_col, column(b_conv))
            load(bwm_col, column(b_wm))
            load(bdc2_col, column(b_dc2))
            load(dssm_col, column(D_ssm))
            load(wconv_s[:, :], w_conv)
            load(epi[:, :, :], episodic[0].rearrange("(c p) k -> p c k", p=128))
            load(w_dc1_s[:, :], w_dc1)
            load(bdc1_col[:, :], column(b_dc1))
            load(w_dc2_s[:, :], w_dc2)
            load(wf[:, :], ffn_w)
            load(fa[:, :], ffn_a)
            load(fb[:, :], ffn_b)
            load(biasrep[:, :], ffn_bias.rearrange("(a n) -> a n", a=1).to_broadcast([128, D]))
            load(w_ssm[:, :], w_ssm_out)
            load(w_x[:, :], w_wm)
            act.wait_ge(const_ready, 1)
            for g in range(KVH):
                act.dma_start(wo_p[32 * g:32 * g + HD, :, :],
                              wo[g * REP * HD:(g + 1) * REP * HD, :].rearrange("(r h) e -> h r e", r=REP)) \
                    .then_inc(w_in, 16)
                n += 1
            assert n == N_W_DMA, n

            act.wait_ge(init, INIT["A_t"])
            for j in range(2):
                ins = nc.scalar.activation(A_rep[64 * j:64 * j + 64, :],
                                           jobP[64 * j:64 * j + 64, 0:D].rearrange("p (g j) -> p g j", j=2)[:, :, j],
                                           ACT.Exp)
            ins.then_inc(init, 1)
            act.wait_ge(init, INIT["A_e"])
            nc.scalar.activation(A_rep[:, :], A_rep[:, :], ACT.Copy, scale=-1.0).then_inc(init, 1)
            act.wait_ge(init, INIT["rel_t"])
            act.wait_ge(const_ready, 2)
            nc.scalar.activation(relpad[:, W:W + 2 * W + 1], jobP[0:H, 0:2 * W + 1], ACT.Copy).then_inc(init, 1)

            def setup_step(s):
                if s == 0:
                    act.wait_ge(w_in, 16 * N_W_DMA)
                    act.wait_ge(init, INIT["epi_t"])
                    nc.scalar.activation(epiT, jobP[0:CD, :], ACT.Copy).then_inc(init, 1)
                if s == 2:
                    act.wait_ge(init, INIT["hid"])
                    nc.scalar.activation(hidT, jobP[0:64, :], ACT.Gelu, bias=bdc1_col[:, :]).then_inc(init, 1)
                if s == 4:
                    act.wait_ge(init, INIT["dec"])
                    nc.scalar.activation(decT, jobP[:, :], ACT.Identity, bias=bdc2_col).then_inc(init, 1)
                    act.wait_ge(init, INIT["dec_c"])
                    nc.scalar.activation(decTs[:, :], decT, ACT.Copy, scale=float(D) ** -0.5).then_inc(init, 1)
                if s == 6:
                    act.wait_ge(init, INIT["dec_t"])
                    nc.scalar.activation(dec_m[:, :, :].rearrange("p c d -> p (c d)"), jobP[:, :], ACT.Copy,
                                         scale=RW_MEM * MEM_MIX).then_inc(init, 1)
                    nc.scalar.activation(wf_abs[:, :], wf[:, :], ACT.Abs).then_inc(init, 1)
                if s == 10:
                    act.wait_ge(init, INIT["w_bc"])
                    nc.scalar.activation(wsc[:, 0:1], jobP[:, 0:1], ACT.Copy).then_inc(init, 1)
                if s == 12:
                    act.wait_ge(init, INIT["fa_t"])
                    nc.scalar.activation(faT[:, :], jobP[0:RANK, 0:D], ACT.Copy).then_inc(init, 1)

            def scale_xn(B):
                wait(act, ln_step, B * N_LN + LN["xa"])
                for t in range(NT):
                    ins = nc.scalar.activation(xn[:, t, :], xa[:, t, :], ACT.Copy, scale=rr2[:, t:t + 1])
                ins.then_inc(ln_step, 1)

            def pre_job(name, B, p):
                wait_job(act, "p", B, name)
                if name == "xaT":
                    ins = nc.scalar.activation(xaT[p][:, HALO:HALO + L], jobP[:, :], ACT.Copy)
                elif name == "xnT":
                    ins = nc.scalar.activation(xnT[:, :], jobP[:, :], ACT.Identity, bias=b_col, scale=g_col)
                elif name == "dti":
                    ins = nc.scalar.activation(dti[:, :], jobP[0:DTR, :], ACT.Copy)
                elif name in "BC":
                    ins = nc.scalar.activation((B2 if name == "B" else C2)[p][:, :], jobP[:, :], ACT.Copy)
                elif name == "dtpre":
                    nc.scalar.activation(sp_e[:, :], jobP[:, :], ACT.Abs, bias=bdt_col).then_inc(sp_step, 1)
                    nc.scalar.activation(sp_r[:, :], jobP[:, :], ACT.Relu, bias=bdt_col).then_inc(sp_step, 1)
                    act.wait_ge(sp_step, B * N_SP + SP["relu"])
                    act.sem_inc(done["p"], 1)
                    return
                elif name == "k":
                    for g in range(KVH):
                        ins = nc.scalar.activation(k4[32 * g:32 * g + 32, g, HALO:HALO + L],
                                                   jobP[32 * g:32 * g + 32, :], ACT.Copy)
                elif name == "v":
                    wait(act, v_in, B * 16 * N_V_DMA)
                    ins = nc.scalar.activation(v_tok[:, :, :].rearrange("p t h -> p (t h)"), jobP[:, :], ACT.Copy)
                else:
                    wait(act, q_in, B * 16 * N_Q_DMA)
                    ins = nc.scalar.activation(qn[:, :], jobP[:, :], ACT.Copy, scale=float(HD) ** -0.5)
                ins.then_inc(done["p"], 1)

            def softplus_logs(B):
                nc.scalar.activation(sp_e[:, :], sp_e[:, :], ACT.Exp, scale=-1.0).then_inc(sp_step, 1)
                act.wait_ge(sp_step, B * N_SP + SP["exp"])
                nc.scalar.activation(sp_l[:, :], sp_e[:, :], ACT.Ln, bias=1.0).then_inc(sp_step, 1)

            def high_parts(B):
                wait(act, parts_in, B * 16 * N_PARTS_DMA)
                wait(act, sp_step, B * N_SP + SP["u"])
                for i, v in enumerate((dtv, uv)):
                    nc.scalar.activation(parts[i][:, 0, :], v[:, :], ACT.Copy).then_inc(sp_step, 1)

            def mid_parts(B):
                wait(act, sp_step, B * N_SP + SP["r1"])
                for i in range(2):
                    nc.scalar.activation(parts[i][:, 1, :], res[i][:, :], ACT.Copy).then_inc(sp_step, 1)

            def front(B, p):
                scale_xn(B)
                for name in ("xaT", "xnT", "dti", "dtpre"):
                    pre_job(name, B, p)
                softplus_logs(B)
                for name in ("B", "C"):
                    pre_job(name, B, p)
                high_parts(B)
                mid_parts(B)
                for name in ("q", "k", "v"):
                    pre_job(name, B, p)
                for s in range(AHEAD):
                    unit_exp(B, s)

            def unit_exp(B, s):
                i, q = divmod(s, 4)
                wait(act, dt_ready, B * UNITS + s + 1)
                wait(act, scan_done, B * UNITS + s - 3)
                g = GROUPS * q + i
                nc.scalar.activation(dA[:, s % 4, :], dtP[s % 2][:, :], ACT.Exp, scale=A_rep[:, g:g + 1]) \
                    .then_inc(exp_done, 1)

            def y_copy(B):
                wait(act, red_done, (B + 1) * GROUPS)
                wait(act, ready["t"], B * N_TAIL)
                nc.scalar.activation(yT[:, :], yP[:, :], ACT.Copy).then_inc(y_evac, 1)

            def probabilities(B, k, half):
                if half == 0:
                    wait(act, s_max, B * NBLK + k + 1)
                    wait(act, pt_ready, B * NBLK + k - 3)
                for g in (2 * half, 2 * half + 1):
                    ins = nc.scalar.activation(prob[:, k % 4, g, :], s_sb[:, k % 2, g, :], ACT.Exp,
                                               bias=nmax[:, k % 2, g:g + 1], accum_out=psum_r[:, k % 4, g:g + 1])
                if half == 1:
                    ins.then_inc(p_exp, 1)

            def probT_copy(B, k):
                wait(act, pt_ready, B * NBLK + k + 1)
                wait(act, pv_ready, B * NBLK + k)
                nc.scalar.activation(probT[:, :, :].rearrange("p g t -> p (g t)"), ptP[0:3 * W, :], ACT.Copy) \
                    .then_inc(pt_evac, 1)

            def ao_copy(B, k):
                wait(act, pv_ready, B * NBLK + k + 1)
                if k == 0:
                    wait(act, ready["t"], B * N_TAIL - N_TAIL + 1)
                nc.scalar.activation(ao4[:, :, k * W:(k + 1) * W],
                                     ptP[:, 0:128].rearrange("p (r q) -> p r q", r=REP), ACT.Copy).then_inc(ao_evac, 1)

            def mem_exp(B, t):
                wait(act, m_max, B * NT + t + 1)
                if t >= 2:
                    wait_job(act, "m", B, f"pt{t - 2}")
                ins = nc.scalar.activation(mprob[:, t % 2, :], jobP[:, :], ACT.Exp, bias=mmx[:, t:t + 1],
                                           accum_out=msum[:, t:t + 1])
                ins.then_inc(m_exp, 1)
                act.wait_ge(m_exp, B * NT + t + 1)
                act.sem_inc(done["m"], 1)

            def memT_copy(B, t):
                wait_job(act, "m", B, f"pt{t}")
                if t == 0:
                    wait(act, ready["t"], B * N_TAIL - N_TAIL + 1)
                nc.scalar.activation(mprobT[:, :, t * 128:(t + 1) * 128],
                                     jobP[:, :].rearrange("p (c t) -> p c t", c=4), ACT.Copy).then_inc(done["m"], 1)

            def conv_bias(B):
                wait_job(act, "m", B, "conv")
                nc.scalar.activation(cv_v[:, :], jobP[:, :], ACT.Identity, bias=bconv_col).then_inc(cv_step, 1)
                act.wait_ge(cv_step, B * N_CV + CV["v"])
                act.sem_inc(done["m"], 1)

            def conv_tanh(B):
                nc.scalar.activation(cv_a[:, :], cv_v[:, :], ACT.Tanh, scale=0.5).then_inc(cv_step, 1)

            def proj_copy(B):
                wait_job(act, "t", B, "proj")
                nc.scalar.activation(fT[:, :], jobP[:, :], ACT.Identity, bias=bwm_s[:, :]).then_inc(done["t"], 1)

            def zT_copy(B):
                wait_job(act, "t", B, "zT")
                nc.scalar.activation(zT[:, :], jobP[:, :], ACT.Copy).then_inc(done["t"], 1)

            def empty_job(fam, name, B, p):
                if fam == "p":
                    if not last(B):
                        pre_job(name, B + 1, 1 - p)
                elif name == "zT":
                    if not first(B):
                        zT_copy(B - 1)
                elif name == "conv":
                    conv_bias(B)
                elif name[:2] == "pt":
                    memT_copy(B, int(name[2]))

            def body(B, p):
                for s in range(UNITS):
                    if s + AHEAD < UNITS:
                        unit_exp(B, s + AHEAD)
                    elif not last(B):
                        unit_exp(B + 1, s + AHEAD - UNITS)
                    if first(B):
                        setup_step(s)
                    else:
                        if s == 5:
                            y_copy(B - 1)
                        if s == 10:
                            proj_copy(B - 1)
                    for half in range(2):
                        k = block_at(s, EXP_LAG[half])
                        if k is not None:
                            probabilities(B, k, half)
                    k = block_at(s, PT_LAG)
                    if k is not None:
                        probT_copy(B, k)
                    k = block_at(s, PV_LAG)
                    if k is not None:
                        ao_copy(B, k)
                    t = memory_tile_at(s, 2)
                    if t is not None:
                        mem_exp(B, t)
                    if s in JOB_AT:
                        empty_job(*JOB_AT[s], B, p)
                    if s == 37:
                        conv_tanh(B)
                    if not last(B):
                        if s == 13:
                            scale_xn(B + 1)
                        if s == 25:
                            softplus_logs(B + 1)
                        if s == 34:
                            high_parts(B + 1)
                        if s == 39:
                            mid_parts(B + 1)

            def tail(B, p):
                y_copy(B)
                proj_copy(B)
                zT_copy(B)

            run_batches(act, front, body, tail)

        @block.tensor
        def _(pe):
            mm = nc.tensor.matmul

            def transposes(srcs, rows, step):
                for c, src in enumerate(srcs):
                    ins = nc.tensor.transpose(jobP[0:rows, c * step:(c + 1) * step], src, ident[:, :])
                return ins

            pe.wait_ge(const_ready, 2)
            pe.wait_ge(a_in, 16 * 3)
            nc.tensor.transpose(jobP[:, 0:D], alog2[:, :, :].rearrange("p j n -> p (j n)"), ident[:, :]).then_inc(init, 1)
            pe.wait_ge(init, INIT["A_n"])
            nc.tensor.transpose(jobP[0:H, 0:2 * W + 1], rel_raw[:, :], ident[0:2 * W + 1, 0:2 * W + 1]).then_inc(init, 1)
            pe.wait_ge(init, INIT["rel_c"])
            pe.wait_ge(const_ready, 4)
            pe.wait_ge(w_first, 16 * N_FIRST_DMA)
            pe.wait_ge(w_padded, 1)

            def setup_step(s):
                if s == 0:
                    pe.wait_ge(w_in, 16 * N_W_DMA)
                    wait(pe, done["p"], job_count("p", 0, "v"))
                    transposes([epi[:, c, :] for c in range(4)], CD, 128).then_inc(init, 1)
                if s == 2:
                    pe.wait_ge(init, INIT["epi_c"])
                    mm(jobP[0:64, :], w_dc1_s[:, :], epiT, start=True, stop=True).then_inc(init, 1)
                if s == 4:
                    pe.wait_ge(init, INIT["gelu"])
                    mm(jobP[:, :], w_dc2_s[:, :], hidT, start=True, stop=True).then_inc(init, 1)
                if s == 6:
                    pe.wait_ge(init, INIT["dec_s"])
                    transposes([decT[:, c * 128:(c + 1) * 128] for c in range(4)], 128, 128).then_inc(init, 1)
                if s == 8:
                    pe.wait_ge(init, INIT["w_max"])
                    nc.tensor.transpose(jobP[0:1, 0:D], wmax[:, :], ident[:, :]).then_inc(init, 1)
                if s == 10:
                    pe.wait_ge(init, INIT["w_max1"])
                    mm(jobP[:, 0:1], ones_row[:, :], wmax1[:, :], start=True, stop=True).then_inc(init, 1)
                if s == 12:
                    pe.wait_ge(init, INIT["w_q3"])
                    nc.tensor.transpose(jobP[0:RANK, 0:D], fa[:, :], ident[:, :]).then_inc(init, 1)
                if s == 13:
                    pe.wait_ge(init, INIT["fa_c"])
                    mm(jobP[:, 0:D], faT[:, :], fb[:, :], start=True, stop=True).then_inc(init, 1)
                if s == 14:
                    pe.wait_ge(init, INIT["W2"])
                    pe.wait_ge(w_scaled, 2)

            before = [None]

            def fill(fam, B, name):
                if before[0] is not None:
                    f, b, n = before[0]
                    wait(pe, done[f], job_count(f, b, n))

            def filled(ins, fam, B, name):
                ins.then_inc(ready[fam], 1)
                before[0] = (fam, B, name)

            def pre_job(name, B, p):
                fill("p", B, name)
                if name == "xaT":
                    wait(pe, ln_step, B * N_LN + LN["xa"])
                    ins = transposes([xa[:, t, :] for t in range(NT)], 128, 128)
                elif name == "xnT":
                    wait(pe, ln_step, B * N_LN + LN["xn"])
                    ins = transposes([xn[:, t, :] for t in range(NT)], 128, 128)
                elif name == "dti":
                    wait(pe, done["p"], job_count("p", B, "xnT"))
                    ins = mm(jobP[0:DTR, :], w_dti[:, :], xnT[:, :], start=True, stop=True)
                elif name == "dtpre":
                    wait(pe, done["p"], job_count("p", B, "dti"))
                    ins = mm(jobP[:, :], w_dt_s[:, :], dti[:, :], start=True, stop=True)
                elif name in "BC":
                    w = w_B2 if name == "B" else w_C2
                    ins = mm(jobP[:, :], w[:, :, :].rearrange("d j n -> d (j n)"), xnT[:, :], start=True, stop=True)
                elif name == "k":
                    ins = mm(jobP[:, :], wk_p[:, :, :].rearrange("d g h -> d (g h)"), xaT[p][:, HALO:HALO + L],
                             start=True, stop=True)
                elif name == "v":
                    for t in range(NT):
                        ins = mm(jobP[:, t * 128:(t + 1) * 128], xaT[p][:, HALO + t * 128:HALO + (t + 1) * 128],
                                 wv_p[:, :, :].rearrange("d g h -> d (g h)"), start=True, stop=True)
                else:
                    ins = mm(jobP[:, :], wq_s[:, :], xaT[p][:, HALO:HALO + L], start=True, stop=True)
                filled(ins, "p", B, name)

            def unit_u(B, p, s):
                i, q = divmod(s, 4)
                wait(pe, dbx_done, B * UNITS + s - 1)
                mm(uP[s % 2][:, :], sel_bc[:, i, :, :].rearrange("k j n -> k (j n)"), spread[1][p][:, q, :],
                   start=True, stop=True).then_inc(u_ready, 1)

            def unit_dt(B, p, s):
                i, q = divmod(s, 4)
                if s == 0:
                    wait(pe, parts_in, (B + 1) * 16 * N_PARTS_DMA)
                wait(pe, exp_done, B * UNITS + s - 1)
                mm(dtP[s % 2][:, :], sel_bc[:, i, :, :].rearrange("k j n -> k (j n)"), spread[0][p][:, q, :],
                   start=True, stop=True).then_inc(dt_ready, 1)

            def front(B, p):
                for name in PRE:
                    pre_job(name, B, p)
                for s in range(AHEAD):
                    unit_dt(B, p, s)
                unit_u(B, p, 0)

            def y_start(B, p):
                if first(B):
                    pe.wait_ge(w_scaled, 1)
                wait(pe, y_evac, B)
                mm(yP[:, :], ddiag[:, :], xaT[p][:, HALO:HALO + L], start=True, stop=False,
                   skip_group_check=True).then_inc(y_started, 1)

            def reduce_group(B, i):
                wait(pe, prod_done, B * UNITS + 4 * i + 4)
                for q in range(4):
                    ins = mm(yP[32 * q:32 * q + 32, :], sel_red[:, i, :], prod[:, (i % 2) * 4 + q, :], start=False,
                             stop=(i == GROUPS - 1), skip_group_check=True)
                ins.then_inc(red_done, 1)

            def scores(B, p, k):
                if k == 0:
                    wait(pe, done["p"], job_count("p", B, "k"))
                    wait(pe, q_in, (B + 1) * 16 * N_Q_DMA)
                wait(pe, s_biased, B * NBLK + k)
                mm(sP[:, 0:KVH * 3 * W], q4[:, k, :, :].rearrange("p r q -> p (r q)"), k4[:, :, k * W:k * W + 3 * W],
                   start=True, stop=True).then_inc(s_ready, 1)

            def prob_transposes(B, k):
                wait(pe, p_norm, B * NBLK + k + 1)
                wait(pe, ao_evac, B * NBLK + k)
                for g in range(KVH):
                    ins = nc.tensor.transpose(ptP[0:3 * W, g * 128:(g + 1) * 128], prob[:, k % 4, g, :], ident[:, :])
                ins.then_inc(pt_ready, 1)

            def values(B, p, k):
                if k == 0:
                    wait(pe, v_in, (B + 1) * 16 * N_V_DMA)
                wait(pe, pt_evac, B * NBLK + k + 1)
                for g in range(KVH):
                    ins = mm(ptP[32 * g:32 * g + 32, 0:128], vw[:, k, g, :], probT[:, g, :], start=True, stop=True)
                ins.then_inc(pv_ready, 1)

            def conv_tap(B, p, tap):
                if tap == 0:
                    fill("m", B, "conv")
                o = HALO - (TAPS - 1) + tap
                ins = mm(jobP[:, :], convdiag[:, tap, :], xaT[p][:, o:o + L], start=(tap == 0), stop=(tap == TAPS - 1))
                if tap == TAPS - 1:
                    filled(ins, "m", B, "conv")

            def mem_job(name, B, p):
                fill("m", B, name)
                if name[:2] == "es":
                    t = int(name[2])
                    ins = mm(jobP[:, :], xaT[p][:, HALO + t * 128:HALO + (t + 1) * 128], decTs[:, :], start=True,
                             stop=True)
                else:
                    t = int(name[2])
                    wait(pe, m_norm, B * NT + t + 1)
                    ins = transposes([mprob[:, t % 2, c * 128:(c + 1) * 128] for c in range(4)], 128, 128)
                filled(ins, "m", B, name)

            def project(B, p, n):
                if n == 0:
                    fill("t", B, "proj")
                    ins = mm(jobP[:, :], w_x[:, :], xaT[p][:, HALO:HALO + L], start=True, stop=False)
                elif n == 1:
                    wait(pe, cv_step, (B + 1) * N_CV)
                    ins = mm(jobP[:, :], cs_id[:, :], cs[:, :], start=False, stop=False)
                elif n < 6:
                    wait(pe, done["m"], job_count("m", B, "pt3"))
                    ins = mm(jobP[:, :], dec_m[:, n - 2, :], mprobT[:, n - 2, :], start=False, stop=False)
                elif n < 10:
                    wait(pe, ao_evac, (B + 1) * NBLK)
                    ins = mm(jobP[:, :], wo_p[:, n - 6, :], ao4[:, n - 6, :], start=False, stop=False)
                else:
                    wait(pe, y_evac, B + 1)
                    ins = mm(jobP[:, :], w_ssm[:, :], yT[:, :], start=False, stop=True)
                    filled(ins, "t", B, "proj")

            def tail_job(name, B, p):
                fill("t", B, name)
                if name == "back":
                    wait(pe, done["t"], job_count("t", B, "proj"))
                    ins = transposes([fT[:, t * 128:(t + 1) * 128] for t in range(NT)], 128, 128)
                elif name == "zT":
                    wait(pe, l2_step, B * N_L2 + L2["z"])
                    ins = transposes([z[:, t, :] for t in range(NT)], 128, 128)
                else:
                    wait(pe, done["t"], job_count("t", B, "zT"))
                    for t in range(NT):
                        ins = mm(jobP[:, t * D:(t + 1) * D], zT[:, t * 128:(t + 1) * 128], W2[:, :], start=True,
                                 stop=True)
                filled(ins, "t", B, name)

            def body(B, p):
                before[0] = ("p", B, "v")
                for s in range(UNITS):
                    if s + AHEAD < UNITS:
                        unit_dt(B, p, s + AHEAD)
                    elif not last(B):
                        unit_dt(B + 1, 1 - p, s + AHEAD - UNITS)
                    if s < UNITS - 1:
                        unit_u(B, p, s + 1)
                    elif not last(B):
                        unit_u(B + 1, 1 - p, 0)
                    if first(B):
                        setup_step(s)
                    else:
                        if s == 3:
                            reduce_group(B - 1, GROUPS - 1)
                        if s < N_PROJ:
                            project(B - 1, 1 - p, s)
                    if s == 6:
                        y_start(B, p)
                    if s >= 7 and s % 4 == 3:
                        reduce_group(B, (s - 7) // 4)
                    k = block_at(s, 0)
                    if k is not None:
                        scores(B, p, k)
                    k = block_at(s, PT_LAG)
                    if k is not None:
                        prob_transposes(B, k)
                    k = block_at(s, PV_LAG)
                    if k is not None:
                        values(B, p, k)
                    if 33 <= s < 33 + TAPS:
                        conv_tap(B, p, s - 33)
                    fam, name = JOB_AT.get(s, ("", ""))
                    if fam == "t" and not first(B):
                        tail_job(name, B - 1, 1 - p)
                    if fam == "p" and not last(B):
                        pre_job(name, B + 1, 1 - p)
                    if fam == "m" and name != "conv":
                        mem_job(name, B, p)

            def tail(B, p):
                reduce_group(B, GROUPS - 1)
                for n in range(N_PROJ):
                    project(B, p, n)
                for name in ("back", "zT", "ffn"):
                    tail_job(name, B, p)

            run_batches(pe, front, body, tail)

        @block.vector
        def _(dve):
            v = nc.vector
            dve.wait_ge(const_ready, 2)
            dve.wait_ge(w_first, 16 * N_FIRST_DMA)
            v.tensor_copy(wv_p[:, :, 0:HD], wv_raw[:, :, :])
            v.tensor_copy(wk_p[:, :, 0:HD], wk_raw[:, :, :]).then_inc(w_padded, 1)

            def setup_step(s):
                if s == 0:
                    dve.wait_ge(bias_in, 16 * 3 * REP)
                    v.memset(bias3[:, 0, :, 0:W], MASKED)
                    v.memset(bias3[:, 2, :, 2 * W:3 * W], MASKED).then_inc(bias_done, 1)
                    dve.wait_ge(bias_done, 1)
                if s == 2:
                    dve.wait_ge(w_in, 16 * N_W_DMA)
                    v.tensor_scalar(wo_p[:, :, :], wo_p[:, :, :], RW_ATTN, None, ALU.mult)
                    v.tensor_scalar(w_ssm[:, :], w_ssm[:, :], RW_SSM, None, ALU.mult)
                    v.scalar_tensor_tensor(w_x[:, :], w_x[:, :], RW_MEM, ident[:, :], ALU.mult, ALU.add)
                    v.tensor_scalar(cs_id[:, :], ident[:, :], 0.5 * RW_CONV, None, ALU.mult)
                    v.tensor_scalar(bwm_s[:, :], bwm_col, RW_MEM, None, ALU.mult)
                    v.tensor_scalar(ddiag[:, :], ident[:, :], dssm_col, None, ALU.mult).then_inc(w_scaled, 1)
                    for k in range(TAPS):
                        ins = v.tensor_scalar(convdiag[:, k, :], ident[:, :], wconv_s[:, k:k + 1], None, ALU.mult)
                    ins.then_inc(w_scaled, 1)
                if s == 6:
                    dve.wait_ge(init, INIT["w_abs"])
                    v.tensor_reduce(wmax[:, :], wf_abs[:, :], AX.X, ALU.max).then_inc(init, 1)
                if s == 8:
                    dve.wait_ge(init, INIT["w_maxt"])
                    v.tensor_reduce(wmax1[:, :], jobP[0:1, 0:D], AX.X, ALU.max).then_inc(init, 1)
                if s == 10:
                    dve.wait_ge(init, INIT["w_c"])
                    v.reciprocal(wsc[:, 3:4], wsc[:, 0:1]).then_inc(init, 1)
                    dve.wait_ge(init, INIT["w_r"])
                    v.tensor_scalar(wsc[:, 1:2], wsc[:, 3:4], 7.0, None, ALU.mult)
                    v.tensor_scalar(wsc[:, 2:3], wsc[:, 0:1], 1.0 / 7.0, None, ALU.mult).then_inc(init, 1)
                    dve.wait_ge(init, INIT["w_s"])
                    v.tensor_scalar(wf_abs[:, :], wf[:, :], wsc[:, 1:2], ROUND, ALU.mult, ALU.add).then_inc(init, 1)
                    dve.wait_ge(init, INIT["w_q1"])
                    v.tensor_scalar(wf_abs[:, :], wf_abs[:, :], ROUND, 7.0, ALU.subtract, ALU.min).then_inc(init, 1)
                    dve.wait_ge(init, INIT["w_q2"])
                    v.tensor_scalar(wf_abs[:, :], wf_abs[:, :], -8.0, wsc[:, 2:3], ALU.max, ALU.mult).then_inc(init, 1)
                if s == 13:
                    dve.wait_ge(init, INIT["ab"])
                    v.tensor_tensor(W2[:, :], wf_abs[:, :], jobP[:, 0:D], ALU.add).then_inc(init, 1)

            def ln_stats(B):
                dve.wait_ge(x_in[0], 16)
                if not first(B):
                    dve.wait_ge(x_in[1], 16 * (NB - 1))
                for t in range(NT):
                    ins = v.bn_stats(st[:, t, :], xin(B)[:, t, :])
                ins.then_inc(ln_step, 1)

            def ln_stats_there(B):
                dve.wait_ge(ln_step, B * N_LN + LN["stats"])

            def ln_aggr(B):
                for t in range(NT):
                    ins = v.bn_aggr(mv[:, t, :], st[:, t, :])
                ins.then_inc(ln_step, 1)
                dve.wait_ge(ln_step, B * N_LN + LN["aggr"])
                v.tensor_scalar(ve[:, :], mv[:, :, 1], EPS, None, ALU.add).then_inc(ln_step, 1)

            def xin(B):
                if isinstance(B, int):
                    return x_sb[:, B, :, :]
                return x_sb[:, bass.ds(B, 1), :, :].rearrange("p a t d -> p (a t) d")

            def ln_apply(B):
                dve.wait_ge(ln_step, B * N_LN + LN["r2"])
                for t in range(NT):
                    ins = v.tensor_scalar(xa[:, t, :], xin(B)[:, t, :], mv[:, t, 0:1], rr[:, t:t + 1], ALU.subtract,
                                          ALU.mult)
                ins.then_inc(ln_step, 1)

            def softplus_rounding(B):
                dve.wait_ge(sp_step, B * N_SP + SP["ln"])
                v.tensor_scalar(sp_t[:, :], sp_e[:, :], 1.0, 1.0, ALU.add, ALU.subtract).then_inc(sp_step, 1)

            def front(B, p):
                ln_stats(B)
                ln_stats_there(B)
                ln_aggr(B)
                ln_apply(B)
                softplus_rounding(B)

            def unit_input(B, p, s):
                if s == 0:
                    wait(dve, done["p"], job_count("p", B, "C"))
                wait(dve, u_ready, B * UNITS + s + 1)
                wait(dve, scan_done, B * UNITS + s - 1)
                v.tensor_tensor(dbx[:, s % 2, :], uP[s % 2][:, :], B2[p][:, :], ALU.mult).then_inc(dbx_done, 1)

            def unit_scan(B, s):
                wait(dve, exp_done, B * UNITS + s + 1)
                wait(dve, dbx_done, B * UNITS + s + 1)
                wait(dve, prod_done, B * UNITS + s - 3)
                v.tensor_tensor_scan(hst[:, s % 4, :], dA[:, s % 4, :], dbx[:, s % 2, :], 0.0, ALU.mult,
                                     ALU.add).then_inc(scan_done, 1)

            def bias_and_max(B, k):
                row = 0 if k == 0 else 2 if k == NBLK - 1 else 1
                wait(dve, s_ready, B * NBLK + k + 1)
                wait(dve, p_exp, B * NBLK + k - 1)
                v.tensor_tensor(s_sb[:, k % 2, :, :], sP[:, 0:KVH * 3 * W].rearrange("p (g k) -> p g k", g=KVH),
                                bias3[:, row, :, :], ALU.add).then_inc(s_biased, 1)
                dve.wait_ge(s_biased, B * NBLK + k + 1)
                v.tensor_reduce(nmax[:, k % 2, :], s_sb[:, k % 2, :, :], AX.X, ALU.max, negate=True).then_inc(s_max, 1)

            def inverse_sums(B, k):
                wait(dve, p_exp, B * NBLK + k + 1)
                wait(dve, p_norm, B * NBLK + k - 3)
                v.reciprocal(pinv[:, k % 4, :], psum_r[:, k % 4, :]).then_inc(p_inv, 1)

            def mem_max(B, t):
                wait_job(dve, "m", B, f"es{t}")
                v.tensor_reduce(mmx[:, t:t + 1], jobP[:, :], AX.X, ALU.max, negate=True).then_inc(m_max, 1)

            def mem_norm(B, t):
                wait(dve, m_exp, B * NT + t + 1)
                v.reciprocal(minv[:, t:t + 1], msum[:, t:t + 1]).then_inc(m_inv, 1)
                dve.wait_ge(m_inv, B * NT + t + 1)
                v.tensor_scalar(mprob[:, t % 2, :], mprob[:, t % 2, :], minv[:, t:t + 1], None, ALU.mult) \
                    .then_inc(m_norm, 1)

            def conv_gate(B):
                wait(dve, cv_step, B * N_CV + CV["tanh"])
                wait(dve, ready["t"], B * N_TAIL - N_TAIL + 1)
                v.scalar_tensor_tensor(cs[:, :], cv_a[:, :], 1.0, cv_v[:, :], ALU.add, ALU.mult).then_inc(cv_step, 1)

            def residual(B):
                wait_job(dve, "t", B, "back")
                v.tensor_tensor(x1[:, :, :], jobP[:, :].rearrange("p (t d) -> p t d", t=NT), xin(B), ALU.add) \
                    .then_inc(l2_step, 1)
                dve.wait_ge(l2_step, B * N_L2 + L2["x1"])
                dve.sem_inc(done["t"], 1)
                for t in range(NT):
                    ins = v.bn_stats(st2[:, t, :], x1[:, t, :])
                ins.then_inc(l2_step, 1)

            def stats2_there(B):
                dve.wait_ge(l2_step, B * N_L2 + L2["stats"])

            def aggr2(B):
                for t in range(NT):
                    ins = v.bn_aggr(mv2[:, t, :], st2[:, t, :])
                ins.then_inc(l2_step, 1)
                dve.wait_ge(l2_step, B * N_L2 + L2["aggr"])
                v.tensor_scalar(vz[:, :], mv2[:, :, 1], EPS, None, ALU.add).then_inc(l2_step, 1)

            def normalise2(B):
                wait(dve, l2_step, B * N_L2 + L2["r"])
                for t in range(NT):
                    ins = v.tensor_scalar(z[:, t, :], x1[:, t, :], mv2[:, t, 0:1], rz[:, t:t + 1], ALU.subtract,
                                          ALU.mult)
                ins.then_inc(l2_step, 1)

            def output(B):
                wait_job(dve, "t", B, "ffn")
                wait(dve, l2_step, B * N_L2 + L2["x1b"])
                wait(dve, out_done, B * 16)
                v.tensor_tensor(outb[:, :, :], jobP[:, :].rearrange("p (t d) -> p t d", t=NT), x1b[:, :, :], ALU.add) \
                    .then_inc(out_ready, 1)
                dve.wait_ge(out_ready, B + 1)
                dve.sem_inc(done["t"], 1)

            def body(B, p):
                for s in range(UNITS):
                    if s == 4 and not last(B):
                        ln_stats_there(B + 1)
                    if s == 14 and not first(B):
                        stats2_there(B - 1)
                    unit_input(B, p, s)
                    if s >= 1:
                        unit_scan(B, s - 1)
                    if first(B):
                        setup_step(s)
                    k = block_at(s, BIAS_LAG)
                    if k is not None:
                        bias_and_max(B, k)
                    k = block_at(s, INV_LAG)
                    if k is not None:
                        inverse_sums(B, k)
                    t = memory_tile_at(s, 1)
                    if t is not None:
                        mem_max(B, t)
                    t = memory_tile_at(s, 3)
                    if t is not None:
                        mem_norm(B, t)
                    if s == 40:
                        conv_gate(B)
                    if not first(B):
                        if s == 13:
                            residual(B - 1)
                        if s == 14:
                            aggr2(B - 1)
                        if s == 16:
                            normalise2(B - 1)
                        if s == 20:
                            output(B - 1)
                    if not last(B):
                        if s == 3:
                            ln_stats(B + 1)
                        if s == 4:
                            ln_aggr(B + 1)
                        if s == 11:
                            ln_apply(B + 1)
                        if s == 26:
                            softplus_rounding(B + 1)
                unit_scan(B, UNITS - 1)

            def tail(B, p):
                residual(B)
                stats2_there(B)
                aggr2(B)
                normalise2(B)
                output(B)

            run_batches(dve, front, body, tail)

        @block.gpsimd
        def _(pool):
            g = nc.gpsimd
            g.memset(wo_p[:, :, :], 0.0).then_inc(const_ready, 1)
            g.memset(ident[:, :], 0.0)
            g.memset(sel_bc[:, :, :, :], 0.0)
            g.memset(sel_red[:, :, :], 0.0)
            g.memset(wv_p[:, :, :], 0.0)
            g.memset(q4[:, :, :, :], 0.0)
            g.memset(wk_p[:, :, :], 0.0)
            g.memset(ones_row[:, :], 1.0)
            g.memset(relpad[:, :], MASKED)
            g.memset(eps_t[:, :], EPS)
            g.memset(mhalf[:, :], -0.5).then_inc(pool_zeros, 1)
            pool.wait_ge(pool_zeros, 1)
            g.affine_select(out=ident[:, :], in_=ident[:, :], compare_op=ALU.not_equal, fill=1.0, base=0,
                            pattern=[[-1, 128]], channel_multiplier=1).then_inc(const_ready, 1)
            pool.wait_ge(const_ready, 2)
            turn = 1
            for part in range(3):
                rows = sel_bc[32 * part:32 * part + 32, :, :, :]
                g.affine_select(out=rows, in_=rows, compare_op=ALU.not_equal, fill=1.0, base=0,
                                pattern=[[-2, GROUPS], [-1, 2], [0, NS]], channel_multiplier=1) \
                    .then_inc(pool_zeros, 1)
                turn += 1
                pool.wait_ge(pool_zeros, turn)
            for j in range(2):
                rows = sel_red[64 * j:64 * j + 64, :, :]
                g.affine_select(out=rows, in_=rows, compare_op=ALU.not_equal, fill=1.0, base=-j,
                                pattern=[[-2, GROUPS], [1, 32]], channel_multiplier=0).then_inc(pool_zeros, 1)
                turn += 1
                pool.wait_ge(pool_zeros, turn)
            g.memset(k4[:, :, :], 0.0)
            g.memset(vw[:, :, :, :], 0.0)
            for p in range(2):
                g.memset(xaT[p][:, 0:HALO], 0.0)
                ins = g.memset(xaT[p][:, HALO + L:LP], 0.0)
            ins.then_inc(const_ready, 2)

            def ln_root_step(B, n):
                o, a, b, op = ((rr, ve[:, :], mhalf, ALU.pow), (vr, mv[:, :, 1], rr, ALU.mult),
                               (vr, vr[:, :], rr, ALU.mult), (vr, vr[:, :], eps_t, ALU.add),
                               (rr2, vr[:, :], mhalf, ALU.pow))[n]
                wait(pool, ln_step, B * N_LN + LN["ve"] + n)
                g.tensor_tensor(o[:, :], a, b[:, :], op).then_inc(ln_step, 1)

            def softplus_step(B, name):
                steps = {"t2": (sp_t, sp_e, sp_t, ALU.subtract),
                         "t3": (sp_l, sp_l, sp_t, ALU.add),
                         "dt": (dtv, sp_l, sp_r, ALU.add),
                         "u": (uv, dtv, xnT, ALU.mult)}
                o, a, b, op = steps[name]
                wait(pool, sp_step, B * N_SP + SP[name] - 1)
                g.tensor_tensor(o[:, :], a[:, :], b[:, :], op).then_inc(sp_step, 1)

            def part_step(B, name):
                i = int(name[-1])
                v = (dtv, uv)[i]
                if name[0] == "r":
                    wait(pool, sp_step, B * N_SP + SP["hi1"] + i)
                    g.tensor_tensor(res[i][:, :], v[:, :], parts[i][:, 0, :], ALU.subtract).then_inc(sp_step, 1)
                else:
                    wait(pool, sp_step, B * N_SP + SP["mid1"] + i)
                    g.tensor_tensor(parts[i][:, 2, :], res[i][:, :], parts[i][:, 1, :], ALU.subtract) \
                        .then_inc(sp_step, 1)

            def front(B, p):
                for n in range(5):
                    ln_root_step(B, n)
                for name in ("t2", "t3", "dt", "u"):
                    softplus_step(B, name)
                for name in ("r0", "r1", "lo0", "lo1"):
                    part_step(B, name)

            def unit_product(B, p, s):
                wait(pool, scan_done, B * UNITS + s + 1)
                if s % 4 == 0:
                    wait(pool, red_done, B * GROUPS + s // 4 - 1)
                g.tensor_tensor(prod[:, s % 8, :], hst[:, s % 4, :], C2[p][:, :], ALU.mult).then_inc(prod_done, 1)

            def prob_norm(B, k):
                wait(pool, p_inv, B * NBLK + k + 1)
                g.tensor_tensor(prob[:, k % 4, :, :], prob[:, k % 4, :, :],
                                pinv[:, k % 4, :].unsqueeze(2).to_broadcast([128, KVH, 3 * W]), ALU.mult) \
                    .then_inc(p_norm, 1)

            def root2(B):
                wait(pool, l2_step, B * N_L2 + L2["ve"])
                g.tensor_tensor(rz[:, :], vz[:, :], mhalf[:, :], ALU.pow).then_inc(l2_step, 1)

            def add_bias(B):
                wait(pool, l2_step, B * N_L2 + L2["z"])
                wait(pool, out_done, B * 16)
                g.tensor_tensor(x1b[:, :, :], x1[:, :, :], biasrep[:, :].unsqueeze(1).to_broadcast([128, NT, D]),
                                ALU.add).then_inc(l2_step, 1)

            SP_AT = {26: "t2", 27: "t3", 28: "dt", 29: "u"}
            PART_AT = {33: "r0", 34: "r1", 39: "lo0", 40: "lo1"}

            def body(B, p):
                for s in range(UNITS):
                    unit_product(B, p, s)
                    k = block_at(s, NORM_LAG)
                    if k is not None:
                        prob_norm(B, k)
                    if not first(B):
                        if s == 12:
                            root2(B - 1)
                        if s == 16:
                            add_bias(B - 1)
                    if not last(B):
                        if 2 <= s < 7:
                            ln_root_step(B + 1, s - 2)
                        if s in SP_AT:
                            softplus_step(B + 1, SP_AT[s])
                        if s in PART_AT:
                            part_step(B + 1, PART_AT[s])

            def tail(B, p):
                root2(B)
                add_bias(B)

            run_batches(pool, front, body, tail)


_INS = ["L0_attn_x", "L0_attn_ln_g", "L0_attn_ln_b", "L0_attn_w_xproj", "L0_attn_w_dt", "L0_attn_b_dt",
        "L0_attn_A_log", "L0_attn_D_ssm", "L0_attn_w_ssm_out", "L0_attn_wq", "L0_attn_wk", "L0_attn_wv",
        "L0_attn_wo", "L0_attn_rel_bias", "L0_attn_w_wm", "L0_attn_b_wm", "L0_attn_episodic", "L0_attn_w_dc1",
        "L0_attn_b_dc1", "L0_attn_w_dc2", "L0_attn_b_dc2", "L0_attn_w_conv", "L0_attn_b_conv", "L0_ffn_kernel",
        "L0_ffn_bias", "L0_ffn_a", "L0_ffn_b"]


def kernel(**inputs):
    import numpy as _np
    import concourse.bacc as _bacc
    from concourse import mybir as _mybir
    from concourse.bass_utils import run_bass_kernel_spmd as _run

    nc = _bacc.Bacc("TRN2", target_bir_lowering=False, num_devices=1)
    arrays, args = {}, []
    for name in _INS:
        a = _np.ascontiguousarray(inputs[name])
        arrays[f"in_{name}_dram"] = a
        args.append(nc.dram_tensor(f"in_{name}_dram", a.shape, _mybir.dt.from_np(a.dtype), kind="ExternalInput").ap())
    rel_dram = nc.dram_tensor("rel_table", [H, W, RELPAD], F32, kind="Internal").ap()
    out = nc.dram_tensor("out_0_dram", (NB, L, D), F32, kind="ExternalOutput").ap()
    hybrid_block_kernel(nc, *args, rel_dram, out)
    r = _run(nc, [arrays], core_ids=[0])
    return r.results[0]["out_0_dram"]
```

```python
from contextlib import ExitStack

import concourse.bass as bass
from concourse import mybir

F32 = mybir.dt.float32
BF16 = mybir.dt.bfloat16
ALU = mybir.AluOpType
ACT = mybir.ActivationFunctionType
AX = mybir.AxisListType

NB = 8
L = 512
D = 128
NT = L // 128
H, KVH, HD = 16, 4, 8
REP = H // KVH
W = 32
NBLK = L // W
HALO = W
LP = L + 2 * HALO
NS = 64
DTR = 64
SE = 512
CD = 16
TAPS = 4
RANK = 16
EPS = 1e-5
MASKED = -1.0e9
BIG = 3.0e38
UNITS = D // 2
PAIRS = UNITS // 2
GROUPS = UNITS // 4
RW_ATTN, RW_SSM, RW_CONV, RW_MEM, MEM_MIX = 0.2, 0.45, 0.15, 0.2, 0.3
ROUND = 12582912.0
RELPAD = 160

PRE = {n: i for i, n in enumerate(["xaT", "xnT", "dti", "dtpre", "B", "C", "q", "k", "v"])}
MEM = {n: i for i, n in enumerate(["es0", "conv", "es1", "pt0", "es2", "pt1", "es3", "pt2", "pt3"])}
TAIL = {n: i for i, n in enumerate(["proj", "back", "zT", "ffn"])}
N_PRE, N_MEM, N_TAIL = len(PRE), len(MEM), len(TAIL)

JOB_AT = {12: ("t", "back"), 14: ("p", "xaT"), 15: ("p", "xnT"), 17: ("t", "zT"), 18: ("t", "ffn"),
          22: ("p", "dti"), 23: ("p", "dtpre"), 27: ("p", "B"), 29: ("p", "C"), 31: ("m", "es0"),
          37: ("m", "conv"), 39: ("m", "es1"), 41: ("m", "pt0"), 44: ("m", "es2"), 47: ("m", "pt1"),
          48: ("m", "es3"), 51: ("p", "q"), 52: ("m", "pt2"), 55: ("m", "pt3"), 56: ("p", "k"),
          62: ("p", "v")}
EMPTY_LAG = 0
N_EARLY = 6
JOB_SLOT = {name: s for s, (_, name) in JOB_AT.items()}
AT = {
    "reduce": 3, "y_copy": 2, "project": 0, "proj_copy": 11, "residual": 13, "aggr2": 15, "root2": 13,
    "normalise2": 16, "output": 20,
    "ln_stats": 0, "ln_aggr": 2, "ln_root": 4, "ln_apply": 11, "scale_xn": 12, "softplus_exp": 23, "sum": 26,
    "softplus_logs": 25, "rounding": 27, "log1p": 25, "dt": 25, "u": 28, "high": 35, "r0": 36, "r1": 37,
    "mid": 41, "lo0": 41, "lo1": 43,
    "y_start": 5, "tanh": 37, "gate": 39,
}
SETUP_AT = 5
M_MAX_LAG, M_EXP_LAG, M_NORM_LAG = 1, 1, 4
SCORES_AT = {33 * k // 10: k for k in range(NBLK)}
BIAS_LAG, EXP_LAG, INV_LAG, NORM_LAG, PT_LAG, PT_COPY_LAG, PV_LAG, AO_COPY_LAG = 2, (3, 4), 6, 5, 10, 10, 12, 12
AHEAD = 2


def block_at(s, lag):
    return SCORES_AT.get(s - lag)


def memory_tile_at(s, lag):
    fam, name = JOB_AT.get(s - lag, ("", ""))
    return int(name[2]) if name[:2] == "es" else None


LN = {n: i + 1 for i, n in enumerate(
    ["stats", "aggr", "ve", "r", "vr", "vrr", "ve2", "r2", "xa", "xn"])}
N_LN = len(LN)
SP = {n: i + 1 for i, n in enumerate(
    ["abs", "relu", "exp", "sum", "ln", "lost", "log1p", "dt", "u", "hi0", "hi1", "r0", "r1", "mid0",
     "mid1", "lo0", "lo1"])}
N_SP = len(SP)
CV = {n: i + 1 for i, n in enumerate(["v", "tanh", "cs"])}
N_CV = len(CV)
L2 = {n: i + 1 for i, n in enumerate(["x1", "stats", "aggr", "ve", "r", "z"])}
N_L2 = len(L2)
N_PARTS_DMA = 24
N_PROJ = 3 + 4 + REP
N_Q_DMA = KVH * REP
N_V_DMA = 12


def hybrid_block_kernel(nc, x, ln_g, ln_b, w_xproj, w_dt, b_dt, A_log, D_ssm, w_ssm_out, wq, wk, wv,
                        wo, rel_bias, w_wm, b_wm, episodic, w_dc1, b_dc1, w_dc2, b_dc2, w_conv,
                        b_conv, ffn_w, ffn_bias, ffn_a, ffn_b, rel_dram, out):
    ctx = ExitStack()
    with ctx:
        def sb(name, shape, dt=F32):
            return ctx.enter_context(nc.sbuf_tensor(name, shape, dt))

        def sem(name):
            return ctx.enter_context(nc.semaphore(name))

        bank = [ctx.enter_context(nc.psum_tensor(f"bank{i}", [128, 512], F32)) for i in range(8)]
        dtP, uP, yP, sP, ptP, jobP = bank[0:2], bank[2:4], bank[4], bank[5], bank[6], bank[7]

        ident = sb("ident", [128, 128])
        sel_bc = sb("sel_bc", [96, GROUPS, 2, NS], BF16)
        sel_red = sb("sel_red", [128, GROUPS, 32])
        mhalf = sb("mhalf", [128, NT])
        eps_t = sb("eps_t", [128, NT])
        w_dti = sb("w_dti", [D, DTR])
        w_B2 = sb("w_B2", [D, 2, NS])
        w_C2 = sb("w_C2", [D, 2, NS])
        w_dt_s = sb("w_dt_s", [DTR, D])
        wq_s = sb("wq_s", [D, H * HD])
        wv_s = sb("wv_s", [D, KVH * HD])
        wk_s = sb("wk_s", [D, KVH * HD])
        wo_p = sb("wo_p", [128, REP, D])
        w_ssm = sb("w_ssm", [D, D])
        w_x = sb("w_x", [D, D])
        cs_id = sb("cs_id", [D, D])
        convdiag = sb("convdiag", [D, TAPS, D])
        ddiag = sb("ddiag", [D, D])
        cols = sb("cols", [128, 8])
        g_col, b_col, bdt_col, bconv_col, bwm_col, bdc2_col, dssm_col = (cols[:, i:i + 1] for i in range(7))
        bwm_s = sb("bwm_s", [128, 1])
        bdc1_col = sb("bdc1_col", [DTR, 1])
        wconv_s = sb("wconv_s", [128, TAPS])
        alog2 = sb("alog2", [D, 2, NS])
        A_rep = sb("A_rep", [128, UNITS])
        epi = sb("epi", [128, 4, CD])
        w_dc1_s = sb("w_dc1_s", [CD, 64])
        w_dc2_s = sb("w_dc2_s", [64, D])
        decTs = sb("decTs", [D, SE])
        dec_m = sb("dec_m", [128, 4, D])
        rel_raw = sb("rel_raw", [2 * W + 1, H])
        relpad = sb("relpad", [H, RELPAD])
        bias3 = sb("bias3", [128, 3, KVH, 3 * W])
        wf = sb("wf", [D, D])
        wf_abs = sb("wf_abs", [D, D])
        wmax = sb("wmax", [D, 1])
        wmax1 = sb("wmax1", [1, 1])
        ones_row = sb("ones_row", [1, 128])
        wsc = sb("wsc", [128, 4])
        W2 = sb("W2", [D, D])
        fa = sb("fa", [D, RANK])
        faT = sb("faT", [RANK, D])
        fb = sb("fb", [RANK, D])
        bias_row = sb("bias_row", [1, D])

        x_sb = sb("x_sb", [128, NB, NT, D])
        st = sb("st", [128, NT, 6])
        mv = sb("mv", [128, NT, 2])
        ve = sb("ve", [128, NT])
        rr = sb("rr", [128, NT])
        vr = sb("vr", [128, NT])
        rr2 = sb("rr2", [128, NT])
        xa = sb("xa", [128, NT, D])
        xn = sb("xn", [128, NT, D])
        xaT = [sb(f"xaT{p}", [D, LP]) for p in range(2)]
        xnT = sb("xnT", [D, L])
        B2 = [sb(f"B2_{p}", [128, L]) for p in range(2)]
        C2 = [sb(f"C2_{p}", [128, L]) for p in range(2)]
        sp_e, sp_r = (t[:, :, :].rearrange("p t d -> p (t d)") for t in (xn, xa))
        sp_l = sb("sp_l", [D, L])
        sp_t = sb("sp_t", [D, L])
        uv = sb("uv", [D, L])
        kn = uv[0:KVH * HD, :]
        dti, dtv, res = sp_l[0:DTR, :], sp_t, (sp_e, sp_r)
        parts = [sb(f"parts{i}", [D, 3, L], BF16) for i in range(2)]
        spread = [[sb(f"spread{i}_{p}", [96, 4, L], BF16) for p in range(2)] for i in range(2)]
        qn = sb("qn", [H * HD, L])
        v_tok = sb("v_tok", [128, NT, KVH, 32])
        q4 = sb("q4", [128, NBLK, REP, W])
        k4 = sb("k4", [128, KVH, LP])
        vw = sb("vw", [3 * W, NBLK, KVH, 32])
        dA = sb("dA", [128, 4, L])
        dbx = sb("dbx", [128, 3, L])
        hst = sb("hst", [128, 4, L])
        prod = sb("prod", [128, 8, L])
        yT = sb("yT", [D, L])
        s_sb = sb("s_sb", [128, 2, KVH, 3 * W])
        nmax = sb("nmax", [128, 2, KVH])
        prob = sb("prob", [128, 4, KVH, 3 * W])
        psum_r = sb("psum_r", [128, 4, KVH])
        pinv = sb("pinv", [128, 4, KVH])
        probT = sb("probT", [3 * W, KVH, 128])
        ao4 = sb("ao4", [128, REP, L])
        mmx = sb("mmx", [128, NT])
        msum = sb("msum", [128, NT])
        minv = sb("minv", [128, NT])
        mprob = sb("mprob", [128, 2, SE])
        mprobT = sb("mprobT", [128, 4, L])
        epiT, hidT, decT = mprobT[0:CD, 0, :], mprobT[0:64, 1, :], mprobT[:, 2, :]
        cv_v = sb("cv_v", [D, L])
        cv_a = sb("cv_a", [D, L])
        cs = sb("cs", [D, L])
        fT = sb("fT", [D, L])
        x1 = sb("x1", [128, NT, D])
        outb = sb("outb", [128, NT, D])
        st2 = sb("st2", [128, NT, 6])
        mv2 = sb("mv2", [128, NT, 2])
        vz = sb("vz", [128, NT])
        rz = sb("rz", [128, NT])
        zT, z = fT, outb

        x_in = [sem(f"x_in{i}") for i in range(2)]
        w_first, w_in = sem("w_first"), sem("w_in")
        a_in = sem("a_in")
        rel_out, bias_in = sem("rel_out"), sem("bias_in")
        bias_done = sem("bias_done")
        pool_zeros = sem("pool_zeros")
        w_scaled = sem("w_scaled")
        const_ready = sem("const_ready")
        init = sem("init")
        dt_ready, u_ready = sem("dt_ready"), sem("u_ready")
        exp_done, dbx_done, scan_done = sem("exp_done"), sem("dbx_done"), sem("scan_done")
        prod_done, red_done, y_started, y_evac = sem("prod_done"), sem("red_done"), sem("y_started"), sem("y_evac")
        s_ready, s_max = sem("s_ready"), sem("s_max")
        p_exp, p_inv, p_norm = sem("p_exp"), sem("p_inv"), sem("p_norm")
        pt_ready, pt_evac, pv_ready, ao_evac = sem("pt_ready"), sem("pt_evac"), sem("pv_ready"), sem("ao_evac")
        ready = {f: sem(f"{f}_job_ready") for f in "pmt"}
        done = {f: sem(f"{f}_job_done") for f in "pmt"}
        ln_step, sp_step, cv_step, l2_step = sem("ln_step"), sem("sp_step"), sem("cv_step"), sem("l2_step")
        parts_in, k_in, v_in = sem("parts_in"), sem("k_in"), sem("v_in")
        q0_in, q_in = sem("q0_in"), sem("q_in")
        m_max, m_exp, m_inv, m_norm = sem("m_max"), sem("m_exp"), sem("m_inv"), sem("m_norm")
        out_ready, out_done = sem("out_ready"), sem("out_done")

        COUNT = {"p": N_PRE, "m": N_MEM, "t": N_TAIL}
        INDEX = {"p": PRE, "m": MEM, "t": TAIL}

        def wait(eng, s, value):
            if isinstance(value, int) and value <= 0:
                return
            eng.wait_ge(s, value)

        def job_count(fam, B, name):
            return B * COUNT[fam] + INDEX[fam][name] + 1

        def column(v):
            return v.rearrange("(p a) -> p a", a=1)

        def job_bank(front, name):
            return bank[4 + PRE[name] % 4] if front else jobP

        def wait_job(eng, fam, B, name):
            wait(eng, ready[fam], job_count(fam, B, name))

        def run_batches(eng, front, body, tail):
            front(0, 0)
            body(0, 0)
            with eng.Fori(0, (NB - 2) // 2) as k:
                body(k * 2 + 1, 1)
                body(k * 2 + 2, 0)
            body(NB - 1, 1)
            tail(NB - 1, 1)

        def first(B):
            return isinstance(B, int) and B == 0

        def last(B):
            return isinstance(B, int) and B == NB - 1

        INIT = {n: i + 1 for i, n in enumerate(
            ["A_t", "A_e", "A_n", "rel_t", "rel_c",
             "epi_t", "epi_c", "hid", "gelu", "dec", "dec_c", "dec_s", "dec_t", "dec_m",
             "w_abs", "w_max", "w_maxt", "w_max1", "w_bc", "w_c", "w_r", "w_s", "w_q1", "w_q2", "w_q3",
             "fa_t", "fa_c", "ab", "W2"])}
        N_FIRST_DMA, N_W_DMA = 13, 18

        def spread_heads(eng, B):
            wait(eng, done["p"], job_count("p", B, "q"))
            for g in range(KVH):
                for r in range(REP):
                    h = g * REP + r
                    eng.dma_start(q4[32 * g:32 * g + HD, :, r, :],
                                  qn[h * HD:(h + 1) * HD, :].rearrange("p (n q) -> p n q", q=W)) \
                        .then_inc(q0_in if first(B) else q_in, 16)

        def wait_heads(eng, B):
            if first(B):
                eng.wait_ge(q0_in, 16 * N_Q_DMA)
            else:
                wait(eng, q_in, B * 16 * N_Q_DMA)

        def softplus_step(eng, B, name):
            steps = {"log1p": (sp_l, sp_l, sp_t, ALU.subtract),
                     "dt": (dtv, sp_l, sp_r, ALU.add),
                     "u": (uv, dtv, xnT, ALU.mult)}
            o, a, b, op = steps[name]
            wait(eng, sp_step, B * N_SP + SP[name] - 1)
            eng.tensor_tensor(o[:, :], a[:, :], b[:, :], op).then_inc(sp_step, 1)

        def part_step(eng, B, name):
            i = int(name[-1])
            v = (dtv, uv)[i]
            if name[0] == "r":
                wait(eng, sp_step, B * N_SP + SP["hi1"] + i)
                eng.tensor_tensor(res[i][:, :], v[:, :], parts[i][:, 0, :], ALU.subtract).then_inc(sp_step, 1)
            else:
                wait(eng, sp_step, B * N_SP + SP["mid1"] + i)
                eng.tensor_tensor(parts[i][:, 2, :], res[i][:, :], parts[i][:, 1, :], ALU.subtract) \
                    .then_inc(sp_step, 1)

        block = ctx.enter_context(nc.Block())

        @block.sync
        def _(sp):
            def x_load(b):
                sp.dma_start(x_sb[:, b, :, :], x[b].rearrange("(t p) d -> p t d", p=128)) \
                    .then_inc(x_in[min(b, 1)], 16)

            x_load(0)
            n = 0
            for dst, src in ((g_col, column(ln_g)), (b_col, column(ln_b)), (w_dti[:, :], w_xproj[:, 0:DTR]),
                             (w_dt_s[:, :], w_dt), (bdt_col, column(b_dt)), (dssm_col, column(D_ssm)),
                             (w_B2[:, 0, :], w_xproj[:, DTR:DTR + NS]), (w_B2[:, 1, :], w_xproj[:, DTR:DTR + NS]),
                             (w_C2[:, 0, :], w_xproj[:, DTR + NS:]), (w_C2[:, 1, :], w_xproj[:, DTR + NS:]),
                             (wq_s[:, :], wq), (wk_s[:, :], wk), (wv_s[:, :], wv)):
                sp.dma_start(dst, src).then_inc(w_first, 16)
                n += 1
                if n == 2:
                    for j in range(2):
                        sp.dma_start(alog2[:, j, :], A_log).then_inc(a_in, 16)
            assert n == N_FIRST_DMA
            sp.dma_start(rel_raw[:, :], rel_bias).then_inc(a_in, 16)
            for b in range(1, NB):
                x_load(b)
            sp.wait_ge(init, INIT["rel_c"])
            sp.dma_start(rel_dram, relpad[:, :].unsqueeze(1).to_broadcast([H, W, RELPAD])).then_inc(rel_out, 16)
            sp.wait_ge(rel_out, 16)
            flat = rel_dram.rearrange("h q k -> (h q k)")
            for v in range(3):
                for r in range(REP):
                    src = bass.AP(flat.tensor, flat.offset + r * W * RELPAD + W,
                                  [[RELPAD - 1, W], [REP * W * RELPAD, KVH], [1, 3 * W]])
                    sp.dma_start(bias3[r * W:(r + 1) * W, v, :, :], src).then_inc(bias_in, 16)

            def body(B, p):
                if not first(B):
                    store(B - 1, 1 - p)
                if not last(B):
                    front(B + 1, 1 - p)

            def load_weights():
                n = 0
                for dst, src in ((bconv_col, column(b_conv)), (bwm_col, column(b_wm)), (bdc2_col, column(b_dc2)),
                                 (wconv_s[:, :], w_conv),
                                 (epi[:, :, :], episodic[0].rearrange("(c p) k -> p c k", p=128)),
                                 (w_dc1_s[:, :], w_dc1), (bdc1_col[:, :], column(b_dc1)), (w_dc2_s[:, :], w_dc2),
                                 (wf[:, :], ffn_w), (fa[:, :], ffn_a), (fb[:, :], ffn_b),
                                 (bias_row[:, :], ffn_bias.rearrange("(a n) -> a n", a=1)),
                                 (w_ssm[:, :], w_ssm_out), (w_x[:, :], w_wm)):
                    sp.dma_start(dst, src).then_inc(w_in, 16)
                    n += 1
                sp.wait_ge(const_ready, 2)
                for g in range(KVH):
                    sp.dma_start(wo_p[32 * g:32 * g + HD, :, :],
                                 wo[g * REP * HD:(g + 1) * REP * HD, :].rearrange("(r h) e -> h r e", r=REP)) \
                        .then_inc(w_in, 16)
                    n += 1
                assert n == N_W_DMA

            def front(B, p):
                wait(sp, u_ready, (B - 1) * UNITS)
                wait(sp, dt_ready, (B - 1) * UNITS)
                for part, made in enumerate(("hi", "mid", "lo")):
                    for i in range(2):
                        wait(sp, sp_step, B * N_SP + SP[f"{made}{i}"])
                        for c in range(4):
                            sp.dma_start(spread[i][p][32 * part:32 * part + 32, c, :],
                                         parts[i][32 * c:32 * c + 32, part, :]).then_inc(parts_in, 16)
                if not first(B):
                    spread_heads(sp, B)
                wait(sp, done["p"], job_count("p", B, "k"))
                for g in range(KVH):
                    sp.dma_start(k4[32 * g:32 * g + HD, g, HALO:HALO + L], kn[g * HD:(g + 1) * HD, :]) \
                        .then_inc(k_in, 16)
                if first(B):
                    load_weights()
                wait(sp, done["p"], job_count("p", B, "v"))
                for j in range(3):
                    for m in range(4):
                        blocks = [n for n in range(NBLK) if 0 <= n - 1 + j < NBLK and (n - 1 + j) % 4 == m]
                        t0 = (blocks[0] - 1 + j) // 4
                        sp.dma_start(vw[32 * j:32 * j + 32, blocks[0]:blocks[-1] + 1:4, :, :]
                                     .rearrange("p n g h -> p n (g h)"),
                                     v_tok[32 * m:32 * m + 32, t0:t0 + len(blocks), :, :]
                                     .rearrange("p t g h -> p t (g h)")).then_inc(v_in, 16)

            def store(B, p):
                wait(sp, out_ready, B + 1)
                dst = out[B] if isinstance(B, int) else out[bass.ds(B, 1)].rearrange("a l d -> (a l) d")
                sp.dma_start(dst.rearrange("(t p) d -> p t d", p=128), outb[:, :, :]).then_inc(out_done, 16)

            run_batches(sp, front, body, store)
            sp.wait_ge(out_done, 16 * NB + 1)

        @block.scalar
        def _(act):
            act.wait_ge(init, INIT["A_t"])
            for j in range(2):
                ins = nc.scalar.activation(A_rep[64 * j:64 * j + 64, :],
                                           jobP[64 * j:64 * j + 64, 0:D].rearrange("p (g j) -> p g j", j=2)[:, :, j],
                                           ACT.Exp)
            ins.then_inc(init, 1)
            act.wait_ge(init, INIT["A_e"])
            nc.scalar.activation(A_rep[:, :], A_rep[:, :], ACT.Copy, scale=-1.0).then_inc(init, 1)
            act.wait_ge(init, INIT["rel_t"])
            act.wait_ge(const_ready, 1)
            nc.scalar.activation(relpad[:, W:W + 2 * W + 1], jobP[0:H, 0:2 * W + 1], ACT.Copy,
                                 scale=-1.0).then_inc(init, 1)

            def setup_step(s):
                if s == 0:
                    act.wait_ge(w_in, 16 * N_W_DMA)
                    act.wait_ge(init, INIT["epi_t"])
                    nc.scalar.activation(epiT, jobP[0:CD, :], ACT.Copy).then_inc(init, 1)
                if s == 1:
                    act.wait_ge(init, INIT["hid"])
                    nc.scalar.activation(hidT, jobP[0:64, :], ACT.Gelu, bias=bdc1_col[:, :]).then_inc(init, 1)
                if s == 2:
                    act.wait_ge(init, INIT["dec"])
                    nc.scalar.activation(decT, jobP[:, :], ACT.Identity, bias=bdc2_col).then_inc(init, 1)
                    act.wait_ge(init, INIT["dec_c"])
                    nc.scalar.activation(decTs[:, :], decT, ACT.Copy, scale=float(D) ** -0.5).then_inc(init, 1)
                if s == 3:
                    act.wait_ge(init, INIT["dec_t"])
                    nc.scalar.activation(dec_m[:, :, :].rearrange("p c d -> p (c d)"), jobP[:, :], ACT.Copy,
                                         scale=RW_MEM * MEM_MIX).then_inc(init, 1)
                    nc.scalar.activation(wf_abs[:, :], wf[:, :], ACT.Abs).then_inc(init, 1)
                if s == 5:
                    act.wait_ge(init, INIT["w_bc"])
                    nc.scalar.activation(wsc[:, 0:1], jobP[:, 0:1], ACT.Copy).then_inc(init, 1)
                if s == 6:
                    act.wait_ge(init, INIT["fa_t"])
                    nc.scalar.activation(faT[:, :], jobP[0:RANK, 0:D], ACT.Copy).then_inc(init, 1)

            def scale_xn(B):
                wait(act, ln_step, B * N_LN + LN["xa"])
                for t in range(NT):
                    ins = nc.scalar.activation(xn[:, t, :], xa[:, t, :], ACT.Copy, scale=rr2[:, t:t + 1])
                ins.then_inc(ln_step, 1)

            def pre_job(name, B, p, front=False):
                job = job_bank(front, name)
                wait_job(act, "p", B, name)
                if name == "xaT":
                    ins = nc.scalar.activation(xaT[p][:, HALO:HALO + L], job[:, :], ACT.Copy)
                elif name == "xnT":
                    ins = nc.scalar.activation(xnT[:, :], job[:, :], ACT.Identity, bias=b_col, scale=g_col)
                elif name == "dti":
                    ins = nc.scalar.activation(dti[:, :], job[0:DTR, :], ACT.Copy)
                elif name in "BC":
                    ins = nc.scalar.activation((B2 if name == "B" else C2)[p][:, :], job[:, :], ACT.Copy)
                elif name == "dtpre":
                    nc.scalar.activation(sp_e[:, :], job[:, :], ACT.Abs, bias=bdt_col).then_inc(sp_step, 1)
                    nc.scalar.activation(sp_r[:, :], job[:, :], ACT.Relu, bias=bdt_col).then_inc(sp_step, 1)
                    act.wait_ge(sp_step, B * N_SP + SP["relu"])
                    act.sem_inc(done["p"], 1)
                    return
                elif name == "k":
                    ins = nc.scalar.activation(kn, job[0:KVH * HD, :], ACT.Copy)
                elif name == "v":
                    wait(act, v_in, B * 16 * N_V_DMA)
                    ins = nc.scalar.activation(v_tok[:, :, :, 0:HD].rearrange("p t g h -> p (t g) h"),
                                               job[:, 0:128].rearrange("p (a h) -> p a h", h=HD), ACT.Copy)
                else:
                    if not first(B):
                        wait_heads(act, B - 1)
                    ins = nc.scalar.activation(qn[:, :], job[:, :], ACT.Copy, scale=-float(HD) ** -0.5)
                ins.then_inc(done["p"], 1)

            def softplus_exp(B):
                wait(act, sp_step, B * N_SP + SP["relu"])
                nc.scalar.activation(sp_e[:, :], sp_e[:, :], ACT.Exp, scale=-1.0).then_inc(sp_step, 1)

            def softplus_logs(B):
                wait(act, sp_step, B * N_SP + SP["sum"])
                nc.scalar.activation(sp_l[:, :], sp_e[:, :], ACT.Ln, bias=1.0).then_inc(sp_step, 1)

            def high_parts(B):
                wait(act, parts_in, B * 16 * N_PARTS_DMA)
                wait(act, sp_step, B * N_SP + SP["u"])
                for i, v in enumerate((dtv, uv)):
                    nc.scalar.activation(parts[i][:, 0, :], v[:, :], ACT.Copy).then_inc(sp_step, 1)

            def mid_parts(B):
                wait(act, sp_step, B * N_SP + SP["r1"])
                for i in range(2):
                    nc.scalar.activation(parts[i][:, 1, :], res[i][:, :], ACT.Copy).then_inc(sp_step, 1)

            def front(B, p):
                scale_xn(B)
                for name in PRE:
                    if name == "B":
                        softplus_exp(B)
                        softplus_logs(B)
                    if name == "q":
                        high_parts(B)
                    if name == "k":
                        mid_parts(B)
                    pre_job(name, B, p, front=True)
                for s in range(AHEAD):
                    unit_exp(B, s)

            def unit_exp(B, s):
                i, q = divmod(s, 4)
                wait(act, dt_ready, B * UNITS + s + 1)
                wait(act, scan_done, B * UNITS + s - 3)
                g = GROUPS * q + i
                nc.scalar.activation(dA[:, s % 4, :], dtP[s % 2][:, :], ACT.Exp, scale=A_rep[:, g:g + 1]) \
                    .then_inc(exp_done, 1)

            def y_copy(B):
                wait(act, red_done, (B + 1) * GROUPS)
                nc.scalar.activation(yT[:, :], yP[:, :], ACT.Copy).then_inc(y_evac, 1)

            def probabilities(B, k, half):
                if half == 0:
                    wait(act, s_max, B * NBLK + k + 1)
                    wait(act, pt_ready, B * NBLK + k - 3)
                for g in (2 * half, 2 * half + 1):
                    ins = nc.scalar.activation(prob[:, k % 4, g, :], s_sb[:, k % 2, g, :], ACT.Exp,
                                               bias=nmax[:, k % 2, g:g + 1], scale=-1.0,
                                               accum_out=psum_r[:, k % 4, g:g + 1])
                if half == 1:
                    ins.then_inc(p_exp, 1)

            def probT_copy(B, k):
                wait(act, pt_ready, B * NBLK + k + 1)
                wait(act, pv_ready, B * NBLK + k)
                nc.scalar.activation(probT[:, :, :].rearrange("p g t -> p (g t)"), ptP[0:3 * W, :], ACT.Copy) \
                    .then_inc(pt_evac, 1)

            def ao_copy(B, k):
                wait(act, pv_ready, B * NBLK + k + 1)
                if k == 0:
                    wait(act, ready["t"], B * N_TAIL - N_TAIL + 1)
                nc.scalar.activation(ao4[:, :, k * W:(k + 1) * W],
                                     ptP[:, 0:128].rearrange("p (r q) -> p r q", r=REP), ACT.Copy).then_inc(ao_evac, 1)

            def mem_exp(B, t):
                wait(act, m_max, B * NT + t + 1)
                if t >= 2:
                    wait_job(act, "m", B, f"pt{t - 2}")
                ins = nc.scalar.activation(mprob[:, t % 2, :], jobP[:, :], ACT.Exp, bias=mmx[:, t:t + 1],
                                           accum_out=msum[:, t:t + 1])
                ins.then_inc(m_exp, 1)
                act.wait_ge(m_exp, B * NT + t + 1)
                act.sem_inc(done["m"], 1)

            def memT_copy(B, t):
                wait_job(act, "m", B, f"pt{t}")
                if t == 0:
                    wait(act, ready["t"], B * N_TAIL - N_TAIL + 1)
                nc.scalar.activation(mprobT[:, :, t * 128:(t + 1) * 128],
                                     jobP[:, :].rearrange("p (c t) -> p c t", c=4), ACT.Copy).then_inc(done["m"], 1)

            def conv_bias(B):
                wait_job(act, "m", B, "conv")
                nc.scalar.activation(cv_v[:, :], jobP[:, :], ACT.Identity, bias=bconv_col).then_inc(cv_step, 1)
                act.wait_ge(cv_step, B * N_CV + CV["v"])
                act.sem_inc(done["m"], 1)

            def conv_tanh(B):
                nc.scalar.activation(cv_a[:, :], cv_v[:, :], ACT.Tanh, scale=0.5).then_inc(cv_step, 1)

            def proj_copy(B):
                wait_job(act, "t", B, "proj")
                nc.scalar.activation(fT[:, :], jobP[:, :], ACT.Identity, bias=bwm_s[:, :]).then_inc(done["t"], 1)

            def zT_copy(B):
                wait_job(act, "t", B, "zT")
                nc.scalar.activation(zT[:, :], jobP[:, :], ACT.Copy).then_inc(done["t"], 1)

            def empty_job(fam, name, B, p):
                if fam == "p":
                    if not last(B):
                        pre_job(name, B + 1, 1 - p)
                elif name == "zT":
                    if not first(B):
                        zT_copy(B - 1)
                elif name == "conv":
                    conv_bias(B)
                elif name[:2] == "pt":
                    memT_copy(B, int(name[2]))

            def body(B, p):
                for s in range(UNITS):
                    if s + AHEAD < UNITS:
                        unit_exp(B, s + AHEAD)
                    elif not last(B):
                        unit_exp(B + 1, s + AHEAD - UNITS)
                    if first(B):
                        setup_step(s - SETUP_AT)
                    else:
                        if s == AT["y_copy"]:
                            y_copy(B - 1)
                        if s == AT["proj_copy"]:
                            proj_copy(B - 1)
                    for half in range(2):
                        k = block_at(s, EXP_LAG[half])
                        if k is not None:
                            probabilities(B, k, half)
                    k = block_at(s, PT_COPY_LAG)
                    if k is not None:
                        probT_copy(B, k)
                    k = block_at(s, AO_COPY_LAG)
                    if k is not None:
                        ao_copy(B, k)
                    t = memory_tile_at(s, M_EXP_LAG)
                    if t is not None:
                        mem_exp(B, t)
                    if s - EMPTY_LAG in JOB_AT:
                        empty_job(*JOB_AT[s - EMPTY_LAG], B, p)
                    if s == AT["tanh"]:
                        conv_tanh(B)
                    if not last(B):
                        if s == AT["scale_xn"]:
                            scale_xn(B + 1)
                        if s == AT["softplus_exp"]:
                            softplus_exp(B + 1)
                        if s == AT["softplus_logs"]:
                            softplus_logs(B + 1)
                        if s == AT["high"]:
                            high_parts(B + 1)
                        if s == AT["mid"]:
                            mid_parts(B + 1)

            def tail(B, p):
                y_copy(B)
                proj_copy(B)
                zT_copy(B)

            run_batches(act, front, body, tail)

        @block.tensor
        def _(pe):
            mm = nc.tensor.matmul

            def transposes(srcs, rows, step, job=jobP):
                for c, src in enumerate(srcs):
                    ins = nc.tensor.transpose(job[0:rows, c * step:(c + 1) * step], src, ident[:, :])
                return ins

            pe.wait_ge(const_ready, 1)
            pe.wait_ge(a_in, 16 * 3)
            nc.tensor.transpose(jobP[:, 0:D], alog2[:, :, :].rearrange("p j n -> p (j n)"), ident[:, :]).then_inc(init, 1)
            pe.wait_ge(init, INIT["A_n"])
            nc.tensor.transpose(jobP[0:H, 0:2 * W + 1], rel_raw[:, :], ident[0:2 * W + 1, 0:2 * W + 1]).then_inc(init, 1)
            pe.wait_ge(init, INIT["rel_c"])
            pe.wait_ge(w_first, 16 * N_FIRST_DMA)

            def setup_step(s):
                if s == 0:
                    pe.wait_ge(w_in, 16 * N_W_DMA)
                    wait(pe, done["p"], job_count("p", 0, "v"))
                    transposes([epi[:, c, :] for c in range(4)], CD, 128).then_inc(init, 1)
                if s == 1:
                    pe.wait_ge(init, INIT["epi_c"])
                    mm(jobP[0:64, :], w_dc1_s[:, :], epiT, start=True, stop=True).then_inc(init, 1)
                if s == 2:
                    pe.wait_ge(init, INIT["gelu"])
                    mm(jobP[:, :], w_dc2_s[:, :], hidT, start=True, stop=True).then_inc(init, 1)
                if s == 3:
                    pe.wait_ge(init, INIT["dec_s"])
                    transposes([decT[:, c * 128:(c + 1) * 128] for c in range(4)], 128, 128).then_inc(init, 1)
                if s == 4:
                    pe.wait_ge(init, INIT["w_max"])
                    nc.tensor.transpose(jobP[0:1, 0:D], wmax[:, :], ident[:, :]).then_inc(init, 1)
                if s == 5:
                    pe.wait_ge(init, INIT["w_max1"])
                    mm(jobP[:, 0:1], ones_row[:, :], wmax1[:, :], start=True, stop=True).then_inc(init, 1)
                if s == 6:
                    pe.wait_ge(init, INIT["w_q3"])
                    nc.tensor.transpose(jobP[0:RANK, 0:D], fa[:, :], ident[:, :]).then_inc(init, 1)
                if s == 7:
                    pe.wait_ge(init, INIT["fa_c"])
                    mm(jobP[:, 0:D], faT[:, :], fb[:, :], start=True, stop=True).then_inc(init, 1)
                if s == 8:
                    pe.wait_ge(init, INIT["W2"])
                    pe.wait_ge(w_scaled, 2)

            before = [None]

            def fill(fam, B, name):
                if before[0] is not None:
                    f, b, n = before[0]
                    wait(pe, done[f], job_count(f, b, n))

            def filled(ins, fam, B, name):
                ins.then_inc(ready[fam], 1)
                before[0] = (fam, B, name)

            def pre_job(name, B, p, front=False):
                job = job_bank(front, name)
                if not front:
                    fill("p", B, name)
                elif PRE[name] >= 4:
                    pe.wait_ge(done["p"], PRE[name] - 3)
                if name == "xaT":
                    wait(pe, ln_step, B * N_LN + LN["xa"])
                    ins = transposes([xa[:, t, :] for t in range(NT)], 128, 128, job)
                elif name == "xnT":
                    wait(pe, ln_step, B * N_LN + LN["xn"])
                    ins = transposes([xn[:, t, :] for t in range(NT)], 128, 128, job)
                elif name == "dti":
                    wait(pe, done["p"], job_count("p", B, "xnT"))
                    ins = mm(job[0:DTR, :], w_dti[:, :], xnT[:, :], start=True, stop=True)
                elif name == "dtpre":
                    wait(pe, done["p"], job_count("p", B, "dti"))
                    ins = mm(job[:, :], w_dt_s[:, :], dti[:, :], start=True, stop=True)
                elif name in "BC":
                    w = w_B2 if name == "B" else w_C2
                    ins = mm(job[:, :], w[:, :, :].rearrange("d j n -> d (j n)"), xnT[:, :], start=True, stop=True)
                elif name == "k":
                    ins = mm(job[0:KVH * HD, :], wk_s[:, :], xaT[p][:, HALO:HALO + L], start=True, stop=True)
                elif name == "v":
                    for t in range(NT):
                        ins = mm(job[:, t * 32:(t + 1) * 32], xaT[p][:, HALO + t * 128:HALO + (t + 1) * 128],
                                 wv_s[:, :], start=True, stop=True)
                else:
                    ins = mm(job[:, :], wq_s[:, :], xaT[p][:, HALO:HALO + L], start=True, stop=True)
                filled(ins, "p", B, name)

            def unit_u(B, p, s):
                i, q = divmod(s, 4)
                wait(pe, dbx_done, B * UNITS + s - 1)
                mm(uP[s % 2][:, :], sel_bc[:, i, :, :].rearrange("k j n -> k (j n)"), spread[1][p][:, q, :],
                   start=True, stop=True).then_inc(u_ready, 1)

            def unit_dt(B, p, s):
                i, q = divmod(s, 4)
                if s == 0:
                    wait(pe, parts_in, (B + 1) * 16 * N_PARTS_DMA)
                wait(pe, exp_done, B * UNITS + s - 1)
                mm(dtP[s % 2][:, :], sel_bc[:, i, :, :].rearrange("k j n -> k (j n)"), spread[0][p][:, q, :],
                   start=True, stop=True).then_inc(dt_ready, 1)

            def front(B, p):
                for name in PRE:
                    if name == "q":
                        pe.wait_ge(const_ready, 3)
                    pre_job(name, B, p, front=True)
                for s in range(AHEAD):
                    unit_dt(B, p, s)
                unit_u(B, p, 0)

            def y_start(B, p):
                if first(B):
                    pe.wait_ge(w_scaled, 1)
                wait(pe, y_evac, B)
                mm(yP[:, :], ddiag[:, :], xaT[p][:, HALO:HALO + L], start=True, stop=False,
                   skip_group_check=True).then_inc(y_started, 1)

            def reduce_group(B, i):
                wait(pe, prod_done, B * PAIRS + 2 * i + 2)
                for q in range(4):
                    ins = mm(yP[32 * q:32 * q + 32, :], sel_red[:, i, :], prod[:, (i % 2) * 4 + q, :], start=False,
                             stop=(i == GROUPS - 1), skip_group_check=True)
                ins.then_inc(red_done, 1)

            def scores(B, p, k):
                if k == 0:
                    wait(pe, k_in, (B + 1) * 16 * KVH)
                    wait_heads(pe, B)
                wait(pe, s_max, B * NBLK + k)
                mm(sP[:, 0:KVH * 3 * W], q4[:, k, :, :].rearrange("p r q -> p (r q)"), k4[:, :, k * W:k * W + 3 * W],
                   start=True, stop=True).then_inc(s_ready, 1)

            def prob_transposes(B, k):
                wait(pe, p_norm, B * NBLK + k + 1)
                wait(pe, ao_evac, B * NBLK + k)
                for g in range(KVH):
                    ins = nc.tensor.transpose(ptP[0:3 * W, g * 128:(g + 1) * 128], prob[:, k % 4, g, :], ident[:, :])
                ins.then_inc(pt_ready, 1)

            def values(B, p, k):
                if k == 0:
                    wait(pe, v_in, (B + 1) * 16 * N_V_DMA)
                wait(pe, pt_evac, B * NBLK + k + 1)
                for g in range(KVH):
                    ins = mm(ptP[32 * g:32 * g + 32, 0:128], vw[:, k, g, :], probT[:, g, :], start=True, stop=True)
                ins.then_inc(pv_ready, 1)

            def conv_tap(B, p, tap):
                if tap == 0:
                    fill("m", B, "conv")
                o = HALO - (TAPS - 1) + tap
                ins = mm(jobP[:, :], convdiag[:, tap, :], xaT[p][:, o:o + L], start=(tap == 0), stop=(tap == TAPS - 1))
                if tap == TAPS - 1:
                    filled(ins, "m", B, "conv")

            def mem_job(name, B, p):
                fill("m", B, name)
                if name[:2] == "es":
                    t = int(name[2])
                    ins = mm(jobP[:, :], xaT[p][:, HALO + t * 128:HALO + (t + 1) * 128], decTs[:, :], start=True,
                             stop=True)
                else:
                    t = int(name[2])
                    wait(pe, m_norm, B * NT + t + 1)
                    ins = transposes([mprob[:, t % 2, c * 128:(c + 1) * 128] for c in range(4)], 128, 128)
                filled(ins, "m", B, name)

            def project(B, p, n):
                if n == 0:
                    fill("t", B, "proj")
                    ins = mm(jobP[:, :], w_x[:, :], xaT[p][:, HALO:HALO + L], start=True, stop=False)
                elif n == 1:
                    wait(pe, cv_step, (B + 1) * N_CV)
                    ins = mm(jobP[:, :], cs_id[:, :], cs[:, :], start=False, stop=False)
                elif n < 6:
                    wait(pe, done["m"], job_count("m", B, "pt3"))
                    ins = mm(jobP[:, :], dec_m[:, n - 2, :], mprobT[:, n - 2, :], start=False, stop=False)
                elif n < 10:
                    wait(pe, ao_evac, (B + 1) * NBLK)
                    ins = mm(jobP[:, :], wo_p[:, n - 6, :], ao4[:, n - 6, :], start=False, stop=False)
                else:
                    wait(pe, y_evac, B + 1)
                    ins = mm(jobP[:, :], w_ssm[:, :], yT[:, :], start=False, stop=True)
                    filled(ins, "t", B, "proj")

            def tail_job(name, B, p):
                fill("t", B, name)
                if name == "back":
                    wait(pe, done["t"], job_count("t", B, "proj"))
                    ins = transposes([fT[:, t * 128:(t + 1) * 128] for t in range(NT)], 128, 128)
                elif name == "zT":
                    wait(pe, l2_step, B * N_L2 + L2["z"])
                    ins = transposes([z[:, t, :] for t in range(NT)], 128, 128)
                else:
                    wait(pe, done["t"], job_count("t", B, "zT"))
                    for t in range(NT):
                        mm(jobP[:, t * D:(t + 1) * D], zT[:, t * 128:(t + 1) * 128], W2[:, :], start=True,
                           stop=False)
                        ins = mm(jobP[:, t * D:(t + 1) * D], ones_row[:, :], bias_row[:, :], start=False, stop=True)
                filled(ins, "t", B, name)

            def body(B, p):
                before[0] = ("p", B, "v")
                for s in range(UNITS):
                    if s + AHEAD < UNITS:
                        unit_dt(B, p, s + AHEAD)
                    elif not last(B):
                        unit_dt(B + 1, 1 - p, s + AHEAD - UNITS)
                    if s < UNITS - 1:
                        unit_u(B, p, s + 1)
                    elif not last(B):
                        unit_u(B + 1, 1 - p, 0)
                    if first(B):
                        setup_step(s - SETUP_AT)
                    else:
                        if s == AT["reduce"]:
                            reduce_group(B - 1, GROUPS - 1)
                        if 0 <= s - AT["project"] < N_PROJ:
                            project(B - 1, 1 - p, s - AT["project"])
                    if s == AT["y_start"]:
                        y_start(B, p)
                    if s >= AT["reduce"] + 4 and (s - AT["reduce"]) % 4 == 0:
                        reduce_group(B, (s - AT["reduce"]) // 4 - 1)
                    k = block_at(s, 0)
                    if k is not None:
                        scores(B, p, k)
                    k = block_at(s, PT_LAG)
                    if k is not None:
                        prob_transposes(B, k)
                    k = block_at(s, PV_LAG)
                    if k is not None:
                        values(B, p, k)
                    tap = s - JOB_SLOT["conv"] + TAPS - 1
                    if 0 <= tap < TAPS:
                        conv_tap(B, p, tap)
                    fam, name = JOB_AT.get(s, ("", ""))
                    if fam == "t" and not first(B):
                        tail_job(name, B - 1, 1 - p)
                    if fam == "p" and not last(B):
                        pre_job(name, B + 1, 1 - p)
                    if fam == "m" and name != "conv":
                        mem_job(name, B, p)
                    if last(B) and 0 < s - JOB_SLOT["pt3"] <= N_EARLY:
                        project(B, p, s - JOB_SLOT["pt3"] - 1)

            def tail(B, p):
                for n in range(N_EARLY, N_PROJ - 1):
                    project(B, p, n)
                reduce_group(B, GROUPS - 1)
                project(B, p, N_PROJ - 1)
                for name in ("back", "zT", "ffn"):
                    tail_job(name, B, p)

            run_batches(pe, front, body, tail)

        @block.vector
        def _(dve):
            v = nc.vector
            dve.sem_inc(out_done, 1)
            def skip_diagonal():
                dve.wait_ge(const_ready, 1)
                dve.wait_ge(w_first, 16 * N_FIRST_DMA)
                v.tensor_scalar(ddiag[:, :], ident[:, :], dssm_col, None, ALU.mult).then_inc(w_scaled, 1)

            def finish_bias():
                dve.wait_ge(bias_in, 16 * 3 * REP)
                v.memset(bias3[:, 0, :, 0:W], -MASKED)
                v.memset(bias3[:, 2, :, 2 * W:3 * W], -MASKED).then_inc(bias_done, 1)
                dve.wait_ge(bias_done, 1)

            def setup_step(s):
                if s == 1:
                    dve.wait_ge(w_in, 16 * N_W_DMA)
                    v.tensor_scalar(wo_p[:, :, :], wo_p[:, :, :], RW_ATTN, None, ALU.mult)
                    v.tensor_scalar(w_ssm[:, :], w_ssm[:, :], RW_SSM, None, ALU.mult)
                    v.scalar_tensor_tensor(w_x[:, :], w_x[:, :], RW_MEM, ident[:, :], ALU.mult, ALU.add)
                    v.tensor_scalar(cs_id[:, :], ident[:, :], 0.5 * RW_CONV, None, ALU.mult)
                    v.tensor_scalar(bwm_s[:, :], bwm_col, RW_MEM, None, ALU.mult)
                    for k in range(TAPS):
                        ins = v.tensor_scalar(convdiag[:, k, :], ident[:, :], wconv_s[:, k:k + 1], None, ALU.mult)
                    ins.then_inc(w_scaled, 1)
                if s == 3:
                    dve.wait_ge(init, INIT["w_abs"])
                    v.tensor_reduce(wmax[:, :], wf_abs[:, :], AX.X, ALU.max).then_inc(init, 1)
                if s == 4:
                    dve.wait_ge(init, INIT["w_maxt"])
                    v.tensor_reduce(wmax1[:, :], jobP[0:1, 0:D], AX.X, ALU.max).then_inc(init, 1)
                if s == 5:
                    dve.wait_ge(init, INIT["w_c"])
                    v.reciprocal(wsc[:, 3:4], wsc[:, 0:1]).then_inc(init, 1)
                    dve.wait_ge(init, INIT["w_r"])
                    v.tensor_scalar(wsc[:, 1:2], wsc[:, 3:4], 7.0, None, ALU.mult)
                    v.tensor_scalar(wsc[:, 2:3], wsc[:, 0:1], 1.0 / 7.0, None, ALU.mult).then_inc(init, 1)
                    dve.wait_ge(init, INIT["w_s"])
                    v.tensor_scalar(wf_abs[:, :], wf[:, :], wsc[:, 1:2], ROUND, ALU.mult, ALU.add).then_inc(init, 1)
                    dve.wait_ge(init, INIT["w_q1"])
                    v.tensor_scalar(wf_abs[:, :], wf_abs[:, :], ROUND, 7.0, ALU.subtract, ALU.min).then_inc(init, 1)
                    dve.wait_ge(init, INIT["w_q2"])
                    v.tensor_scalar(wf_abs[:, :], wf_abs[:, :], -8.0, wsc[:, 2:3], ALU.max, ALU.mult).then_inc(init, 1)
                if s == 7:
                    dve.wait_ge(init, INIT["ab"])
                    v.tensor_tensor(W2[:, :], wf_abs[:, :], jobP[:, 0:D], ALU.add).then_inc(init, 1)

            def ln_stats(B):
                dve.wait_ge(x_in[0], 16)
                if not first(B):
                    dve.wait_ge(x_in[1], 16 * (NB - 1))
                for t in range(NT):
                    ins = v.bn_stats(st[:, t, :], xin(B)[:, t, :])
                ins.then_inc(ln_step, 1)

            def ln_stats_there(B):
                dve.wait_ge(ln_step, B * N_LN + LN["stats"])

            def ln_aggr(B):
                for t in range(NT):
                    ins = v.bn_aggr(mv[:, t, :], st[:, t, :])
                ins.then_inc(ln_step, 1)
                dve.wait_ge(ln_step, B * N_LN + LN["aggr"])
                v.tensor_scalar(ve[:, :], mv[:, :, 1], EPS, None, ALU.add).then_inc(ln_step, 1)

            def xin(B):
                if isinstance(B, int):
                    return x_sb[:, B, :, :]
                return x_sb[:, bass.ds(B, 1), :, :].rearrange("p a t d -> p (a t) d")

            def ln_apply(B):
                dve.wait_ge(ln_step, B * N_LN + LN["r2"])
                for t in range(NT):
                    ins = v.tensor_scalar(xa[:, t, :], xin(B)[:, t, :], mv[:, t, 0:1], rr[:, t:t + 1], ALU.subtract,
                                          ALU.mult)
                ins.then_inc(ln_step, 1)

            def softplus_sum(B):
                dve.wait_ge(sp_step, B * N_SP + SP["exp"])
                v.tensor_scalar(sp_t[:, :], sp_e[:, :], 1.0, None, ALU.add).then_inc(sp_step, 1)

            def softplus_rounding(B):
                dve.wait_ge(sp_step, B * N_SP + SP["ln"])
                v.scalar_tensor_tensor(sp_t[:, :], sp_t[:, :], 1.0, sp_e[:, :], ALU.subtract, ALU.subtract) \
                    .then_inc(sp_step, 1)

            def front(B, p):
                ln_stats(B)
                ln_stats_there(B)
                ln_aggr(B)
                ln_apply(B)
                skip_diagonal()
                softplus_sum(B)
                softplus_rounding(B)
                for name in ("log1p", "dt", "u"):
                    softplus_step(v, B, name)
                for name in ("r0", "r1", "lo0", "lo1"):
                    part_step(v, B, name)
                finish_bias()

            def unit_input(B, p, s):
                if s == 0:
                    wait(dve, done["p"], job_count("p", B, "C"))
                wait(dve, u_ready, B * UNITS + s + 1)
                wait(dve, scan_done, B * UNITS + (s - 2 if s else 0))
                v.tensor_tensor(dbx[:, s % 3, :], uP[s % 2][:, :], B2[p][:, :], ALU.mult).then_inc(dbx_done, 1)

            def unit_scan(B, s):
                wait(dve, exp_done, B * UNITS + s + 1)
                wait(dve, dbx_done, B * UNITS + s + 1)
                wait(dve, prod_done, B * PAIRS + s // 2 - 1)
                v.tensor_tensor_scan(hst[:, s % 4, :], dA[:, s % 4, :], dbx[:, s % 3, :], 0.0, ALU.mult,
                                     ALU.add).then_inc(scan_done, 1)

            def scores_there(B, k):
                wait(dve, s_ready, B * NBLK + k + 1)
                wait(dve, p_exp, B * NBLK + k - 1)

            def bias_and_max(B, k):
                row = 0 if k == 0 else 2 if k == NBLK - 1 else 1
                for g in range(KVH):
                    ins = v.tensor_tensor_reduce(s_sb[:, k % 2, g, :], sP[:, g * 3 * W:(g + 1) * 3 * W],
                                                 bias3[:, row, g, :], 1.0, BIG, ALU.add, ALU.min,
                                                 nmax[:, k % 2, g:g + 1])
                ins.then_inc(s_max, 1)

            def inverse_sums(B, k):
                wait(dve, p_exp, B * NBLK + k + 1)
                wait(dve, p_norm, B * NBLK + k - 3)
                v.reciprocal(pinv[:, k % 4, :], psum_r[:, k % 4, :]).then_inc(p_inv, 1)

            def mem_max(B, t):
                wait_job(dve, "m", B, f"es{t}")
                v.tensor_reduce(mmx[:, t:t + 1], jobP[:, :], AX.X, ALU.max, negate=True).then_inc(m_max, 1)

            def mem_norm(B, t):
                wait(dve, m_exp, B * NT + t + 1)
                v.reciprocal(minv[:, t:t + 1], msum[:, t:t + 1]).then_inc(m_inv, 1)
                dve.wait_ge(m_inv, B * NT + t + 1)
                v.tensor_scalar(mprob[:, t % 2, :], mprob[:, t % 2, :], minv[:, t:t + 1], None, ALU.mult) \
                    .then_inc(m_norm, 1)

            def conv_gate(B):
                wait(dve, cv_step, B * N_CV + CV["tanh"])
                wait(dve, ready["t"], B * N_TAIL - N_TAIL + 1)
                v.scalar_tensor_tensor(cs[:, :], cv_a[:, :], 1.0, cv_v[:, :], ALU.add, ALU.mult).then_inc(cv_step, 1)

            def residual(B):
                wait_job(dve, "t", B, "back")
                v.tensor_tensor(x1[:, :, :], jobP[:, :].rearrange("p (t d) -> p t d", t=NT), xin(B), ALU.add) \
                    .then_inc(l2_step, 1)
                dve.wait_ge(l2_step, B * N_L2 + L2["x1"])
                dve.sem_inc(done["t"], 1)
                for t in range(NT):
                    ins = v.bn_stats(st2[:, t, :], x1[:, t, :])
                ins.then_inc(l2_step, 1)

            def stats2_there(B):
                dve.wait_ge(l2_step, B * N_L2 + L2["stats"])

            def aggr2(B):
                for t in range(NT):
                    ins = v.bn_aggr(mv2[:, t, :], st2[:, t, :])
                ins.then_inc(l2_step, 1)
                dve.wait_ge(l2_step, B * N_L2 + L2["aggr"])
                v.tensor_scalar(vz[:, :], mv2[:, :, 1], EPS, None, ALU.add).then_inc(l2_step, 1)

            def normalise2(B):
                wait(dve, l2_step, B * N_L2 + L2["r"])
                wait(dve, out_done, B * 16 + 1)
                for t in range(NT):
                    ins = v.tensor_scalar(z[:, t, :], x1[:, t, :], mv2[:, t, 0:1], rz[:, t:t + 1], ALU.subtract,
                                          ALU.mult)
                ins.then_inc(l2_step, 1)

            def output(B):
                wait_job(dve, "t", B, "ffn")
                v.tensor_tensor(outb[:, :, :], jobP[:, :].rearrange("p (t d) -> p t d", t=NT), x1[:, :, :], ALU.add) \
                    .then_inc(out_ready, 1)
                dve.wait_ge(out_ready, B + 1)
                dve.sem_inc(done["t"], 1)

            def body(B, p):
                for s in range(UNITS):
                    if s == AT["ln_aggr"] and not last(B):
                        ln_stats_there(B + 1)
                    k = block_at(s, BIAS_LAG)
                    if k is not None:
                        scores_there(B, k)
                    if s == AT["aggr2"] and not first(B):
                        stats2_there(B - 1)
                    unit_input(B, p, s)
                    if s >= 1:
                        unit_scan(B, s - 1)
                    if first(B):
                        setup_step(s - SETUP_AT)
                    k = block_at(s, BIAS_LAG)
                    if k is not None:
                        bias_and_max(B, k)
                    k = block_at(s, INV_LAG)
                    if k is not None:
                        inverse_sums(B, k)
                    t = memory_tile_at(s, M_MAX_LAG)
                    if t is not None:
                        mem_max(B, t)
                    t = memory_tile_at(s, M_NORM_LAG)
                    if t is not None:
                        mem_norm(B, t)
                    if s == AT["gate"]:
                        conv_gate(B)
                    if not first(B):
                        if s == AT["residual"]:
                            residual(B - 1)
                        if s == AT["aggr2"]:
                            aggr2(B - 1)
                        if s == AT["normalise2"]:
                            normalise2(B - 1)
                        if s == AT["output"]:
                            output(B - 1)
                    if not last(B):
                        if s == AT["ln_stats"]:
                            ln_stats(B + 1)
                        if s == AT["ln_aggr"]:
                            ln_aggr(B + 1)
                        if s == AT["ln_apply"]:
                            ln_apply(B + 1)
                        if s == AT["sum"]:
                            softplus_sum(B + 1)
                        if s == AT["rounding"]:
                            softplus_rounding(B + 1)
                unit_scan(B, UNITS - 1)

            def tail(B, p):
                residual(B)
                stats2_there(B)
                aggr2(B)
                normalise2(B)
                output(B)

            run_batches(dve, front, body, tail)

        @block.gpsimd
        def _(pool):
            g = nc.gpsimd
            g.memset(eps_t[:, :], EPS)
            g.memset(mhalf[:, :], -0.5)
            g.memset(relpad[:, :], -MASKED)
            g.memset(ident[:, :], 0.0).then_inc(pool_zeros, 1)
            pool.wait_ge(pool_zeros, 1)
            g.affine_select(out=ident[:, :], in_=ident[:, :], compare_op=ALU.not_equal, fill=1.0, base=0,
                            pattern=[[-1, 128]], channel_multiplier=1).then_inc(const_ready, 1)

            def other_constants():
                g.memset(wo_p[:, :, :], 0.0)
                g.memset(v_tok[:, :, :, :], 0.0).then_inc(const_ready, 1)
                g.memset(k4[:, :, :], 0.0)
                for p in range(2):
                    g.memset(xaT[p][:, 0:HALO], 0.0)
                    g.memset(xaT[p][:, HALO + L:LP], 0.0)
                g.memset(sel_bc[:, :, :, :], 0.0)
                g.memset(sel_red[:, :, :], 0.0)
                g.memset(q4[:, :, :, :], 0.0)
                g.memset(vw[:, :, :, :], 0.0)
                g.memset(ones_row[:, :], 1.0).then_inc(pool_zeros, 1)
                turn = 2
                pool.wait_ge(pool_zeros, turn)
                for part in range(3):
                    rows = sel_bc[32 * part:32 * part + 32, :, :, :]
                    g.affine_select(out=rows, in_=rows, compare_op=ALU.not_equal, fill=1.0, base=0,
                                    pattern=[[-2, GROUPS], [-1, 2], [0, NS]], channel_multiplier=1) \
                        .then_inc(pool_zeros, 1)
                    turn += 1
                    pool.wait_ge(pool_zeros, turn)
                for j in range(2):
                    rows = sel_red[64 * j:64 * j + 64, :, :]
                    ins = g.affine_select(out=rows, in_=rows, compare_op=ALU.not_equal, fill=1.0, base=-j,
                                          pattern=[[-2, GROUPS], [1, 32]], channel_multiplier=0)
                    if j == 0:
                        ins.then_inc(pool_zeros, 1)
                        turn += 1
                        pool.wait_ge(pool_zeros, turn)
                ins.then_inc(const_ready, 1)

            def ln_root_step(B, n):
                o, a, b, op = ((rr, ve[:, :], mhalf, ALU.pow), (vr, mv[:, :, 1], rr, ALU.mult),
                               (vr, vr[:, :], rr, ALU.mult), (vr, vr[:, :], eps_t, ALU.add),
                               (rr2, vr[:, :], mhalf, ALU.pow))[n]
                wait(pool, ln_step, B * N_LN + LN["ve"] + n)
                g.tensor_tensor(o[:, :], a, b[:, :], op).then_inc(ln_step, 1)

            def front(B, p):
                for n in range(5):
                    ln_root_step(B, n)
                other_constants()
                spread_heads(pool, B)

            def pair_product(B, p, m):
                wait(pool, scan_done, B * UNITS + 2 * m + 2)
                if m % 2 == 0:
                    wait(pool, red_done, B * GROUPS + m // 2 - 1)
                g.tensor_tensor(prod[:, 2 * (m % 4):2 * (m % 4) + 2, :], hst[:, 2 * (m % 2):2 * (m % 2) + 2, :],
                                C2[p][:, :].unsqueeze(1).to_broadcast([128, 2, L]), ALU.mult).then_inc(prod_done, 1)

            def prob_norm(B, k):
                wait(pool, p_inv, B * NBLK + k + 1)
                g.tensor_tensor(prob[:, k % 4, :, :], prob[:, k % 4, :, :],
                                pinv[:, k % 4, :].unsqueeze(2).to_broadcast([128, KVH, 3 * W]), ALU.mult) \
                    .then_inc(p_norm, 1)

            def root2(B):
                wait(pool, l2_step, B * N_L2 + L2["ve"])
                g.tensor_tensor(rz[:, :], vz[:, :], mhalf[:, :], ALU.pow).then_inc(l2_step, 1)

            def body(B, p):
                for s in range(UNITS):
                    if s % 2 == 1:
                        pair_product(B, p, s // 2)
                    k = block_at(s, NORM_LAG)
                    if k is not None:
                        prob_norm(B, k)
                    if not first(B):
                        if s == AT["root2"]:
                            root2(B - 1)
                    if not last(B):
                        if 0 <= s - AT["ln_root"] < 5:
                            ln_root_step(B + 1, s - AT["ln_root"])
                        for name in ("log1p", "dt", "u"):
                            if s == AT[name]:
                                softplus_step(g, B + 1, name)
                        for name in ("r0", "r1", "lo0", "lo1"):
                            if s == AT[name]:
                                part_step(g, B + 1, name)

            def tail(B, p):
                root2(B)

            run_batches(pool, front, body, tail)


_INS = ["L0_attn_x", "L0_attn_ln_g", "L0_attn_ln_b", "L0_attn_w_xproj", "L0_attn_w_dt", "L0_attn_b_dt",
        "L0_attn_A_log", "L0_attn_D_ssm", "L0_attn_w_ssm_out", "L0_attn_wq", "L0_attn_wk", "L0_attn_wv",
        "L0_attn_wo", "L0_attn_rel_bias", "L0_attn_w_wm", "L0_attn_b_wm", "L0_attn_episodic", "L0_attn_w_dc1",
        "L0_attn_b_dc1", "L0_attn_w_dc2", "L0_attn_b_dc2", "L0_attn_w_conv", "L0_attn_b_conv", "L0_ffn_kernel",
        "L0_ffn_bias", "L0_ffn_a", "L0_ffn_b"]


def kernel(**inputs):
    import numpy as _np
    import concourse.bacc as _bacc
    from concourse import mybir as _mybir
    from concourse.bass_utils import run_bass_kernel_spmd as _run

    nc = _bacc.Bacc("TRN2", target_bir_lowering=False, num_devices=1)
    arrays, args = {}, []
    for name in _INS:
        a = _np.ascontiguousarray(inputs[name])
        arrays[f"in_{name}_dram"] = a
        args.append(nc.dram_tensor(f"in_{name}_dram", a.shape, _mybir.dt.from_np(a.dtype), kind="ExternalInput").ap())
    rel_dram = nc.dram_tensor("rel_table", [H, W, RELPAD], F32, kind="Internal").ap()
    out = nc.dram_tensor("out_0_dram", (NB, L, D), F32, kind="ExternalOutput").ap()
    hybrid_block_kernel(nc, *args, rel_dram, out)
    r = _run(nc, [arrays], core_ids=[0])
    return r.results[0]["out_0_dram"]
```
